# Optimizing a Trainium2 kernel written in Bass

```python
import numpy as np
import jax
import jax.numpy as jnp

def _softmax(x, axis=-1):
    return jax.nn.softmax(x, axis=axis)

def _gelu(x):
    return jax.nn.gelu(x, approximate=True)

def _silu(x):
    return jax.nn.silu(x)

def _sigmoid(x):
    return jax.nn.sigmoid(x)

def _layernorm(x, axis=-1, eps=1e-05):
    m = jnp.mean(x, axis=axis, keepdims=True)
    v = jnp.var(x, axis=axis, keepdims=True)
    return (x - m) / jnp.sqrt(v + eps)

def _scatter_add(tgt, idx, src, axis=0):
    return tgt.at[idx].add(src)

def _segment_sum(src, seg, n):
    return jax.ops.segment_sum(src, seg, n)
kernel_name = 'mk_decoder_postln_d1_seqx_r4_03840c'

def setup_inputs(seed: int=0):
    np.random.seed(seed)
    _w = jnp.asarray

    def _rec_inputs():
        import jax
        import jax.numpy as jnp
        _rk = jax.random.key(seed)
        x = -0.0002928 + 1 * jax.random.normal(jax.random.fold_in(_rk, 1), (4, 1024, 256), jnp.float32)
        _lenS = 1024 - jax.random.randint(jax.random.fold_in(_rk, 7), (4,), 0, max(1, 1024 // 4) + 1, jnp.int32)
        _lenS2 = 77 - jax.random.randint(jax.random.fold_in(_rk, 8), (4,), 0, max(1, 77 // 4) + 1, jnp.int32)
        _ctx_1024P = jax.random.normal(jax.random.fold_in(_rk, 11), (4, 16, 256), jnp.float32)
        _ctx_1024c = jax.random.dirichlet(jax.random.fold_in(_rk, 511), 0.3 * jnp.ones((16,), jnp.float32), (4, 77))
        _ctx_1024t = jnp.einsum('bsk,bkd->bsd', _ctx_1024c, _ctx_1024P)
        _ctx_1024t = _ctx_1024t * jax.lax.rsqrt(jnp.mean(jnp.square(_ctx_1024t)) + 1e-12) * 0.953939
        ctx_1024 = -1.39393e-06 + 0.999914 * (_ctx_1024t + 0.3 * jax.random.normal(jax.random.fold_in(_rk, 611), (4, 77, 256), jnp.float32))
        return (x, ctx_1024)
    x, ctx_1024 = _rec_inputs()

    def _L0_attn_setup():
        import jax, jax.numpy as jnp
        import numpy as np
        B, L, IN_DIM = (4, 512, 256)
        H, D = (16, 64)
        OUT_DIM = 256
        key = jax.random.key(seed)
        k1, k2, k3 = jax.random.split(key, 3)
        inputs = jax.random.normal(k1, (B, L, IN_DIM), dtype=jnp.float32)
        W_qkv = jax.random.normal(k2, (IN_DIM, 3 * H * D), dtype=jnp.float32) * IN_DIM ** (-0.5)
        W_out = jax.random.normal(k3, (H * D, OUT_DIM), dtype=jnp.float32) * (H * D) ** (-0.5)
        return {'inputs': inputs, 'W_qkv': W_qkv, 'W_out': W_out}
    _L0_attn_all = _L0_attn_setup()
    _L0_attn_in = {k: v for k, v in _L0_attn_all.items() if k in ('W_qkv', 'W_out')}
    del _L0_attn_all

    def _L0_xattn_setup():
        import jax, jax.numpy as jnp
        import numpy as np
        D = 256
        H = 16

        def _heads(x):
            b, n, d = x.shape
            return x.reshape(b, n, H, d // H).transpose(0, 2, 1, 3)
        key = jax.random.key(seed)
        ks = jax.random.split(key, 10)
        xav = 1.0 / jnp.sqrt(jnp.float32(2.0))
        lim = xav * jnp.sqrt(6.0 / (D + D))

        def w(k):
            return jax.random.uniform(k, (D, D), jnp.float32, -lim, lim)
        return {'x_q': jax.random.normal(ks[0], (2, 512, D), jnp.float32), 'x_kv': jax.random.normal(ks[1], (2, 512, D), jnp.float32), 'W_q': w(ks[2]), 'b_q': jnp.zeros((D,), jnp.float32), 'W_k': w(ks[3]), 'b_k': jnp.zeros((D,), jnp.float32), 'W_v': w(ks[4]), 'b_v': jnp.zeros((D,), jnp.float32), 'W_out': w(ks[5]), 'b_out': jnp.zeros((D,), jnp.float32)}
    _L0_xattn_all = _L0_xattn_setup()
    _L0_xattn_in = {k: v for k, v in _L0_xattn_all.items() if k in ('W_q', 'b_q', 'W_k', 'b_k', 'W_v', 'b_v', 'W_out', 'b_out')}
    del _L0_xattn_all

    def _L0_ffn_setup():
        import jax, jax.numpy as jnp
        import numpy as np
        D_MODEL = 256
        D_HIDDEN = 1024
        NUM_EXPERTS = 8
        B, T = (2, 512)
        key = jax.random.key(seed)
        ks = jax.random.split(key, 8)
        s = 0.02
        x = jax.random.normal(ks[0], (B, T, D_MODEL), dtype=jnp.float32)
        Wg = jax.random.normal(ks[1], (D_MODEL, NUM_EXPERTS), dtype=jnp.float32) * s
        bg = jnp.zeros((NUM_EXPERTS,), dtype=jnp.float32)
        W1 = jax.random.normal(ks[2], (NUM_EXPERTS, D_MODEL, D_HIDDEN), dtype=jnp.float32) * s
        b1 = jnp.zeros((NUM_EXPERTS, D_HIDDEN), dtype=jnp.float32)
        W2 = jax.random.normal(ks[3], (NUM_EXPERTS, D_HIDDEN, D_MODEL), dtype=jnp.float32) * s
        b2 = jnp.zeros((NUM_EXPERTS, D_MODEL), dtype=jnp.float32)
        return {'x': x, 'Wg': Wg, 'bg': bg, 'W1': W1, 'b1': b1, 'W2': W2, 'b2': b2}
    _L0_ffn_all = _L0_ffn_setup()
    _L0_ffn_in = {k: v for k, v in _L0_ffn_all.items() if k in ('Wg', 'bg', 'W1', 'b1', 'W2', 'b2')}
    del _L0_ffn_all
    return {'x': x, 'ctx_1024': ctx_1024, 'L0_attn_W_qkv': _L0_attn_in['W_qkv'], 'L0_attn_W_out': _L0_attn_in['W_out'], 'L0_xattn_W_q': _L0_xattn_in['W_q'], 'L0_xattn_b_q': _L0_xattn_in['b_q'], 'L0_xattn_W_k': _L0_xattn_in['W_k'], 'L0_xattn_b_k': _L0_xattn_in['b_k'], 'L0_xattn_W_v': _L0_xattn_in['W_v'], 'L0_xattn_b_v': _L0_xattn_in['b_v'], 'L0_xattn_W_out': _L0_xattn_in['W_out'], 'L0_xattn_b_out': _L0_xattn_in['b_out'], 'L0_ffn_Wg': _L0_ffn_in['Wg'], 'L0_ffn_bg': _L0_ffn_in['bg'], 'L0_ffn_W1': _L0_ffn_in['W1'], 'L0_ffn_b1': _L0_ffn_in['b1'], 'L0_ffn_W2': _L0_ffn_in['W2'], 'L0_ffn_b2': _L0_ffn_in['b2']}

def reference(x, ctx_1024, L0_attn_W_qkv, L0_attn_W_out, L0_xattn_W_q, L0_xattn_b_q, L0_xattn_W_k, L0_xattn_b_k, L0_xattn_W_v, L0_xattn_b_v, L0_xattn_W_out, L0_xattn_b_out, L0_ffn_Wg, L0_ffn_bg, L0_ffn_W1, L0_ffn_b1, L0_ffn_W2, L0_ffn_b2):
    import jax
    import jax.numpy as jnp

    def _L0_attn_ref(inputs, W_qkv, W_out):
        import jax, jax.numpy as jnp
        import numpy as np
        B, L, IN_DIM = (4, 512, 256)
        H, D = (16, 64)
        OUT_DIM = 256
        b, l, _ = inputs.shape
        qkv = inputs @ W_qkv
        q, k, v = jnp.split(qkv, 3, axis=-1)
        q = q.reshape(b, l, H, D)
        k = k.reshape(b, l, H, D)
        v = v.reshape(b, l, H, D)
        score = jnp.einsum('bihd,bjhd->bijh', q, k) / D ** 0.5
        mask = jnp.tril(jnp.ones((l, l), dtype=score.dtype))[None, :, :, None]
        masked_score = score * mask + 1e+30 * (mask - 1.0)
        wmat = jax.nn.softmax(masked_score, axis=2)
        out = jnp.einsum('bijh,bjhd->bihd', wmat, v).reshape(b, l, H * D)
        return out @ W_out

    def _L0_xattn_ref(x_q, x_kv, W_q, b_q, W_k, b_k, W_v, b_v, W_out, b_out):
        import jax, jax.numpy as jnp
        import numpy as np
        D = 256
        H = 16

        def _heads(x):
            b, n, d = x.shape
            return x.reshape(b, n, H, d // H).transpose(0, 2, 1, 3)
        q = x_q @ W_q.T + b_q
        k = x_kv @ W_k.T + b_k
        v = x_kv @ W_v.T + b_v
        q, k, v = (_heads(q), _heads(k), _heads(v))
        d_head = q.shape[-1]
        scores = jnp.einsum('bhqd,bhkd->bhqk', q, k) / jnp.sqrt(jnp.float32(d_head))
        attn = jax.nn.softmax(scores, axis=-1)
        x = jnp.einsum('bhqk,bhkd->bhqd', attn, v)
        b, h, n, dh = x.shape
        x = x.transpose(0, 2, 1, 3).reshape(b, n, h * dh)
        return x @ W_out.T + b_out

    def _L0_ffn_ref(x, Wg, bg, W1, b1, W2, b2):
        import jax, jax.numpy as jnp
        import numpy as np
        D_MODEL = 256
        D_HIDDEN = 1024
        NUM_EXPERTS = 8
        B, T = (2, 512)
        gate_logits = jnp.einsum('btd,de->bte', x, Wg) + bg
        gate_scores = jax.nn.softmax(gate_logits, axis=-1)
        top1_idx = jnp.argmax(gate_scores, axis=-1)
        top1_mask = jax.nn.one_hot(top1_idx, NUM_EXPERTS, dtype=x.dtype)
        top1_weight = jnp.sum(gate_scores * top1_mask, axis=-1, keepdims=True)
        h = jax.nn.silu(jnp.einsum('btd,edh->bteh', x, W1) + b1)
        o = jnp.einsum('bteh,ehd->bted', h, W2) + b2
        y = jnp.sum(o * top1_mask[..., None], axis=2) * top1_weight
        return y
    x = _layernorm(x + _L0_attn_ref(x, L0_attn_W_qkv, L0_attn_W_out), axis=-1)
    x = _layernorm(x + _L0_xattn_ref(x, ctx_1024, L0_xattn_W_q, L0_xattn_b_q, L0_xattn_W_k, L0_xattn_b_k, L0_xattn_W_v, L0_xattn_b_v, L0_xattn_W_out, L0_xattn_b_out), axis=-1)
    x = _layernorm(x + _L0_ffn_ref(x, L0_ffn_Wg, L0_ffn_bg, L0_ffn_W1, L0_ffn_b1, L0_ffn_W2, L0_ffn_b2), axis=-1)
    return x

_drawn_inputs = setup_inputs


def setup_inputs(seed=0):
    import zlib

    import numpy as np

    out = dict(_drawn_inputs(seed))
    spreads = {'L0_xattn_b_q': (0.0, 0.8),
     'L0_xattn_b_k': (0.0, 0.8),
     'L0_xattn_b_v': (0.0, 0.1),
     'L0_xattn_b_out': (0.0, 0.1),
     'L0_ffn_bg': (0.0, 0.559),
     'L0_ffn_b1': (0.0, 0.8),
     'L0_ffn_b2': (0.0, 0.402)}
    factors = {'L0_ffn_W1': 2.725}
    for name, (base, spread) in spreads.items():
        noise = np.random.default_rng([zlib.crc32(name.encode()), seed]).standard_normal(out[name].shape)
        drawn = base * np.exp(spread * noise) if base else spread * noise
        out[name] = jnp.asarray(drawn.astype(out[name].dtype))
    for name, factor in factors.items():
        out[name] = (out[name] * factor).astype(out[name].dtype)
    return out
```

```python
import concourse.bass as bass
from concourse import mybir
from contextlib import ExitStack

F32 = mybir.dt.float32
F32R = mybir.dt.float32r
BF16 = mybir.dt.bfloat16
I32 = mybir.dt.int32
U32 = mybir.dt.uint32
ALU = mybir.AluOpType
ACT = mybir.ActivationFunctionType
AX = mybir.AxisListType

P = 128
B, L, DM = 4, 1024, 256
TOK = B * L
H, D = 16, 64
PAIRS = H // 2
NI = B * PAIRS
KT = DM // P
LT = L // P
SC = 77
XD = DM // H
E, FF = 8, 1024
NT = TOK // P
XT = NT + E - 1
ROW = 264
EPS = 1e-5
BIG = -1e30


def lookahead(s):
    return (s + 2) // 16, (s + 2) % 16


def self_attention(nc, sem, xT, w_qkv, OT, XS):
    with ExitStack() as ctx:
        def sb(name, shape, dt=F32):
            return ctx.enter_context(nc.sbuf_tensor(name, shape, dt))

        xf = sb("xf", [P, KT, L])
        xh = sb("xh", [P, KT, L], F32R)
        xl = sb("xl", [P, KT, L], F32R)
        wraw = sb("wraw", [P, 2, KT, 3, P])
        wh = sb("wh", [P, 2, KT, 2, P], F32R)
        wl = sb("wl", [P, 2, KT, 2, P], F32R)
        qs = sb("qs", [P, 2, 2, L], F32R)
        k1 = sb("k1", [P, 2, 2, L], F32R)
        k2 = sb("k2", [P, 2, 2, L], F32R)
        v = sb("v", [P, 2, LT, P])
        prob = sb("prob", [P, 2, L])
        pt = [sb("pt0", [P, 2, 4, 512]), sb("pt1", [P, 2, 8, 512])]
        nmax = sb("nmax", [P, 2])
        sums = sb("sums", [P, 2, LT, 2])
        rec = sb("rec", [P, 2, LT, 2 * D])
        inv = sb("inv", [P, 8])
        rb = sb("rb", [P, 2, 512])
        ob = sb("ob", [P, 2, 512])
        ident = sb("ident", [P, P])
        identb = sb("identb", [P, P], BF16)
        maskb = sb("maskb", [P, P], BF16)
        S = [ctx.enter_context(nc.psum_tensor(f"S{i}", [P, L], F32)) for i in range(2)]
        TP = [ctx.enter_context(nc.psum_tensor(f"TP{i}", [P, 512], F32)) for i in range(2)]
        OP = ctx.enter_context(nc.psum_tensor("OP", [P, 512], F32))
        PR = ctx.enter_context(nc.psum_tensor("PR", [P, 512], F32))

        zero = sb("zero", [P, ROW])
        const_ready = sem("const_ready")
        zero_ready = sem("zero_ready")
        zero_out = sem("zero_out")
        passed = sem("a_passed")
        x_in = sem("x_in")
        w_in = [sem("w_in0"), sem("w_in1")]
        w_split = sem("w_split")
        pr_ready = sem("pr_ready")
        hi_ready = sem("hi_ready")
        lo_ready = sem("lo_ready")
        v_ready = sem("v_ready")
        k2_ready = sem("k2_ready")
        s_ready = sem("s_ready")
        max_ready = sem("max_ready")
        p_ready = sem("p_ready")
        tp_ready = [sem("tp_ready0"), sem("tp_ready1")]
        pt_ready = [sem("pt_ready0"), sem("pt_ready1")]
        inv_ready = sem("inv_ready")
        rec_ready = sem("rec_ready")
        r_ready = sem("r_ready")
        rb_ready = sem("rb_ready")
        o_ready = sem("o_ready")
        ob_ready = sem("ob_ready")
        o_out = [sem("o_out0"), sem("o_out1")]
        block = ctx.enter_context(nc.Block())

        wv = w_qkv.rearrange("(kt p) (three c) -> p kt three c", p=P, three=3)

        def load_w(eng, par, pair):
            for kt in range(KT):
                eng.dma_start(wraw[:, par, kt], wv[:, kt, :, pair * P:(pair + 1) * P]).then_inc(w_in[par], 16)

        @block.sync
        def _(sp):
            def load_x(b):
                sp.dma_start(xf[:, :, :], xT[:, :, bass.ds(b * L, L)]).then_inc(x_in, 16)

            def swap(par, count):
                sp.wait_ge(lo_ready, count)
                for h in range(2):
                    for half in range(2):
                        a, z = half * 64, 64 - half * 64
                        sp.dma_start(k2[a:a + 64, par, h].bitcast(F32), k1[z:z + 64, par, h].bitcast(F32)).then_inc(k2_ready, 16)

            def store(n, c, count):
                sp.wait_ge(ob_ready, count)
                sp.dma_start(OT[n, :, c * 512:(c + 1) * 512], ob[:, c]).then_inc(o_out[c], 16)

            load_x(0)
            load_w(sp, 0, 0)
            load_w(sp, 1, 1)
            sp.wait_ge(zero_ready, 1)
            sp.dma_start(XS.rearrange("(t p) n -> p t n", p=P),
                         zero[:, :].unsqueeze(1).to_broadcast([P, XT, ROW])).then_inc(zero_out, 16)
            swap(0, 8)

            def batch(b, first, last):
                for n8 in range(PAIRS):
                    n = b * PAIRS + n8
                    if not (first and n8 == 0):
                        store(n - 1, 1, 2 * n)
                    if not (last and n8 == PAIRS - 1):
                        swap((n8 + 1) % 2, 8 * n + 16)
                    if not (last and n8 >= PAIRS - 2):
                        if n8 == PAIRS - 2:
                            sp.wait_ge(v_ready, 2 * n + 4)
                            load_x(b + 1)
                        load_w(sp, n8 % 2, (n8 + 2) % PAIRS)
                    store(n, 0, 2 * n + 1)

            batch(0, True, False)
            with sp.Fori(1, B - 1) as b:
                batch(b, False, False)
            batch(B - 1, False, True)
            store(NI - 1, 1, 2 * NI)
            for c in range(2):
                sp.wait_ge(o_out[c], 16 * NI)
            sp.wait_ge(zero_out, 16)

        @block.gpsimd
        def _(pool):
            pool.memset(ident[:, :], 0.0).then_inc(const_ready, 1)
            pool.memset(maskb[:, :], 0.0).then_inc(const_ready, 1)
            pool.memset(zero[:, :], 0.0).then_inc(zero_ready, 1)
            pool.wait_ge(const_ready, 2)
            pool.affine_select(out=ident[:, :], in_=ident[:, :], compare_op=ALU.not_equal, fill=1.0,
                               base=0, pattern=[[-1, P]], channel_multiplier=1).then_inc(const_ready, 1)
            pool.affine_select(out=maskb[:, :], in_=maskb[:, :], compare_op=ALU.is_ge, fill=BIG,
                               base=0, pattern=[[-1, P]], channel_multiplier=1).then_inc(const_ready, 1)
            pool.wait_ge(const_ready, 4)
            pool.tensor_copy(identb[:, :], ident[:, :]).then_inc(const_ready, 1)

            def batch(b):
                pool.wait_ge(x_in, 16 * b + 16)
                pool.sem_inc(passed, 1)
                pool.tensor_copy(xh[:, :, :], xf[:, :, :]).then_inc(const_ready, 1)
                pool.wait_ge(const_ready, 6 + b * 9)
                pool.tensor_tensor(xl[:, :, :], xf[:, :, :], xh[:, :, :], ALU.subtract)
                for k8 in range(PAIRS):
                    par = k8 % 2
                    pool.wait_ge(w_in[par], 128 * b + 32 * (k8 // 2 + 1))
                    pool.sem_inc(passed, 1)
                    pool.tensor_copy(wh[:, par], wraw[:, par, :, 0:2, :]).then_inc(const_ready, 1)
                    pool.wait_ge(const_ready, 6 + b * 9 + k8 + 1)
                    pool.tensor_tensor(wl[:, par], wraw[:, par, :, 0:2, :], wh[:, par],
                                       ALU.subtract).then_inc(w_split, 1)

            batch(0)
            with pool.Fori(1, B) as b:
                batch(b)

        def pairs(eng, body):
            body(0, 0, True, False)
            body(1, 1, False, False)
            with eng.Fori(1, NI // 2 - 1) as m:
                body(2 * m, 0, False, False)
                body(2 * m + 1, 1, False, False)
            body(NI - 2, 0, False, False)
            body(NI - 1, 1, False, True)

        @block.tensor
        def _(pe):
            pe.wait_ge(const_ready, 5)

            def project(k, par, j, first=False):
                if j == 0:
                    pe.wait_ge(w_split, k + 1)
                if j == 0 and not first:
                    pe.wait_ge(v_ready, 2 * k)
                if 1 <= j <= 4:
                    pe.wait_ge(lo_ready, 8 * k + 2 * j)
                if j == 5:
                    pe.wait_ge(v_ready, 2 * k + 1)
                if j < 4:
                    qk, c = j // 2, j % 2
                    terms = [(w, x, kt) for kt in range(KT) for w, x in ((wl, xh), (wh, xl), (wh, xh))]
                    for i, (w, x, kt) in enumerate(terms):
                        mm = pe.matmul(PR[:, :], w[:, par, kt, qk, :], x[:, kt, c * 512:(c + 1) * 512],
                                       start=(i == 0), stop=(i == len(terms) - 1))
                else:
                    for a in range(4):
                        t = (j - 4) * 4 + a
                        for kt in range(KT):
                            mm = pe.matmul(PR[:, a * P:(a + 1) * P], xf[:, kt, t * P:(t + 1) * P],
                                           wraw[:, par, kt, 2, :], start=(kt == 0), stop=(kt == KT - 1))
                mm.then_inc(pr_ready, 1)

            def scores(n, par, s, fresh=False):
                t, h = s // 2, s % 2
                if s == 0:
                    pe.wait_ge(lo_ready, 8 * n + 8)
                    pe.wait_ge(k2_ready, 64 * n + 64)
                if not (fresh and s < 2):
                    pe.wait_ge(p_ready, 16 * n + s - 1)
                width = (t + 1) * P
                for c in range((width + 511) // 512):
                    n_cols = max(min(width - 512 * c, 512), 256)
                    cols = slice(512 * c, 512 * c + n_cols)
                    q = qs[:, par, h, t * P:(t + 1) * P]
                    pe.matmul(S[s % 2][:, cols], q, k2[:, par, h, cols], start=True, stop=False)
                    mm = pe.matmul(S[s % 2][:, cols], q, k1[:, par, h, cols], start=False, stop=True)
                pe.matmul(S[s % 2][:, t * P:(t + 1) * P], identb[:, :], maskb[:, :], start=False, stop=True,
                          skip_group_check=True).then_inc(s_ready, 1)

            def transposes(n, s, fresh=False):
                t = s // 2
                pe.wait_ge(p_ready, 16 * n + s + 1)
                for bank in ([s % 2] if t < 4 else [0, 1]):
                    use = s // 2 if s < 8 else s - 4
                    if not (fresh and use == 0):
                        pe.wait_ge(pt_ready[bank], 12 * n + use)
                    j0 = 0 if t < 4 else 4 * bank
                    for j in range(j0, min(j0 + 4, t + 1)):
                        mm = pe.transpose(TP[bank][:, (j - j0) * P:(j - j0 + 1) * P],
                                          prob[:, s % 2, j * P:(j + 1) * P], ident[:, :])
                    mm.then_inc(tp_ready[bank], 1)

            def spread(n, par, c, k=None):
                pe.wait_ge(rec_ready, 2 * n + c + 1)
                if c == 0:
                    pe.wait_ge(v_ready, 2 * k + 2)
                else:
                    pe.wait_ge(rb_ready, 2 * n + 1)
                for a in range(4):
                    mm = pe.transpose(PR[:, a * P:(a + 1) * P],
                                      rec[:, par, 4 * c + a, :], ident[:, :])
                mm.then_inc(r_ready, 1)

            def weigh(n, par, c, fresh=False):
                for bank in range(2):
                    pe.wait_ge(pt_ready[bank], 12 * n + (4 if c == 0 else 12))
                pe.wait_ge(v_ready, 2 * n + 2)
                if not fresh:
                    pe.wait_ge(ob_ready, 2 * n + c)
                for j in range(4 * c + 4):
                    i0 = max(0, j - 4 * c) * P
                    for h in range(2):
                        mm = pe.matmul(OP[h * D:(h + 1) * D, i0:512], v[:, par, j, h * D:(h + 1) * D],
                                       pt[c][:, h, j, i0:512], start=(j == 0), stop=(j == 4 * c + 3))
                mm.then_inc(o_ready, 1)

            for j in range(6):
                project(0, 0, j, first=(j == 0))
            scores(0, 0, 0, fresh=True)
            scores(0, 0, 1, fresh=True)

            def iteration(n, par, first, last):
                for s in range(16):
                    transposes(n, s, fresh=first)
                    ahead, s2 = lookahead(s)
                    if not (last and ahead):
                        scores(n + ahead, (par + ahead) % 2, s2)
                    if s == 0 and not first:
                        spread(n - 1, 1 - par, 1)
                        weigh(n - 1, 1 - par, 1)
                    if 1 <= s <= 6 and not last:
                        if s == 1 and not first:
                            pe.wait_ge(rb_ready, 2 * n)
                        project(n + 1, 1 - par, s - 1)
                    if s == 8:
                        spread(n, par, 0, n if last else n + 1)
                        weigh(n, par, 0, fresh=first)

            pairs(pe, iteration)
            spread(NI - 1, 1, 1)
            weigh(NI - 1, 1, 1)

        @block.scalar
        def _(act):
            def high(k, par, j, first=False):
                c = j % 2
                act.wait_ge(pr_ready, 6 * k + j + 1)
                for h in range(2):
                    rows = slice(h * 64, h * 64 + 64)
                    out = (qs if j < 2 else k1)[rows, par, h, c * 512:(c + 1) * 512]
                    act.activation(out, PR[rows, :], ACT.Copy,
                                   scale=D ** -0.5 if j < 2 else 1.0).then_inc(hi_ready, 1)

            def expo(n, par, s):
                t, h = s // 2, s % 2
                act.wait_ge(max_ready, 16 * n + s + 1)
                act.activation(prob[:, s % 2, 0:(t + 1) * P], S[s % 2][:, 0:(t + 1) * P], ACT.Exp,
                               bias=nmax[:, s % 2:s % 2 + 1],
                               accum_out=sums[:, par, t, h:h + 1]).then_inc(p_ready, 1)

            def evacuate(n, s):
                t, h = s // 2, s % 2
                use = s // 2 if s < 8 else s - 4
                act.wait_ge(tp_ready[0], 12 * n + use + 1)
                nb = min(4, t + 1)
                act.activation(pt[t // 4][:, h, 0:nb, (t % 4) * P:(t % 4 + 1) * P],
                               TP[0][:, 0:nb * P].rearrange("p (j i) -> p j i", i=P),
                               ACT.Copy).then_inc(pt_ready[0], 1)

            def spread_copy(n, c):
                act.wait_ge(r_ready, 2 * n + c + 1)
                act.activation(rb[:, c], PR[:, :], ACT.Copy).then_inc(rb_ready, 1)

            for j in range(4):
                high(0, 0, j)
            expo(0, 0, 0)
            expo(0, 0, 1)

            def iteration(n, par, first, last):
                for s in range(16):
                    if s >= 8 or s % 2 == 0:
                        evacuate(n, s)
                    ahead, s2 = lookahead(s)
                    if not (last and ahead):
                        expo(n + ahead, (par + ahead) % 2, s2)
                    if s == 0 and not first:
                        spread_copy(n - 1, 1)
                    if 1 <= s <= 4 and not last:
                        high(n + 1, 1 - par, s - 1)
                    if s == 8:
                        spread_copy(n, 0)

            pairs(act, iteration)
            spread_copy(NI - 1, 1)

        @block.vector
        def _(dve):
            def low(k, par, j):
                c = j % 2
                for h in range(2):
                    rows, other = slice(h * 64, h * 64 + 64), slice(64 - h * 64, 128 - h * 64)
                    stack = (qs if j < 2 else k1)
                    dve.wait_ge(hi_ready, 8 * k + 2 * j + 2)
                    dve.scalar_tensor_tensor(
                        out=stack[other, par, h, c * 512:(c + 1) * 512], in0=PR[rows, :],
                        scalar=D ** -0.5 if j < 2 else 1.0,
                        in1=stack[rows, par, h, c * 512:(c + 1) * 512].bitcast(F32),
                        op0=ALU.mult, op1=ALU.subtract).then_inc(lo_ready, 1)

            def values(k, par, j):
                dve.wait_ge(pr_ready, 6 * k + j + 1)
                dve.tensor_copy(v[:, par, 4 * (j - 4):4 * (j - 4) + 4, :],
                                PR[:, :].rearrange("p (a c) -> p a c", c=P)).then_inc(v_ready, 1)

            def row_max(n, s):
                t = s // 2
                dve.wait_ge(s_ready, 16 * n + s + 1)
                dve.tensor_reduce(nmax[:, s % 2:s % 2 + 1], S[s % 2][:, 0:(t + 1) * P], AX.X, ALU.max,
                                  negate=True).then_inc(max_ready, 1)

            def evacuate(n, s):
                t, h = s // 2, s % 2
                use = s // 2 if s < 8 else s - 4
                dve.wait_ge(tp_ready[1], 12 * n + use + 1)
                j0 = 0 if t < 4 else 4
                nb = t + 1 - j0
                dve.tensor_copy(pt[t // 4][:, h, j0:j0 + nb, (t % 4) * P:(t % 4 + 1) * P],
                                TP[1][:, 0:nb * P].rearrange("p (j i) -> p j i", i=P)).then_inc(pt_ready[1], 1)

            def reciprocals(n, par, c):
                dve.wait_ge(p_ready, 16 * n + 8 * c + 8)
                dve.reciprocal(inv[:, :], sums[:, par, 4 * c:4 * c + 4, :].rearrange("p t h -> p (t h)"))\
                   .then_inc(inv_ready, 1)
                dve.wait_ge(inv_ready, 2 * n + c + 1)
                dve.tensor_copy(rec[:, par, 4 * c:4 * c + 4, :].rearrange("p t (h d) -> p (t h) d", h=2),
                                inv[:, :].unsqueeze(2).to_broadcast([P, 8, D])).then_inc(rec_ready, 1)

            def normalise(n, c, fresh):
                dve.wait_ge(o_ready, 2 * n + c + 1)
                dve.wait_ge(rb_ready, 2 * n + c + 1)
                if not fresh:
                    dve.wait_ge(o_out[c], 16 * n)
                dve.tensor_tensor(ob[:, c], OP[:, :], rb[:, c], ALU.mult).then_inc(ob_ready, 1)

            for j in range(6):
                (low if j < 4 else values)(0, 0, j)
            row_max(0, 0)
            row_max(0, 1)

            def iteration(n, par, first, last, second=False):
                for s in range(16):
                    if s >= 8 or s % 2 == 1:
                        evacuate(n, s)
                    ahead, s2 = lookahead(s)
                    if not (last and ahead):
                        row_max(n + ahead, s2)
                    if s == 0 and not first:
                        normalise(n - 1, 1, fresh=isinstance(n, int) and n == 1)
                    if 1 <= s <= 6 and not last:
                        (low if s < 5 else values)(n + 1, 1 - par, s - 1)
                    if s == 7:
                        reciprocals(n, par, 0)
                    if s == 8:
                        normalise(n, 0, fresh=first)
                    if s == 15:
                        reciprocals(n, par, 1)

            pairs(dve, iteration)
            normalise(NI - 1, 1, fresh=False)


class Steps:

    def __init__(self):
        self.base, self.n = 0, 0

    def start(self, base):
        self.base, self.n = base, 0

    def one(self):
        self.n += 1
        return 1

    def now(self):
        return self.base + self.n


def token_groups(nc, sem, d, OT, x2r, logits):
    NG, GT = TOK // 512, 4
    HC = 4
    with ExitStack() as ctx:
        def sb(name, shape, dt=F32):
            return ctx.enter_context(nc.sbuf_tensor(name, shape, dt))

        wo = sb("wo", [P, PAIRS, DM])
        wq = sb("wq", [P, KT, DM])
        wk = sb("wk", [P, KT, DM])
        wvx = sb("wvx", [P, KT, DM])
        wox = sb("wox", [P, 4, DM])
        wg = sb("wg", [P, KT, E])
        ctxT = sb("ctxT", [P, KT, B * SC])
        bq = sb("bq", [P, KT])
        bk = sb("bk", [P, KT])
        bv = sb("bv", [SC, DM])
        bo = sb("bo", [P, DM])
        bg = sb("bg", [P, E])
        ident = sb("ident2", [P, P])
        hmask = sb("hmask", [P, 8])
        kT = sb("kT", [P, KT, B * SC])
        kbd_all = sb("kbd_all", [P, B, KT, 8 * SC])
        vx_all = sb("vx_all", [SC, B, H, 32])
        kbd = sb("kbd", [P, KT, 8 * SC])
        vx = sb("vx", [SC, H, 32])
        ot = sb("ot", [P, PAIRS, 512])
        xin = sb("xin", [P, GT, DM])
        r = sb("r", [P, 2, DM])
        st = sb("st", [P, 6])
        mv = sb("mv", [P, 2, 2])
        rstd = sb("rstd", [P, 2])
        veps = sb("veps", [P, 1])
        mhalf = sb("mhalf", [P, 1])
        x1 = sb("x1", [P, 2, GT, DM])
        x1b = sb("x1b", [P, 2, GT, DM])
        x1T = sb("x1T", [P, KT, 512])
        qT = sb("qT", [P, KT, 512])
        sc = sb("sc", [P, GT, H * SC])
        mx = sb("mx", [P, GT, H])
        sm = sb("sm", [P, GT, H])
        rc = sb("rc", [P, GT, H])
        pT = sb("pT", [SC, H, 512])
        oT = sb("oT", [P, 4, 512])
        x2 = sb("x2", [P, GT, DM])
        x2T = sb("x2T", [P, 2, KT, P])
        SP = [ctx.enter_context(nc.psum_tensor(f"SP{i}", [P, 512], F32)) for i in range(4)]
        M = [ctx.enter_context(nc.psum_tensor(f"M{i}", [P, 512], F32)) for i in range(2)]
        T = [ctx.enter_context(nc.psum_tensor(f"T{i}", [P, 512], F32)) for i in range(2)]

        w_in = sem("g_w_in")
        small_in = sem("g_small_in")
        consts = sem("g_consts")
        kv_psum = sem("g_kv_psum")
        kv_sb = sem("g_kv_sb")
        kv_all = sem("g_kv_all")
        kv_now = sem("g_kv_now")
        in_ready = sem("g_in")
        m_ready = [sem("g_m_ready0"), sem("g_m_ready1")]
        m_free = [sem("g_m_free0"), sem("g_m_free1")]
        t_ready = [sem("g_t_ready0"), sem("g_t_ready1")]
        t_free = [sem("g_t_free0"), sem("g_t_free1")]
        sc_ready = sem("g_sc_ready")
        sc_free = sem("g_sc_free")
        exp_ready = sem("g_exp_ready")
        inv_ready = sem("g_inv_ready")
        p_ready = sem("g_p_ready")
        x1_ready = sem("g_x1_ready")
        x1b_ready = sem("g_x1b_ready")
        x2_ready = sem("g_x2_ready")
        x2_kept = sem("g_x2_kept")
        veps_ready = sem("g_veps_ready")
        var_ready = sem("g_var_ready")
        rstd_ready = sem("g_rstd_ready")
        passed = sem("g_passed")
        dstep = sem("g_dstep")
        block = ctx.enter_context(nc.Block())

        TURN, GATE = (18, 19, 21, 23), (20, 22, 24, 25)

        def use(g, u, last=False):
            return u % 2, 2 + 13 * g + (u - 4 if last and u >= 10 else u) // 2

        def groups(eng, body):
            body(0, 0, True, False)
            body(1, 1, False, False)
            with eng.Fori(1, NG // 2 - 1) as m:
                body(2 * m, 0, False, False)
                body(2 * m + 1, 1, False, False)
            body(NG - 2, 0, False, False)
            body(NG - 1, 1, False, True)

        OTv = OT.rearrange("(b r) p (c i) -> p b r c i", b=B, c=2)

        @block.sync
        def _(sp):
            def load(b, c):
                sp.dma_start(ot[:, :, :], OTv[:, b, :, c, :]).then_inc(in_ready, 16)
                sp.dma_start(xin[:, :, :], d["x"][:, b, c]).then_inc(in_ready, 16)

            sp.dma_start(wk[:, :, :], d["wk"]).then_inc(w_in, 16)
            sp.dma_start(wvx[:, :, :], d["wv"]).then_inc(w_in, 16)
            sp.dma_start(ctxT[:, :, :], d["ctxT"]).then_inc(w_in, 16)
            sp.dma_start(wo[:, :, :], d["wo"]).then_inc(w_in, 16)
            load(0, 0)
            sp.dma_start(wq[:, :, :], d["wq"]).then_inc(w_in, 16)
            sp.dma_start(wg[:, :, :], d["wg"]).then_inc(w_in, 16)
            sp.wait_ge(x1_ready, 4)
            load(0, 1)
            with sp.Fori(1, B) as b:
                sp.wait_ge(x1_ready, 8 * b)
                load(b, 0)
                sp.wait_ge(x1_ready, 8 * b + 4)
                load(b, 1)

        @block.gpsimd
        def _(pool):
            pool.memset(ident[:, :], 0.0).then_inc(consts, 1)
            pool.memset(hmask[:, :], 1.0).then_inc(consts, 1)
            pool.memset(mhalf[:, :], -0.5)
            pool.memset(vx_all[:, :, :, :], 0.0).then_inc(consts, 1)
            pool.memset(wox[:, :, :], 0.0).then_inc(consts, 1)
            pool.memset(x2r[:, :, DM:ROW], 0.0).then_inc(consts, 1)
            pool.wait_ge(consts, 5)
            pool.affine_select(out=ident[:, :], in_=ident[:, :], compare_op=ALU.not_equal, fill=1.0,
                               base=0, pattern=[[-1, P]], channel_multiplier=1).then_inc(consts, 1)
            pool.affine_select(out=hmask[:, :], in_=hmask[:, :], compare_op=ALU.is_ge, fill=0.0,
                               base=0, pattern=[[-XD, 8]], channel_multiplier=1).then_inc(consts, 1)
            pool.wait_ge(consts, 7)
            pool.affine_select(out=hmask[:, :], in_=hmask[:, :], compare_op=ALU.is_ge, fill=0.0,
                               base=XD - 1, pattern=[[XD, 8]], channel_multiplier=-1).then_inc(consts, 1)
            pool.wait_ge(small_in, 16 * 9)
            pool.wait_ge(kv_all, 4 * KT + B)

            def group(g, par, first, last):
                if par == 0:
                    if not first:
                        bank, before = use(g - 1, 13)
                        pool.wait_ge(m_ready[bank], before + 1)
                    b = batch[0]
                    pool.sem_inc(passed, 1)
                    pool.tensor_copy(kbd[:, :, :], kbd_all[:, b]).then_inc(kv_now, 1)
                    pool.tensor_copy(vx[:, :, :], vx_all[:, b]).then_inc(kv_now, 1)
                if first:
                    for a in range(GT):
                        root(a, a)
                    bias_x1(0, 0)
                for a in range(GT):
                    pool.wait_ge(inv_ready, 4 * g + a + 1)
                    pv = sc[:, a].rearrange("p (h j) -> p h j", j=SC)
                    pool.tensor_tensor(pv, pv, rc[:, a].unsqueeze(2).to_broadcast([P, H, SC]),
                                       ALU.mult).then_inc(p_ready, 1)
                    if not last:
                        root(8 * g + 4 + a, a)
                if not last:
                    bias_x1(g + 1, 1 - par)
                for a in range(GT + 1):
                    if a < GT:
                        root(8 * g + (4 if last else 8) + a, a)
                    if a >= 1:
                        pool.wait_ge(x2_ready, 4 * g + a)
                        pool.sem_inc(passed, 1)
                        pool.tensor_copy(x2r[:, 4 * g + a - 1, 0:DM], x2[:, a - 1]).then_inc(x2_kept, 1)

            def root(i, a):
                pool.wait_ge(var_ready, i + 1)
                if not (isinstance(i, int) and i == 0):
                    pool.wait_ge(rstd_ready, i)
                pool.sem_inc(passed, 1)
                pool.tensor_scalar(veps[:, :], mv[:, a % 2, 1:2], EPS, None, ALU.add).then_inc(veps_ready, 1)
                pool.wait_ge(veps_ready, i + 1)
                pool.tensor_tensor(rstd[:, a % 2:a % 2 + 1], veps[:, :], mhalf[:, :], ALU.pow).then_inc(rstd_ready, 1)

            def bias_x1(g, par):
                for a in range(GT):
                    pool.wait_ge(x1_ready, 4 * g + a + 1)
                    pool.tensor_tensor(x1b[:, par, a], x1[:, par, a], bo[:, :], ALU.add).then_inc(x1b_ready, 1)

            batch = [0]
            group(0, 0, True, False)
            group(1, 1, False, False)
            with pool.Fori(1, NG // 2 - 1) as m:
                batch[0] = m
                group(2 * m, 0, False, False)
                group(2 * m + 1, 1, False, False)
            batch[0] = B - 1
            group(NG - 2, 0, False, False)
            group(NG - 1, 1, False, True)

        @block.tensor
        def _(pe):
            pe.wait_ge(w_in, 16 * 6)
            pe.wait_ge(consts, 8)
            for kt in range(KT):
                for i in range(KT):
                    mm = pe.matmul(M[kt][:, 0:B * SC], wk[:, i, kt * P:(kt + 1) * P], ctxT[:, i, :],
                                   start=(i == 0), stop=(i == KT - 1))
                mm.then_inc(kv_psum, 1)
            for b in range(B):
                for i in range(KT):
                    mm = pe.matmul(SP[b][0:SC, 0:DM], ctxT[:, i, b * SC:(b + 1) * SC], wvx[:, i, :],
                                   start=(i == 0), stop=(i == KT - 1))
                mm.then_inc(kv_psum, 1)
            pe.wait_ge(kv_all, 4 * KT + B)

            def take(bank_uses):
                bank, before = bank_uses
                if not (isinstance(before, int) and before == 0):
                    pe.wait_ge(m_free[bank], before)
                return M[bank], m_ready[bank]

            def project(g, par, a, bank_uses):
                if a == 0:
                    pe.wait_ge(in_ready, 32 * g + 32)
                m, ready = take(bank_uses)
                for i in range(PAIRS):
                    mm = pe.matmul(m[:, 0:DM], ot[:, i, a * P:(a + 1) * P], wo[:, i, :],
                                   start=(i == 0), stop=(i == PAIRS - 1))
                mm.then_inc(ready, 1)

            for a in range(GT):
                project(0, 0, a, (a % 2, a // 2))

            def x_scores(g, a):
                if a == 0:
                    pe.wait_ge(kv_now, 2 * batch[0] + 2)
                for c in range(4):
                    if not (isinstance(g, int) and g == 0 and a == 0):
                        pe.wait_ge(sc_free, 16 * g + 4 * a + c - 3)
                    pe.matmul(SP[c][:, 0:HC * SC], qT[:, c // 2, a * P:(a + 1) * P],
                              kbd[:, c // 2, (c % 2) * HC * SC:(c % 2 + 1) * HC * SC],
                              start=True, stop=True).then_inc(sc_ready, 1)

            def x_transposes(g, a):
                pe.wait_ge(p_ready, 4 * g + a + 1)
                for q in range(4):
                    bank, before = q % 2, 8 * g + 2 * a + q // 2
                    if not (isinstance(before, int) and before == 0):
                        pe.wait_ge(t_free[bank], before)
                    for i in range(4):
                        h = 4 * q + i
                        mm = pe.transpose(T[bank][0:SC, i * P:(i + 1) * P], sc[:, a, h * SC:(h + 1) * SC], ident[:, :])
                    mm.then_inc(t_ready[bank], 1)

            def group(g, par, first, last):
                for a in range(GT):
                    pe.wait_ge(x1_ready, 4 * g + a + 1)
                    m, ready = take(use(g, a))
                    for i in range(KT):
                        mm = pe.transpose(m[:, i * P:(i + 1) * P], x1[:, par, a, i * P:(i + 1) * P], ident[:, :])
                    mm.then_inc(ready, 1)
                for kt in range(KT):
                    m, ready = take(use(g, 4 + kt))
                    for bank, before in (use(g, 2), use(g, 3)):
                        pe.wait_ge(m_free[bank], before + 1)
                    for i in range(KT):
                        mm = pe.matmul(m[:, :], wq[:, i, kt * P:(kt + 1) * P], x1T[:, i, :],
                                       start=(i == 0), stop=(i == KT - 1))
                    mm.then_inc(ready, 1)
                for bank, before in (use(g, 4), use(g, 5)):
                    pe.wait_ge(m_free[bank], before + 1)
                x_scores(g, 0)
                x_scores(g, 1)
                for a in range(2):
                    if not last:
                        project(g + 1, 1 - par, a, use(g, 6 + a))
                    x_scores(g, 2 + a)
                for a in range(GT):
                    x_transposes(g, a)
                    if a < 2 and not last:
                        project(g + 1, 1 - par, 2 + a, use(g, 8 + a))
                for bank in range(2):
                    pe.wait_ge(t_free[bank], 8 * g + 8)
                for hg in range(4):
                    m, ready = take(use(g, 10 + hg, last))
                    for i in range(4):
                        mm = pe.matmul(m[32 * i:32 * i + 32, :], vx[:, 4 * hg + i, :], pT[:, 4 * hg + i, :],
                                       start=True, stop=True)
                    mm.then_inc(ready, 1)
                for a in range(GT):
                    m, ready = take(use(g, 14 + a, last))
                    for bank, before in (use(g, 12, last), use(g, 13, last)):
                        pe.wait_ge(m_free[bank], before + 1)
                    for i in range(4):
                        mm = pe.matmul(m[:, 0:DM], oT[:, i, a * P:(a + 1) * P], wox[:, i, :],
                                       start=(i == 0), stop=(i == 3))
                    mm.then_inc(ready, 1)
                for a in range(GT):
                    pe.wait_ge(x2_ready, 4 * g + a + 1)
                    m, ready = take(use(g, TURN[a], last))
                    for i in range(KT):
                        mm = pe.transpose(m[:, i * P:(i + 1) * P], x2[:, a, i * P:(i + 1) * P], ident[:, :])
                    mm.then_inc(ready, 1)
                    if a >= 1:
                        gate(g, a - 1, last)
                gate(g, GT - 1, last)

            def gate(g, a, last):
                bank, before = use(g, TURN[a], last)
                pe.wait_ge(m_free[bank], before + 1)
                m, ready = take(use(g, GATE[a], last))
                for i in range(KT):
                    mm = pe.matmul(m[:, 0:E], x2T[:, a % 2, i, :], wg[:, i, :],
                                   start=(i == 0), stop=(i == KT - 1))
                mm.then_inc(ready, 1)

            batch = [0]
            group(0, 0, True, False)
            group(1, 1, False, False)
            with pe.Fori(1, NG // 2 - 1) as m_:
                batch[0] = m_
                group(2 * m_, 0, False, False)
                group(2 * m_ + 1, 1, False, False)
            batch[0] = B - 1
            group(NG - 2, 0, False, False)
            group(NG - 1, 1, False, True)

        @block.scalar
        def _(act):
            act.dma_start(bq[:, :], d["bq"]).then_inc(small_in, 16)
            act.dma_start(bk[:, :], d["bk"]).then_inc(small_in, 16)
            act.dma_start(bv[:, :], d["bv"].partition_broadcast(SC)).then_inc(small_in, 16)
            act.dma_start(bo[:, :], d["bo"].partition_broadcast(P)).then_inc(small_in, 16)
            act.dma_start(bg[:, :], d["bg"].partition_broadcast(P)).then_inc(small_in, 16)
            act.wait_ge(consts, 5)
            for i in range(4):
                act.dma_start(wox[32 * i:32 * i + XD], d["wox"][i]).then_inc(small_in, 16)
            act.wait_ge(small_in, 16 * 9)
            for kt in range(KT):
                act.wait_ge(kv_psum, kt + 1)
                act.activation(kT[:, kt, :], M[kt][:, 0:B * SC], ACT.Identity,
                               bias=bk[:, kt:kt + 1]).then_inc(kv_sb, 1)

            def group(g, par, first, last):
                def read(u, out, rearranged=None, bias=None):
                    bank, before = use(g, u, last)
                    act.wait_ge(m_ready[bank], before + 1)
                    m = M[bank][:, 0:512] if rearranged is None else rearranged(M[bank])
                    if bias is None:
                        act.activation(out, m, ACT.Copy).then_inc(m_free[bank], 1)
                    else:
                        act.activation(out, m, ACT.Identity, bias=bias).then_inc(m_free[bank], 1)

                def two(m):
                    return m[:, 0:DM].rearrange("p (k i) -> p k i", k=KT)

                for a in range(GT):
                    read(a, x1T[:, :, a * P:(a + 1) * P], two)
                for kt in range(KT):
                    read(4 + kt, qT[:, kt, :], bias=bq[:, kt:kt + 1])
                for a in range(GT):
                    act.wait_ge(sc_free, 16 * g + 4 * a + 4)
                    act.activation(sc[:, a], sc[:, a], ACT.Exp, scale=XD ** -0.5).then_inc(exp_ready, 1)
                for a in range(GT):
                    for q in range(4):
                        bank, before = q % 2, 8 * g + 2 * a + q // 2
                        act.wait_ge(t_ready[bank], before + 1)
                        act.activation(pT[:, 4 * q:4 * q + 4, a * P:(a + 1) * P],
                                       T[bank][0:SC, :].rearrange("p (h i) -> p h i", i=P),
                                       ACT.Copy).then_inc(t_free[bank], 1)
                for hg in (0, 2):
                    read(10 + hg, oT[:, hg, :])
                for a in range(GT):
                    read(TURN[a], x2T[:, a % 2], two)

            groups(act, group)

        @block.vector
        def _(dve):
            step = Steps()
            dve.wait_ge(small_in, 16 * 9)
            dve.wait_ge(consts, 8)
            for kt in range(KT):
                dve.wait_ge(kv_sb, kt + 1)
                for b in range(B):
                    dve.tensor_tensor(kbd_all[:, b, kt].rearrange("p (h j) -> p h j", j=SC),
                                      kT[:, kt, b * SC:(b + 1) * SC].unsqueeze(1).to_broadcast([P, 8, SC]),
                                      hmask[:, :].unsqueeze(2).to_broadcast([P, 8, SC]), ALU.mult).then_inc(kv_all, 1)
            for b in range(B):
                dve.wait_ge(kv_psum, KT + b + 1)
                dve.tensor_tensor(vx_all[:, b, :, 0:XD], SP[b][0:SC, 0:DM].rearrange("p (h e) -> p h e", e=XD),
                                  bv[:, :].rearrange("p (h e) -> p h e", e=XD), ALU.add).then_inc(kv_all, 1)

            def less_max(g, a):
                for c in range(4):
                    dve.wait_ge(sc_ready, 16 * g + 4 * a + c + 1)
                    dve.tensor_reduce(mx[:, a, HC * c:HC * c + HC],
                                      SP[c][:, 0:HC * SC].rearrange("p (h j) -> p h j", j=SC),
                                      AX.X, ALU.max).then_inc(dstep, step.one())
                dve.wait_ge(dstep, step.now())
                for c in range(4):
                    dve.tensor_tensor(sc[:, a, HC * SC * c:HC * SC * (c + 1)].rearrange("p (h j) -> p h j", j=SC),
                                      SP[c][:, 0:HC * SC].rearrange("p (h j) -> p h j", j=SC),
                                      mx[:, a, HC * c:HC * c + HC].unsqueeze(2).to_broadcast([P, HC, SC]),
                                      ALU.subtract).then_inc(sc_free, 1)

            def inverse(g, a):
                dve.wait_ge(exp_ready, 4 * g + a + 1)
                dve.tensor_reduce(sm[:, a], sc[:, a].rearrange("p (h j) -> p h j", j=SC), AX.X,
                                  ALU.add).then_inc(dstep, step.one())
                dve.wait_ge(dstep, step.now())
                dve.reciprocal(rc[:, a], sm[:, a]).then_inc(inv_ready, 1)

            def statistics(i, bank_uses, residual, a):
                bank, before = bank_uses
                dve.wait_ge(m_ready[bank], before + 1)
                dve.tensor_tensor(r[:, a % 2], M[bank][:, 0:DM], residual, ALU.add).then_inc(m_free[bank], 1)
                dve.wait_ge(m_free[bank], before + 1)
                if not (isinstance(i, int) and i == 0):
                    dve.wait_ge(var_ready, i)
                dve.bn_stats(st[:, :], r[:, a % 2]).then_inc(dstep, step.one())
                dve.wait_ge(dstep, step.now())
                dve.sem_inc(passed, 1)
                dve.bn_aggr(mv[:, a % 2], st[:, :]).then_inc(var_ready, 1)

            def norm(i, a, out, ready):
                dve.wait_ge(rstd_ready, i + 1)
                dve.tensor_scalar(out, r[:, a % 2], mv[:, a % 2, 0:1], rstd[:, a % 2:a % 2 + 1],
                                  ALU.subtract, ALU.mult).then_inc(ready, 1)

            def statistics1(i, g, a, bank_uses):
                if a == 0:
                    dve.wait_ge(in_ready, 32 * g + 32)
                if a >= 2:
                    dve.wait_ge(x1_ready, 4 * g + a - 1)
                elif not (isinstance(g, int) and g <= 1):
                    dve.wait_ge(x2_ready, 4 * g - 4)
                elif g == 1:
                    dve.wait_ge(x1_ready, 4)
                statistics(i, bank_uses, xin[:, a], a)

            for a in range(GT):
                statistics1(a, 0, a, (a % 2, a // 2))
                norm(a, a, x1[:, 0, a], x1_ready)
            before_groups = step.now()
            a_group = 4 * 4 + 4 + 4 + 4

            def group(g, par, first, last):
                step.start(before_groups + a_group * g)
                less_max(g, 0)
                less_max(g, 1)
                inverse(g, 0)
                for a in range(GT):
                    if not last:
                        statistics1(8 * g + 4 + a, g + 1, a, use(g, 6 + a))
                    if a < 2:
                        less_max(g, 2 + a)
                    if a < 3:
                        inverse(g, a + 1)
                    if not last:
                        norm(8 * g + 4 + a, a, x1[:, 1 - par, a], x1_ready)
                for hg in (1, 3):
                    bank, before = use(g, 10 + hg, last)
                    dve.wait_ge(m_ready[bank], before + 1)
                    dve.tensor_copy(oT[:, hg, :], M[bank][:, :]).then_inc(m_free[bank], 1)
                for a in range(GT + 1):
                    if a < GT:
                        dve.wait_ge(x1b_ready, 4 * g + a + 1)
                        if a >= 2:
                            dve.wait_ge(x2_ready, 4 * g + a - 1)
                        elif last:
                            dve.wait_ge(x2_ready, 4 * g)
                        else:
                            dve.wait_ge(x1_ready, 4 * g + 8)
                        statistics(8 * g + (4 if last else 8) + a, use(g, 14 + a, last), x1b[:, par, a], a)
                    if a >= 1:
                        if not first:
                            dve.wait_ge(x2_kept, 4 * g + a - 4)
                        norm(8 * g + (4 if last else 8) + a - 1, a - 1, x2[:, a - 1], x2_ready)
                for a in range(GT):
                    bank, before = use(g, GATE[a], last)
                    dve.wait_ge(m_ready[bank], before + 1)
                    dve.tensor_tensor(logits[:, 4 * g + a, :], M[bank][:, 0:E], bg[:, :],
                                      ALU.add).then_inc(m_free[bank], 1)

            groups(dve, group)


def route(nc, sem, x2r, logits, pos, tile_e, XS):
    with ExitStack() as ctx:
        def sb(name, shape, dt=F32):
            return ctx.enter_context(nc.sbuf_tensor(name, shape, dt))

        tri = sb("tri", [P, P])
        ones = sb("ones", [P, P])
        eidx = sb("eidx", [P, E])
        t128 = sb("t128", [P, NT])
        tnum = sb("tnum", [1, XT])
        best = sb("best", [P, NT])
        p = sb("p", [P, NT, E])
        total = sb("total", [P, NT])
        inv = sb("inv3", [P, NT])
        first = sb("first", [P, NT])
        oh = sb("oh", [P, NT, E])
        cum = [sb("cum0", [P, NT, E]), sb("cum1", [P, NT, E])]
        count = sb("count", [P, E])
        more = sb("more", [P, E, NT])
        ntile = sb("ntile", [P, E])
        start = sb("start", [P, E])
        posf = sb("posf", [P, NT])
        tgt = sb("tgt", [1, XT, E])
        tef = sb("tef", [1, XT])
        U = ctx.enter_context(nc.psum_tensor("U", [P, 512], F32))
        V = ctx.enter_context(nc.psum_tensor("V", [P, 512], F32))
        consts = sem("r_consts")
        less_ready = sem("r_less")
        exp_ready = sem("r_exp")
        oh_ready = sem("r_oh")
        sums_ready = sem("r_sums")
        pos_ready = sem("r_pos")
        dstep = sem("r_dstep")
        sent = sem("r_sent")
        block = ctx.enter_context(nc.Block())

        @block.gpsimd
        def _(pool):
            pool.memset(tri[:, :], 1.0).then_inc(consts, 1)
            pool.memset(ones[:, :], 1.0).then_inc(consts, 1)
            pool.iota(eidx[:, :], [[1, E]], base=-E, channel_multiplier=0,
                      allow_small_or_imprecise_dtypes=True).then_inc(consts, 1)
            pool.iota(t128[:, :], [[P, NT]], base=0, channel_multiplier=0,
                      allow_small_or_imprecise_dtypes=True).then_inc(consts, 1)
            pool.iota(tnum[:, :], [[1, XT]], base=0, channel_multiplier=0,
                      allow_small_or_imprecise_dtypes=True).then_inc(consts, 1)
            pool.wait_ge(consts, 5)
            pool.affine_select(out=tri[:, :], in_=tri[:, :], compare_op=ALU.is_gt, fill=0.0,
                               base=0, pattern=[[1, P]], channel_multiplier=-1).then_inc(consts, 1)
            pool.wait_ge(pos_ready, 1)
            for t in range(NT):
                pool.indirect_dma_start(XS, bass.IndirectOffsetOnAxis(ap=pos[:, t:t + 1], axis=0),
                                        x2r[:, t, :], None).then_inc(sent, 16)
            pool.wait_ge(sent, 16 * NT)

        @block.scalar
        def _(act):
            act.wait_ge(less_ready, 1)
            act.activation(p[:, :, :], p[:, :, :], ACT.Exp).then_inc(exp_ready, 1)

        @block.tensor
        def _(pe):
            pe.wait_ge(consts, 6)
            pe.wait_ge(oh_ready, 1)
            flat = oh[:, :, :].rearrange("p t e -> p (t e)")
            pe.matmul(U[:, 0:NT * E], tri[:, :], flat, start=True, stop=True)
            pe.matmul(V[:, 0:NT * E], ones[:, :], flat, start=True, stop=True).then_inc(sums_ready, 1)

        @block.vector
        def _(dve):
            step = Steps()

            def done(ins):
                return ins.then_inc(dstep, step.one())

            def wide(a):
                return a.unsqueeze(2).to_broadcast([P, NT, E])

            def every(a, n=NT):
                return a.unsqueeze(1).to_broadcast([P, n, E])

            dve.wait_ge(consts, 6)
            done(dve.tensor_reduce(best[:, :], logits[:, :, :], AX.X, ALU.max))
            dve.wait_ge(dstep, step.now())
            dve.tensor_tensor(p[:, :, :], logits[:, :, :], wide(best[:, :]), ALU.subtract).then_inc(less_ready, 1)
            dve.wait_ge(exp_ready, 1)
            done(dve.tensor_reduce(total[:, :], p[:, :, :], AX.X, ALU.add))
            done(dve.tensor_reduce(best[:, :], p[:, :, :], AX.X, ALU.max))
            dve.wait_ge(dstep, step.now())
            done(dve.reciprocal(inv[:, :], total[:, :]))
            done(dve.tensor_tensor(oh[:, :, :], p[:, :, :], wide(best[:, :]), ALU.is_equal))
            dve.wait_ge(dstep, step.now())
            done(dve.tensor_tensor(x2r[:, :, DM], best[:, :], inv[:, :], ALU.mult))
            done(dve.tensor_tensor(p[:, :, :], oh[:, :, :], every(eidx[:, :]), ALU.mult))
            dve.wait_ge(dstep, step.now())
            done(dve.tensor_reduce(first[:, :], p[:, :, :], AX.X, ALU.min))
            dve.wait_ge(dstep, step.now())
            dve.tensor_tensor(oh[:, :, :], every(eidx[:, :]), wide(first[:, :]), ALU.is_equal).then_inc(oh_ready, 1)

            dve.wait_ge(sums_ready, 1)
            done(dve.memset(cum[0][:, 0, :], 0.0))
            done(dve.tensor_copy(cum[0][:, 1:NT, :], V[:, 0:(NT - 1) * E].rearrange("p (t e) -> p t e", e=E)))
            now, shift = 0, 1
            while shift < NT:
                a, b = cum[now], cum[1 - now]
                dve.wait_ge(dstep, step.now())
                done(dve.tensor_copy(b[:, 0:shift, :], a[:, 0:shift, :]))
                done(dve.tensor_tensor(b[:, shift:NT, :], a[:, shift:NT, :], a[:, 0:NT - shift, :], ALU.add))
                now, shift = 1 - now, 2 * shift
            c = cum[now]
            dve.wait_ge(dstep, step.now())
            done(dve.tensor_tensor(count[:, :], V[:, (NT - 1) * E:NT * E], c[:, NT - 1, :], ALU.add))
            done(dve.tensor_tensor(cum[1 - now][:, :, :], U[:, 0:NT * E].rearrange("p (t e) -> p t e", e=E),
                                   c[:, :, :], ALU.add))
            rank = cum[1 - now]
            dve.wait_ge(dstep, step.now())
            done(dve.tensor_tensor(more[:, :, :], count[:, :].unsqueeze(2).to_broadcast([P, E, NT]),
                                   t128[:, :].unsqueeze(1).to_broadcast([P, E, NT]), ALU.is_gt))
            dve.wait_ge(dstep, step.now())
            done(dve.tensor_reduce(ntile[:, :], more[:, :, :], AX.X, ALU.add))
            done(dve.memset(start[:, 0:1], 0.0))
            for e in range(1, E):
                dve.wait_ge(dstep, step.now())
                done(dve.tensor_tensor(start[:, e:e + 1], start[:, e - 1:e], ntile[:, e - 1:e], ALU.add))
            dve.wait_ge(dstep, step.now())
            done(dve.tensor_tensor(tgt[:, :, 0:E - 1], tnum[:, :].unsqueeze(2).to_broadcast([1, XT, E - 1]),
                                   start[0:1, 1:E].unsqueeze(1).to_broadcast([1, XT, E - 1]), ALU.is_ge))
            dve.wait_ge(dstep, step.now())
            done(dve.tensor_scalar(start[:, :], start[:, :], float(P), None, ALU.mult))
            dve.wait_ge(dstep, step.now())
            done(dve.tensor_reduce(tef[:, :], tgt[:, :, 0:E - 1], AX.X, ALU.add))
            done(dve.tensor_tensor(rank[:, :, :], rank[:, :, :], every(start[:, :]), ALU.add))
            dve.wait_ge(dstep, step.now())
            done(dve.tensor_copy(tile_e[:, :], tef[:, :]))
            done(dve.tensor_tensor(rank[:, :, :], rank[:, :, :], oh[:, :, :], ALU.mult))
            dve.wait_ge(dstep, step.now())
            done(dve.tensor_reduce(posf[:, :], rank[:, :, :], AX.X, ALU.add))
            dve.wait_ge(dstep, step.now())
            dve.tensor_copy(pos[:, :], posf[:, :]).then_inc(pos_ready, 1)


def experts(nc, sem, d, XS, FS, tile_e):
    with ExitStack() as ctx:
        def sb(name, shape, dt=F32):
            return ctx.enter_context(nc.sbuf_tensor(name, shape, dt))

        w1 = sb("w1", [P, E, KT, FF])
        w2 = sb("w2", [P, E, FF // P, DM])
        b1 = sb("b1", [P, E, FF])
        b2 = sb("b2", [P, E, DM])
        ident = sb("ident4", [P, P])
        xs = sb("xs", [P, 4, ROW])
        xsT = sb("xsT", [P, 2, KT, P])
        hid = sb("hid", [P, 2, FF])
        hT = sb("hT", [P, FF // P, P])
        y = sb("y", [P, DM])
        r = sb("r4", [P, DM])
        st = sb("st4", [P, 6])
        mv = sb("mv4", [P, 2])
        rstd = sb("rstd4", [P, 1])
        veps = sb("veps4", [P, 1])
        mhalf = sb("mhalf4", [P, 1])
        fo = sb("fo", [P, 2, DM])
        HP = [ctx.enter_context(nc.psum_tensor(f"HP{i}", [P, FF], F32)) for i in range(2)]
        HT = [ctx.enter_context(nc.psum_tensor(f"HT{i}", [P, 512], F32)) for i in range(2)]
        XP = ctx.enter_context(nc.psum_tensor("XP", [P, 512], F32))
        YP = ctx.enter_context(nc.psum_tensor("YP", [P, 512], F32))
        consts = sem("e_consts")
        b_in = sem("e_b_in")
        w_in = sem("e_w_in")
        x_in = [sem(f"e_x_in{i}") for i in range(4)]
        xp_ready, xt_ready = sem("e_xp"), sem("e_xt")
        hp_ready, pre_ready = sem("e_hp"), sem("e_pre")
        act_ready = sem("e_act")
        ht_ready = [sem("e_ht0"), sem("e_ht1")]
        hs_ready = [sem("e_hs0"), sem("e_hs1")]
        yp_ready, y_ready = sem("e_yp"), sem("e_y")
        veps_ready = sem("e_veps")
        var_ready, rstd_ready = sem("e_var"), sem("e_rstd")
        f_ready = sem("e_f")
        f_out = [sem("e_fo0"), sem("e_fo1")]
        dstep = sem("e_dstep")
        passed = sem("e_passed")
        block = ctx.enter_context(nc.Block())
        XSv = XS.rearrange("(t p) n -> t p n", p=P)
        FSv = FS.rearrange("(t p) n -> t p n", p=P)
        HEAD, TAIL = 3, 4

        def tiles(eng, body):
            for t in range(HEAD):
                body(0, t)
            with eng.Fori(0, (XT - HEAD - TAIL) // 4) as m:
                for i in range(4):
                    body(m, HEAD + i)
            for t in range(XT - TAIL, XT):
                body(0, t)

        def is_last(m, k):
            return isinstance(m, int) and k == XT - 1

        def loads_ahead(m, k):
            return not (isinstance(m, int) and k >= XT - 2)

        @block.sync
        def _(sp):
            for e in range(E):
                sp.dma_start(w1[:, e], d["W1"][e].rearrange("(kt p) n -> p kt n", p=P)).then_inc(w_in, 16)
                sp.dma_start(w2[:, e], d["W2"][e].rearrange("(kt p) n -> p kt n", p=P)).then_inc(w_in, 16)
                sp.wait_ge(w_in, 32 * e + 32)

        @block.gpsimd
        def _(pool):
            for t in range(2):
                pool.dma_start(xs[:, t], XSv[t]).then_inc(x_in[t], 16)
            pool.memset(mhalf[:, :], -0.5)
            pool.memset(ident[:, :], 0.0).then_inc(consts, 1)
            pool.wait_ge(consts, 1)
            pool.affine_select(out=ident[:, :], in_=ident[:, :], compare_op=ALU.not_equal, fill=1.0,
                               base=0, pattern=[[-1, P]], channel_multiplier=1).then_inc(consts, 1)

            def tile(m, k):
                t, q = 4 * m + k, k % 4
                if loads_ahead(m, k):
                    pool.dma_start(xs[:, (q + 2) % 4], XSv[t + 2]).then_inc(x_in[(q + 2) % 4], 16)
                pool.wait_ge(var_ready, t + 1)
                pool.sem_inc(passed, 1)
                pool.tensor_scalar(veps[:, :], mv[:, 1:2], EPS, None, ALU.add).then_inc(veps_ready, 1)
                pool.wait_ge(veps_ready, t + 1)
                pool.tensor_tensor(rstd[:, :], veps[:, :], mhalf[:, :], ALU.pow).then_inc(rstd_ready, 1)
                pool.wait_ge(f_ready, t + 1)
                pool.dma_start(FSv[t], fo[:, q % 2]).then_inc(f_out[q % 2], 16)

            tiles(pool, tile)
            pool.wait_ge(f_out[0], 16 * 20)
            pool.wait_ge(f_out[1], 16 * 19)

        @block.tensor
        def _(pe):
            pe.wait_ge(consts, 2)

            def turn_x(t, q, x_count, fresh=False):
                pe.wait_ge(x_in[q], 16 * x_count)
                if not fresh:
                    pe.wait_ge(xt_ready, t)
                for i in range(KT):
                    mm = pe.transpose(XP[:, i * P:(i + 1) * P], xs[:, q, i * P:(i + 1) * P], ident[:, :])
                mm.then_inc(xp_ready, 1)

            def up(t, q, e, fresh=False):
                pe.wait_ge(w_in, 32 * e + 32)
                pe.wait_ge(xt_ready, t + 1)
                if not fresh:
                    pe.wait_ge(pre_ready, t - 1)
                for c in range(2):
                    for i in range(KT):
                        mm = pe.matmul(HP[q % 2][:, c * 512:(c + 1) * 512], xsT[:, q % 2, i, :],
                                       w1[:, e, i, c * 512:(c + 1) * 512], start=(i == 0), stop=(i == KT - 1))
                mm.then_inc(hp_ready, 1)

            def expert(t):
                return pe.value_load(tile_e[0:1, bass.ds(t, 1)], min_val=0, max_val=E - 1)

            turn_x(0, 0, 1, fresh=True)
            turn_x(1, 1, 1)
            up(0, 0, expert(0), fresh=True)

            def tile(m, k):
                t, q, first = 4 * m + k, k % 4, isinstance(m, int) and k == 0
                if not is_last(m, k):
                    up(t + 1, (q + 1) % 4, expert(t + 1), fresh=first)
                if loads_ahead(m, k):
                    turn_x(t + 2, (q + 2) % 4, m + (k + 2) // 4 + 1)
                pe.wait_ge(act_ready, t + 1)
                for bank in range(2):
                    if not first:
                        pe.wait_ge(hs_ready[bank], t)
                    for i in range(4):
                        j = 4 * bank + i
                        mm = pe.transpose(HT[bank][:, i * P:(i + 1) * P], hid[:, q % 2, j * P:(j + 1) * P], ident[:, :])
                    mm.then_inc(ht_ready[bank], 1)
                e = expert(t)
                if not first:
                    pe.wait_ge(y_ready, t)
                for j in range(FF // P):
                    if j % 4 == 0:
                        pe.wait_ge(hs_ready[j // 4], t + 1)
                    mm = pe.matmul(YP[:, 0:DM], hT[:, j, :], w2[:, e, j, :], start=(j == 0), stop=(j == FF // P - 1))
                mm.then_inc(yp_ready, 1)

            tiles(pe, tile)

        @block.scalar
        def _(act):
            act.dma_start(b1[:, :, :], d["b1"].partition_broadcast(P)).then_inc(b_in, 16)
            act.dma_start(b2[:, :, :], d["b2"].partition_broadcast(P)).then_inc(b_in, 16)

            def tile(m, k):
                t, q = 4 * m + k, k % 4
                act.wait_ge(pre_ready, t + 1)
                act.activation(hid[:, q % 2], hid[:, q % 2], ACT.Silu).then_inc(act_ready, 1)
                act.wait_ge(ht_ready[0], t + 1)
                act.activation(hT[:, 0:4, :], HT[0][:, :].rearrange("p (j i) -> p j i", i=P),
                               ACT.Copy).then_inc(hs_ready[0], 1)

            tiles(act, tile)

        @block.vector
        def _(dve):
            step = Steps()
            dve.wait_ge(b_in, 32)

            def expert(t):
                return dve.value_load(tile_e[0:1, bass.ds(t, 1)], min_val=0, max_val=E - 1)

            def turned(t, q):
                dve.wait_ge(xp_ready, t + 1)
                dve.tensor_copy(xsT[:, q % 2], XP[:, 0:DM].rearrange("p (k i) -> p k i", i=P)).then_inc(xt_ready, 1)

            def biased(t, q):
                e = expert(t)
                dve.wait_ge(hp_ready, t + 1)
                dve.tensor_tensor(hid[:, q % 2], HP[q % 2][:, :], b1[:, e, :], ALU.add).then_inc(pre_ready, 1)

            turned(0, 0)
            turned(1, 1)
            biased(0, 0)

            def tile(m, k):
                t, q = 4 * m + k, k % 4
                step.start(2 * t)
                if not is_last(m, k):
                    biased(t + 1, (q + 1) % 4)
                if loads_ahead(m, k):
                    turned(t + 2, (q + 2) % 4)
                dve.wait_ge(ht_ready[1], t + 1)
                dve.tensor_copy(hT[:, 4:8, :], HT[1][:, :].rearrange("p (j i) -> p j i", i=P)).then_inc(hs_ready[1], 1)
                e = expert(t)
                dve.wait_ge(yp_ready, t + 1)
                dve.tensor_tensor(y[:, :], YP[:, 0:DM], b2[:, e, :], ALU.add).then_inc(y_ready, 1)
                dve.wait_ge(y_ready, t + 1)
                dve.scalar_tensor_tensor(out=r[:, :], in0=y[:, :], scalar=xs[:, q, DM:DM + 1], in1=xs[:, q, 0:DM],
                                         op0=ALU.mult, op1=ALU.add).then_inc(dstep, step.one())
                dve.wait_ge(dstep, step.now())
                dve.bn_stats(st[:, :], r[:, :]).then_inc(dstep, step.one())
                dve.wait_ge(dstep, step.now())
                dve.sem_inc(passed, 1)
                dve.bn_aggr(mv[:, :], st[:, :]).then_inc(var_ready, 1)
                dve.wait_ge(rstd_ready, t + 1)
                if not (isinstance(m, int) and k < 2):
                    dve.wait_ge(f_out[k % 2], 32 * m + 16 * (k // 2))
                dve.tensor_scalar(fo[:, q % 2], r[:, :], mv[:, 0:1], rstd[:, :], ALU.subtract,
                                  ALU.mult).then_inc(f_ready, 1)

            tiles(dve, tile)


def unsort(nc, sem, FS, pos, out):
    with ExitStack() as ctx:
        rows = ctx.enter_context(nc.sbuf_tensor("rows", [P, NT, DM], F32))
        got = [sem(f"u_got{i}") for i in range(NT // 4)]
        stored = sem("u_stored")
        block = ctx.enter_context(nc.Block())
        outv = out.rearrange("(t p) n -> p t n", p=P)

        @block.gpsimd
        def _(pool):
            for t in range(NT):
                pool.indirect_dma_start(rows[:, t, :], None, FS,
                                        bass.IndirectOffsetOnAxis(ap=pos[:, t:t + 1], axis=0)).then_inc(got[t // 4], 16)

        @block.sync
        def _(sp):
            for i in range(NT // 4):
                sp.wait_ge(got[i], 64)
                sp.dma_start(outv[:, 4 * i:4 * i + 4, :], rows[:, 4 * i:4 * i + 4, :]).then_inc(stored, 16)
            sp.wait_ge(stored, 16 * (NT // 4))


def decoder_layer(nc, a, out):
    OT = nc.dram_tensor("attention_t", (NI, P, L), F32).ap()
    XS = nc.dram_tensor("sorted_rows", (XT * P, ROW), F32).ap()
    FS = nc.dram_tensor("sorted_out", (XT * P, DM), F32).ap()

    def by_row_tile(w):
        return w.rearrange("(k p) n -> p k n", p=P)

    d = {
        "x": a["x"].rearrange("b (c a p) n -> p b c a n", c=2, p=P),
        "wo": by_row_tile(a["attn_W_out"]), "ctxT": by_row_tile(a["ctxT"]),
        "wq": by_row_tile(a["xattn_W_qT"]), "wk": by_row_tile(a["xattn_W_kT"]),
        "wv": by_row_tile(a["xattn_W_vT"]),
        "wox": a["xattn_W_outT"].rearrange("(g i e) n -> i e g n", i=4, e=XD),
        "bq": a["xattn_b_q"], "bk": a["xattn_b_k"], "bv": a["xattn_b_v"], "bo": a["xattn_b_out"],
        "wg": by_row_tile(a["ffn_Wg"]), "bg": a["ffn_bg"],
        "W1": a["ffn_W1"], "b1": a["ffn_b1"], "W2": a["ffn_W2"], "b2": a["ffn_b2"],
    }
    with ExitStack() as ctx:
        def sem(name):
            return ctx.enter_context(nc.semaphore(name))

        pos = ctx.enter_context(nc.sbuf_tensor("pos", [P, NT], I32))
        tile_e = ctx.enter_context(nc.sbuf_tensor("tile_e", [1, XT], I32))
        self_attention(nc, sem, by_row_tile(a["xT"]), a["attn_W_qkv"], OT, XS)
        with ExitStack() as rows:
            x2r = rows.enter_context(nc.sbuf_tensor("x2r", [P, NT, ROW], F32))
            logits = rows.enter_context(nc.sbuf_tensor("logits", [P, NT, E], F32))
            token_groups(nc, sem, d, OT, x2r, logits)
            route(nc, sem, x2r, logits, pos, tile_e, XS)
        experts(nc, sem, d, XS, FS, tile_e)
        unsort(nc, sem, FS, pos, out)


def kernel(**inputs):
    import numpy as np
    import concourse.bacc as bacc
    from concourse.bass_utils import run_bass_kernel_spmd

    i = {k: np.asarray(v) for k, v in inputs.items()}
    lay = {
        "x": i["x"], "xT": i["x"].reshape(TOK, DM).T,
        "ctxT": i["ctx_1024"].reshape(B * SC, DM).T,
        "attn_W_qkv": i["L0_attn_W_qkv"], "attn_W_out": i["L0_attn_W_out"],
        "xattn_W_qT": i["L0_xattn_W_q"].T, "xattn_W_kT": i["L0_xattn_W_k"].T,
        "xattn_W_vT": i["L0_xattn_W_v"].T, "xattn_W_outT": i["L0_xattn_W_out"].T,
        "xattn_b_q": i["L0_xattn_b_q"].reshape(KT, P).T, "xattn_b_k": i["L0_xattn_b_k"].reshape(KT, P).T,
        "xattn_b_v": i["L0_xattn_b_v"], "xattn_b_out": i["L0_xattn_b_out"],
        "ffn_Wg": i["L0_ffn_Wg"], "ffn_bg": i["L0_ffn_bg"], "ffn_W1": i["L0_ffn_W1"],
        "ffn_b1": i["L0_ffn_b1"], "ffn_W2": i["L0_ffn_W2"], "ffn_b2": i["L0_ffn_b2"],
    }
    nc = bacc.Bacc("TRN2", target_bir_lowering=False, num_devices=1)
    arrays, aps = {}, {}
    for name, v in lay.items():
        arrays[f"in_{name}"] = np.ascontiguousarray(v)
        aps[name] = nc.dram_tensor(f"in_{name}", v.shape, F32, kind="ExternalInput").ap()
    out = nc.dram_tensor("out", (TOK, DM), F32, kind="ExternalOutput").ap()
    decoder_layer(nc, aps, out)
    r = run_bass_kernel_spmd(nc, [arrays], core_ids=[0])
    return r.results[0]["out"].reshape(B, L, DM)
```

```python
import concourse.bass as bass
from concourse import mybir
from contextlib import ExitStack

F32 = mybir.dt.float32
F32R = mybir.dt.float32r
BF16 = mybir.dt.bfloat16
I32 = mybir.dt.int32
U32 = mybir.dt.uint32
ALU = mybir.AluOpType
ACT = mybir.ActivationFunctionType
AX = mybir.AxisListType

P = 128
B, L, DM = 4, 1024, 256
TOK = B * L
H, D = 16, 64
PAIRS = H // 2
NI = B * PAIRS
KT = DM // P
LT = L // P
SC = 77
XD = DM // H
E, FF = 8, 1024
NT = TOK // P
XT = NT + E - 1
ROW = 264
EPS = 1e-5
BIG = -1e30


PROJECT = {1: 0, 3: 1, 6: 2, 8: 3, 10: 4, 12: 5}
KEYS1 = {0: [0], 2: [1, 2], 4: [3, 4], 5: [5, 6, 7]}
KEYS0 = {11: [0], 13: [1], 14: [2, 3]}
SPREAD0 = 9


def lookahead(s):
    return (s + 2) // 16, (s + 2) % 16


def self_attention(nc, sem, xT, w_qkv, OT, XS):
    with ExitStack() as ctx:
        def sb(name, shape, dt=F32):
            return ctx.enter_context(nc.sbuf_tensor(name, shape, dt))

        xf = sb("xf", [P, KT, L])
        xh = sb("xh", [P, KT, L], F32R)
        xl = sb("xl", [P, KT, L], F32R)
        wraw = sb("wraw", [P, 2, KT, 3, P])
        wh = sb("wh", [P, 2, KT, 2, P], F32R)
        wl = sb("wl", [P, 2, KT, 2, P], F32R)
        qs = sb("qs", [P, 2, 2, L], F32R)
        k1 = sb("k1", [P, 2, 2, L], F32R)
        k2 = sb("k2", [P, 2, 2, L], F32R)
        v = sb("v", [P, 2, LT, P])
        prob = sb("prob", [P, 4, L])
        pt = [sb("pt0", [P, 2, 4, 512]), sb("pt1", [P, 2, 8, 512])]
        nmax = sb("nmax", [P, 2])
        sums = sb("sums", [P, 2, LT, 2])
        rec = sb("rec", [P, 2, LT, 2 * D])
        inv = sb("inv", [P, 8])
        rb = sb("rb", [P, 2, 512])
        ob = sb("ob", [P, 2, 512])
        ident = sb("ident", [P, P])
        identb = sb("identb", [P, P], BF16)
        maskb = sb("maskb", [P, P], BF16)
        S = [ctx.enter_context(nc.psum_tensor(f"S{i}", [P, L], F32)) for i in range(2)]
        TP = [ctx.enter_context(nc.psum_tensor(f"TP{i}", [P, 512], F32)) for i in range(2)]
        OP = ctx.enter_context(nc.psum_tensor("OP", [P, 512], F32))
        PR = ctx.enter_context(nc.psum_tensor("PR", [P, 512], F32))

        zero = sb("zero", [P, ROW])
        const_ready = sem("const_ready")
        zero_ready = sem("zero_ready")
        zero_out = sem("zero_out")
        passed = sem("a_passed")
        x_in = [sem("x_in0"), sem("x_in1")]
        w_in = [sem("w_in0"), sem("w_in1")]
        split = sem("split")
        high_split = sem("high_split")
        pr_ready = sem("pr_ready")
        hi_ready = sem("hi_ready")
        lo_ready = sem("lo_ready")
        v_ready = sem("v_ready")
        k2_ready = sem("k2_ready")
        s_ready = sem("s_ready")
        max_ready = sem("max_ready")
        p_ready = sem("p_ready")
        tp_ready = [sem("tp_ready0"), sem("tp_ready1")]
        pt_ready = [sem("pt_ready0"), sem("pt_ready1")]
        inv_ready = sem("inv_ready")
        rec_ready = sem("rec_ready")
        r_ready = sem("r_ready")
        rb_ready = sem("rb_ready")
        o_ready = sem("o_ready")
        ob_ready = sem("ob_ready")
        o_out = [sem("o_out0"), sem("o_out1")]
        block = ctx.enter_context(nc.Block())

        wv = w_qkv.rearrange("(kt p) (three c) -> p kt three c", p=P, three=3)

        def load_w(eng, par, pair):
            for kt in range(KT):
                eng.dma_start(wraw[:, par, kt], wv[:, kt, :, pair * P:(pair + 1) * P]).then_inc(w_in[par], 16)

        @block.sync
        def _(sp):
            def load_x(b, c):
                sp.dma_start(xf[:, :, c * 512:(c + 1) * 512],
                             xT[:, :, bass.ds(b * L + c * 512, 512)]).then_inc(x_in[c], 16)

            def swap(par, count):
                sp.wait_ge(lo_ready, count)
                for h in range(2):
                    for half in range(2):
                        a, z = half * 64, 64 - half * 64
                        sp.dma_start(k2[a:a + 64, par, h].bitcast(F32), k1[z:z + 64, par, h].bitcast(F32)).then_inc(k2_ready, 16)

            def store(n, c, count):
                sp.wait_ge(ob_ready, count)
                sp.dma_start(OT[n, :, c * 512:(c + 1) * 512], ob[:, c]).then_inc(o_out[c], 16)

            load_w(sp, 0, 0)
            load_x(0, 0)
            load_x(0, 1)
            load_w(sp, 1, 1)
            sp.wait_ge(zero_ready, 1)
            sp.dma_start(XS.rearrange("(t p) n -> p t n", p=P),
                         zero[:, :].unsqueeze(1).to_broadcast([P, XT, ROW])).then_inc(zero_out, 16)
            swap(0, 4)

            def batch(b, first, last):
                for n8 in range(PAIRS):
                    n = b * PAIRS + n8
                    if not (first and n8 == 0):
                        store(n - 1, 1, 2 * n)
                    if not (last and n8 == PAIRS - 1):
                        swap((n8 + 1) % 2, 8 * n + 12)
                    if not (last and n8 >= PAIRS - 2):
                        load_w(sp, n8 % 2, (n8 + 2) % PAIRS)
                        if n8 == PAIRS - 2:
                            for c in range(2):
                                sp.wait_ge(v_ready, 2 * n + 3 + c)
                                load_x(b + 1, c)
                    store(n, 0, 2 * n + 1)

            batch(0, True, False)
            with sp.Fori(1, B - 1) as b:
                batch(b, False, False)
            batch(B - 1, False, True)
            store(NI - 1, 1, 2 * NI)
            for c in range(2):
                sp.wait_ge(o_out[c], 16 * NI)
            sp.wait_ge(zero_out, 16)

        @block.gpsimd
        def _(pool):
            pool.memset(ident[:, :], 0.0).then_inc(const_ready, 1)
            pool.memset(maskb[:, :], 0.0).then_inc(const_ready, 1)
            pool.memset(zero[:, :], 0.0).then_inc(zero_ready, 1)
            pool.wait_ge(const_ready, 2)
            pool.affine_select(out=ident[:, :], in_=ident[:, :], compare_op=ALU.not_equal, fill=1.0,
                               base=0, pattern=[[-1, P]], channel_multiplier=1).then_inc(const_ready, 1)
            pool.affine_select(out=maskb[:, :], in_=maskb[:, :], compare_op=ALU.is_ge, fill=BIG,
                               base=0, pattern=[[-1, P]], channel_multiplier=1).then_inc(const_ready, 1)
            pool.wait_ge(const_ready, 4)
            pool.tensor_copy(identb[:, :], ident[:, :]).then_inc(const_ready, 1)

            step = Steps()

            def split_in_two(high, low, whole, last=None):
                pool.tensor_copy(high, whole).then_inc(high_split, step.one())
                pool.wait_ge(high_split, step.now())
                ins = pool.tensor_tensor(low, whole, high, ALU.subtract)
                if last is not None:
                    ins.then_inc(last, 1)

            def batch(b):
                step.start((2 * PAIRS + 2) * b)
                for k8 in range(PAIRS):
                    par = k8 % 2
                    for c, qk in ((0, 1), (1, 0)):
                        if k8 == 0:
                            pool.wait_ge(x_in[c], 16 * b + 16)
                            pool.sem_inc(passed, 1)
                            cols = slice(c * 512, (c + 1) * 512)
                            split_in_two(xh[:, :, cols], xl[:, :, cols], xf[:, :, cols])
                        if c == 0:
                            pool.wait_ge(w_in[par], 128 * b + 32 * (k8 // 2 + 1))
                            pool.sem_inc(passed, 1)
                        split_in_two(wh[:, par, :, qk, :], wl[:, par, :, qk, :], wraw[:, par, :, qk, :], split)

            batch(0)
            with pool.Fori(1, B) as b:
                batch(b)

        def pairs(eng, body):
            body(0, 0, True, False)
            body(1, 1, False, False)
            with eng.Fori(1, NI // 2 - 1) as m:
                body(2 * m, 0, False, False)
                body(2 * m + 1, 1, False, False)
            body(NI - 2, 0, False, False)
            body(NI - 1, 1, False, True)

        @block.tensor
        def _(pe):
            pe.wait_ge(const_ready, 5)

            def project(k, par, j, first=False):
                if j <= 1:
                    pe.wait_ge(split, 2 * k + j + 1)
                if j == 0 and not first:
                    pe.wait_ge(v_ready, 2 * k)
                    if not (isinstance(k, int) and k == 1):
                        pe.wait_ge(rb_ready, 2 * k - 2)
                if 1 <= j <= 3 or (first and j == 4):
                    pe.wait_ge(lo_ready, 8 * k + 2 * j)
                if j == 4 and not first:
                    pe.wait_ge(rb_ready, 2 * k - 1)
                if j == 5:
                    pe.wait_ge(v_ready, 2 * k + 1)
                if j < 4:
                    qk, c = 1 - j // 2, j % 2
                    terms = [(w, x, kt) for kt in range(KT) for w, x in ((wl, xh), (wh, xl), (wh, xh))]
                    for i, (w, x, kt) in enumerate(terms):
                        mm = pe.matmul(PR[:, :], w[:, par, kt, qk, :], x[:, kt, c * 512:(c + 1) * 512],
                                       start=(i == 0), stop=(i == len(terms) - 1))
                else:
                    for a in range(4):
                        t = (j - 4) * 4 + a
                        for kt in range(KT):
                            mm = pe.matmul(PR[:, a * P:(a + 1) * P], xf[:, kt, t * P:(t + 1) * P],
                                           wraw[:, par, kt, 2, :], start=(kt == 0), stop=(kt == KT - 1))
                mm.then_inc(pr_ready, 1)

            def scores(n, par, s, fresh=False):
                t, h = s // 2, s % 2
                if s == 0:
                    pe.wait_ge(lo_ready, 8 * n + 8)
                    pe.wait_ge(k2_ready, 64 * n + 64)
                if not (fresh and s < 2):
                    pe.wait_ge(p_ready, 16 * n + s - 1)
                width = (t + 1) * P
                for c in range((width + 511) // 512):
                    n_cols = max(min(width - 512 * c, 512), 256)
                    cols = slice(512 * c, 512 * c + n_cols)
                    q = qs[:, par, h, t * P:(t + 1) * P]
                    pe.matmul(S[s % 2][:, cols], q, k2[:, par, h, cols], start=True, stop=False)
                    mm = pe.matmul(S[s % 2][:, cols], q, k1[:, par, h, cols], start=False, stop=True)
                pe.matmul(S[s % 2][:, t * P:(t + 1) * P], identb[:, :], maskb[:, :], start=False, stop=True,
                          skip_group_check=True).then_inc(s_ready, 1)

            def transposes(n, s, fresh=False):
                t = s // 2
                pe.wait_ge(p_ready, 16 * n + s + 1)
                for bank in ([s % 2] if t < 4 else [0, 1]):
                    use = s // 2 if s < 8 else s - 4
                    if not (fresh and use == 0):
                        pe.wait_ge(pt_ready[bank], 12 * n + use)
                    j0 = 0 if t < 4 else 4 * bank
                    for j in range(j0, min(j0 + 4, t + 1)):
                        mm = pe.transpose(TP[bank][:, (j - j0) * P:(j - j0 + 1) * P],
                                          prob[:, s % 4, j * P:(j + 1) * P], ident[:, :])
                    mm.then_inc(tp_ready[bank], 1)

            def spread(n, par, c, last=False):
                pe.wait_ge(rec_ready, 2 * n + c + 1)
                if last:
                    pe.wait_ge(rb_ready, 2 * n + c)
                elif c == 0:
                    pe.wait_ge(lo_ready, 8 * n + 16)
                else:
                    pe.wait_ge(v_ready, 2 * n + 4)
                for a in range(4):
                    mm = pe.transpose(PR[:, a * P:(a + 1) * P],
                                      rec[:, par, 4 * c + a, :], ident[:, :])
                mm.then_inc(r_ready, 1)

            def weigh(n, par, c, keys, fresh=False):
                if keys[0] == 0:
                    for bank in range(2):
                        pe.wait_ge(pt_ready[bank], 12 * n + (4 if c == 0 else 12))
                    pe.wait_ge(v_ready, 2 * n + 2)
                    if not fresh:
                        pe.wait_ge(ob_ready, 2 * n + c)
                for j in keys:
                    i0 = max(0, j - 4 * c) * P
                    for h in range(2):
                        mm = pe.matmul(OP[h * D:(h + 1) * D, i0:512], v[:, par, j, h * D:(h + 1) * D],
                                       pt[c][:, h, j, i0:512], start=(j == 0), stop=(j == 4 * c + 3))
                if keys[-1] == 4 * c + 3:
                    mm.then_inc(o_ready, 1)

            for j in range(6):
                project(0, 0, j, first=True)
            scores(0, 0, 0, fresh=True)
            scores(0, 0, 1, fresh=True)

            def iteration(n, par, first, last):
                for s in range(16):
                    ahead, s2 = lookahead(s)
                    if not (last and ahead):
                        scores(n + ahead, (par + ahead) % 2, s2)
                    transposes(n, s, fresh=first)
                    if not first and s == 0:
                        spread(n - 1, 1 - par, 1)
                    if not first and s in KEYS1:
                        weigh(n - 1, 1 - par, 1, KEYS1[s])
                    if not last and s in PROJECT:
                        project(n + 1, 1 - par, PROJECT[s])
                    if s == SPREAD0:
                        spread(n, par, 0, last)
                    if s in KEYS0:
                        weigh(n, par, 0, KEYS0[s], fresh=first)

            pairs(pe, iteration)
            spread(NI - 1, 1, 1, True)
            weigh(NI - 1, 1, 1, range(8))

        @block.scalar
        def _(act):
            def high(k, par, j, first=False):
                c = j % 2
                act.wait_ge(pr_ready, 6 * k + j + 1)
                for h in range(2):
                    rows = slice(h * 64, h * 64 + 64)
                    out = (k1 if j < 2 else qs)[rows, par, h, c * 512:(c + 1) * 512]
                    act.activation(out, PR[rows, :], ACT.Copy,
                                   scale=1.0 if j < 2 else D ** -0.5).then_inc(hi_ready, 1)

            def expo(n, par, s):
                t, h = s // 2, s % 2
                act.wait_ge(max_ready, 16 * n + s + 1)
                act.activation(prob[:, s % 4, 0:(t + 1) * P], S[s % 2][:, 0:(t + 1) * P], ACT.Exp,
                               bias=nmax[:, s % 2:s % 2 + 1],
                               accum_out=sums[:, par, t, h:h + 1]).then_inc(p_ready, 1)

            def evacuate(n, s):
                t, h = s // 2, s % 2
                use = s // 2 if s < 8 else s - 4
                act.wait_ge(tp_ready[0], 12 * n + use + 1)
                nb = min(4, t + 1)
                act.activation(pt[t // 4][:, h, 0:nb, (t % 4) * P:(t % 4 + 1) * P],
                               TP[0][:, 0:nb * P].rearrange("p (j i) -> p j i", i=P),
                               ACT.Copy).then_inc(pt_ready[0], 1)

            def spread_copy(n, c):
                act.wait_ge(r_ready, 2 * n + c + 1)
                act.activation(rb[:, c], PR[:, :], ACT.Copy).then_inc(rb_ready, 1)

            for j in range(4):
                high(0, 0, j)
            expo(0, 0, 0)
            expo(0, 0, 1)

            def iteration(n, par, first, last):
                for s in range(16):
                    if s >= 8 or s % 2 == 0:
                        evacuate(n, s)
                    ahead, s2 = lookahead(s)
                    if not (last and ahead):
                        expo(n + ahead, (par + ahead) % 2, s2)
                    if s == 0 and not first:
                        spread_copy(n - 1, 1)
                    if not last and PROJECT.get(s, 4) < 4:
                        high(n + 1, 1 - par, PROJECT[s])
                    if s == SPREAD0:
                        spread_copy(n, 0)

            pairs(act, iteration)
            spread_copy(NI - 1, 1)

        @block.vector
        def _(dve):
            def low(k, par, j):
                c = j % 2
                for h in range(2):
                    rows, other = slice(h * 64, h * 64 + 64), slice(64 - h * 64, 128 - h * 64)
                    stack = (k1 if j < 2 else qs)
                    dve.wait_ge(hi_ready, 8 * k + 2 * j + 2)
                    dve.scalar_tensor_tensor(
                        out=stack[other, par, h, c * 512:(c + 1) * 512], in0=PR[rows, :],
                        scalar=1.0 if j < 2 else D ** -0.5,
                        in1=stack[rows, par, h, c * 512:(c + 1) * 512].bitcast(F32),
                        op0=ALU.mult, op1=ALU.subtract).then_inc(lo_ready, 1)

            def values(k, par, j):
                dve.wait_ge(pr_ready, 6 * k + j + 1)
                dve.tensor_copy(v[:, par, 4 * (j - 4):4 * (j - 4) + 4, :],
                                PR[:, :].rearrange("p (a c) -> p a c", c=P)).then_inc(v_ready, 1)

            def row_max(n, s):
                t = s // 2
                dve.wait_ge(s_ready, 16 * n + s + 1)
                dve.tensor_reduce(nmax[:, s % 2:s % 2 + 1], S[s % 2][:, 0:(t + 1) * P], AX.X, ALU.max,
                                  negate=True).then_inc(max_ready, 1)

            def evacuate(n, s):
                t, h = s // 2, s % 2
                use = s // 2 if s < 8 else s - 4
                dve.wait_ge(tp_ready[1], 12 * n + use + 1)
                j0 = 0 if t < 4 else 4
                nb = t + 1 - j0
                dve.tensor_copy(pt[t // 4][:, h, j0:j0 + nb, (t % 4) * P:(t % 4 + 1) * P],
                                TP[1][:, 0:nb * P].rearrange("p (j i) -> p j i", i=P)).then_inc(pt_ready[1], 1)

            def reciprocals(n, par, c):
                dve.wait_ge(p_ready, 16 * n + 8 * c + 8)
                dve.reciprocal(inv[:, :], sums[:, par, 4 * c:4 * c + 4, :].rearrange("p t h -> p (t h)"))\
                   .then_inc(inv_ready, 1)
                dve.wait_ge(inv_ready, 2 * n + c + 1)
                dve.tensor_copy(rec[:, par, 4 * c:4 * c + 4, :].rearrange("p t (h d) -> p (t h) d", h=2),
                                inv[:, :].unsqueeze(2).to_broadcast([P, 8, D])).then_inc(rec_ready, 1)

            def normalise(n, c, fresh):
                dve.wait_ge(o_ready, 2 * n + c + 1)
                dve.wait_ge(rb_ready, 2 * n + c + 1)
                if not fresh:
                    dve.wait_ge(o_out[c], 16 * n)
                dve.tensor_tensor(ob[:, c], OP[:, :], rb[:, c], ALU.mult).then_inc(ob_ready, 1)

            for j in range(6):
                (low if j < 4 else values)(0, 0, j)
            row_max(0, 0)
            row_max(0, 1)

            def iteration(n, par, first, last):
                for s in range(16):
                    ahead, s2 = lookahead(s)
                    if not (last and ahead):
                        row_max(n + ahead, s2)
                    if s >= 8 or s % 2 == 1:
                        evacuate(n, s)
                    if not last and s in PROJECT:
                        (low if PROJECT[s] < 4 else values)(n + 1, 1 - par, PROJECT[s])
                    if s == max(KEYS1) + 1 and not first:
                        normalise(n - 1, 1, fresh=isinstance(n, int) and n == 1)
                    if s == SPREAD0 - 1:
                        reciprocals(n, par, 0)
                    if s == max(KEYS0) + 1:
                        normalise(n, 0, fresh=first)
                    if s == 15:
                        reciprocals(n, par, 1)

            pairs(dve, iteration)
            normalise(NI - 1, 1, fresh=False)


class Steps:

    def __init__(self):
        self.base, self.n = 0, 0

    def start(self, base):
        self.base, self.n = base, 0

    def one(self):
        self.n += 1
        return 1

    def now(self):
        return self.base + self.n


def token_groups(nc, sem, d, OT, x2r, logits):
    NG, GT = TOK // 512, 4
    HC = 4
    with ExitStack() as ctx:
        def sb(name, shape, dt=F32):
            return ctx.enter_context(nc.sbuf_tensor(name, shape, dt))

        wo = sb("wo", [P, PAIRS, DM])
        wq = sb("wq", [P, KT, DM])
        wk = sb("wk", [P, KT, DM])
        wvx = sb("wvx", [P, KT, DM])
        wox = sb("wox", [P, 4, DM])
        wg = sb("wg", [P, KT, E])
        ctxT = sb("ctxT", [P, KT, B * SC])
        bq = sb("bq", [P, KT])
        bk = sb("bk", [P, KT])
        bv = sb("bv", [SC, DM])
        bo = sb("bo", [P, DM])
        bg = sb("bg", [P, E])
        ident = sb("ident2", [P, P])
        hmask = sb("hmask", [P, 8])
        kbd_all = sb("kbd_all", [P, B, KT, 8 * SC])
        vx_all = sb("vx_all", [SC, B, H, 32])
        kbd = sb("kbd", [P, KT, 8 * SC])
        vx = sb("vx", [SC, H, 32])
        ot = sb("ot", [P, PAIRS, 512])
        xin = sb("xin", [P, GT, DM])
        r = sb("r", [P, 2, DM])
        st = sb("st", [P, 6])
        mv = sb("mv", [P, 2, 2])
        rstd = sb("rstd", [P, 2])
        veps = sb("veps", [P, 1])
        mhalf = sb("mhalf", [P, 1])
        x1 = sb("x1", [P, 2, GT, DM])
        x1b = sb("x1b", [P, 2, GT, DM])
        x1T = sb("x1T", [P, KT, 512])
        kT = x1T[:, :, 0:B * SC]
        qT = sb("qT", [P, KT, 512])
        sc = sb("sc", [P, GT, H * SC])
        mx = sb("mx", [P, GT, H])
        sm = sb("sm", [P, GT, H])
        rc = sb("rc", [P, GT, H])
        pT = sb("pT", [SC, H, 512])
        oT = sb("oT", [P, 4, 512])
        x2 = sb("x2", [P, GT, DM])
        x2T = sb("x2T", [P, GT, KT, P])
        SP = [ctx.enter_context(nc.psum_tensor(f"SP{i}", [P, 512], F32)) for i in range(4)]
        M = [ctx.enter_context(nc.psum_tensor(f"M{i}", [P, 512], F32)) for i in range(2)]
        T = [ctx.enter_context(nc.psum_tensor(f"T{i}", [P, 512], F32)) for i in range(2)]

        w_in = sem("g_w_in")
        small_in = sem("g_small_in")
        consts = sem("g_consts")
        kv_psum = sem("g_kv_psum")
        kv_sb = sem("g_kv_sb")
        kv_all = sem("g_kv_all")
        k_now, v_now = sem("g_k_now"), sem("g_v_now")
        in_ready = sem("g_in")
        m_ready = [sem("g_m_ready0"), sem("g_m_ready1")]
        m_free = [sem("g_m_free0"), sem("g_m_free1")]
        t_ready = [sem("g_t_ready0"), sem("g_t_ready1")]
        t_free = [sem("g_t_free0"), sem("g_t_free1")]
        sc_ready = sem("g_sc_ready")
        sc_free = sem("g_sc_free")
        exp_ready = sem("g_exp_ready")
        inv_ready = sem("g_inv_ready")
        p_ready = sem("g_p_ready")
        x1_ready = sem("g_x1_ready")
        x1b_ready = sem("g_x1b_ready")
        x2_ready = sem("g_x2_ready")
        x2_kept = sem("g_x2_kept")
        veps_ready = sem("g_veps_ready")
        var_ready = sem("g_var_ready")
        rstd_ready = sem("g_rstd_ready")
        passed = sem("g_passed")
        dstep = sem("g_dstep")
        block = ctx.enter_context(nc.Block())

        BEFORE = "p0 p1 p2 p3 x0 x1 x2 x3 q0 q1".split()
        DURING = "p0 p1 p2 p3 x0 x1 x2 x3 o0 o1 o2 o3 q0 y0 y1 q1 y2 y3".split()
        LAST = "o0 o1 o2 o3 y0 y1 y2 y3".split()

        def use(g, name):
            names = BEFORE if g is None else LAST if isinstance(g, int) and g == NG - 1 else DURING
            u = names.index(name)
            return u % 2, (0 if g is None else 5 + 9 * g) + u // 2

        def t_use(g, name):
            bank, nth = {"t0": (0, 0), "t1": (1, 0), "t2": (0, 1), "t3": (1, 1), "logits": (0, 2)}[name]
            return bank, (11 * g - 3, 10 * g - 2)[bank] + nth

        def p_use(g, a, q):
            bank, nth = q % 2, 2 * a + q // 2
            return bank, nth if isinstance(g, int) and g == 0 else (11 * g, 10 * g)[bank] + nth

        def groups(eng, body):
            body(0, 0, True, False)
            body(1, 1, False, False)
            with eng.Fori(1, NG // 2 - 1) as m:
                body(2 * m, 0, False, False)
                body(2 * m + 1, 1, False, False)
            body(NG - 2, 0, False, False)
            body(NG - 1, 1, False, True)

        OTv = OT.rearrange("(b r) p (c i) -> p b r c i", b=B, c=2)

        @block.sync
        def _(sp):
            def load(b, c):
                sp.dma_start(ot[:, :, :], OTv[:, b, :, c, :]).then_inc(in_ready, 16)
                sp.dma_start(xin[:, :, :], d["x"][:, b, c]).then_inc(in_ready, 16)

            sp.dma_start(wk[:, :, :], d["wk"]).then_inc(w_in, 16)
            sp.dma_start(wvx[:, :, :], d["wv"]).then_inc(w_in, 16)
            sp.dma_start(ctxT[:, :, :], d["ctxT"]).then_inc(w_in, 16)
            sp.dma_start(wo[:, :, :], d["wo"]).then_inc(w_in, 16)
            load(0, 0)
            sp.dma_start(wq[:, :, :], d["wq"]).then_inc(w_in, 16)
            sp.dma_start(wg[:, :, :], d["wg"]).then_inc(w_in, 16)
            sp.wait_ge(x1_ready, 4)
            load(0, 1)
            with sp.Fori(1, B) as b:
                sp.wait_ge(x1_ready, 8 * b)
                load(b, 0)
                sp.wait_ge(x1_ready, 8 * b + 4)
                load(b, 1)

        @block.gpsimd
        def _(pool):
            pool.memset(ident[:, :], 0.0).then_inc(consts, 1)
            pool.memset(hmask[:, :], 1.0).then_inc(consts, 1)
            pool.memset(mhalf[:, :], -0.5)
            pool.memset(vx_all[:, :, :, :], 0.0).then_inc(consts, 1)
            pool.memset(wox[:, :, :], 0.0).then_inc(consts, 1)
            pool.memset(x2r[:, :, DM:ROW], 0.0).then_inc(consts, 1)
            pool.wait_ge(consts, 5)
            pool.affine_select(out=ident[:, :], in_=ident[:, :], compare_op=ALU.not_equal, fill=1.0,
                               base=0, pattern=[[-1, P]], channel_multiplier=1).then_inc(consts, 1)
            pool.affine_select(out=hmask[:, :], in_=hmask[:, :], compare_op=ALU.is_ge, fill=0.0,
                               base=0, pattern=[[-XD, 8]], channel_multiplier=1).then_inc(consts, 1)
            pool.wait_ge(consts, 7)
            pool.affine_select(out=hmask[:, :], in_=hmask[:, :], compare_op=ALU.is_ge, fill=0.0,
                               base=XD - 1, pattern=[[XD, 8]], channel_multiplier=-1).then_inc(consts, 1)
            pool.wait_ge(small_in, 16 * 9)
            pool.wait_ge(kv_all, 4 * KT + B)

            def group(g, par, first, last):
                b = batch[0]
                if par == 0:
                    if not first:
                        bank, before = use(g - 1, "o3")
                        pool.wait_ge(m_ready[bank], before + 1)
                        pool.sem_inc(passed, 1)
                    pool.tensor_copy(vx[:, :, :], vx_all[:, b]).then_inc(v_now, 1)
                if first:
                    pool.tensor_copy(kbd[:, :, :], kbd_all[:, 0]).then_inc(k_now, 1)
                    for a in range(GT):
                        root(a, a)
                    bias_x1(0, 0)
                for a in range(3):
                    if not last:
                        root(8 * g + 4 + a, a)
                    share_out(g, a)
                share_out(g, 3)
                if not last:
                    root(8 * g + 7, 3)
                if par == 1 and not last:
                    pool.wait_ge(sc_ready, 16 * g + 16)
                    pool.sem_inc(passed, 1)
                    pool.tensor_copy(kbd[:, :, :], kbd_all[:, b + 1]).then_inc(k_now, 1)
                if not last:
                    bias_x1(g + 1, 1 - par)
                for a in range(GT + 1):
                    if a < GT:
                        root(8 * g + (4 if last else 8) + a, a)
                    if a >= 1:
                        pool.wait_ge(x2_ready, 4 * g + a)
                        pool.sem_inc(passed, 1)
                        pool.tensor_copy(x2r[:, 4 * g + a - 1, 0:DM], x2[:, a - 1]).then_inc(x2_kept, 1)

            def share_out(g, a):
                pool.wait_ge(inv_ready, 4 * g + a + 1)
                pv = sc[:, a].rearrange("p (h j) -> p h j", j=SC)
                pool.tensor_tensor(pv, pv, rc[:, a].unsqueeze(2).to_broadcast([P, H, SC]),
                                   ALU.mult).then_inc(p_ready, 1)

            def root(i, a):
                pool.wait_ge(var_ready, i + 1)
                if not (isinstance(i, int) and i == 0):
                    pool.wait_ge(rstd_ready, i)
                pool.sem_inc(passed, 1)
                pool.tensor_scalar(veps[:, :], mv[:, a % 2, 1:2], EPS, None, ALU.add).then_inc(veps_ready, 1)
                pool.wait_ge(veps_ready, i + 1)
                pool.tensor_tensor(rstd[:, a % 2:a % 2 + 1], veps[:, :], mhalf[:, :], ALU.pow).then_inc(rstd_ready, 1)

            def bias_x1(g, par):
                for a in range(GT):
                    pool.wait_ge(x1_ready, 4 * g + a + 1)
                    pool.tensor_tensor(x1b[:, par, a], x1[:, par, a], bo[:, :], ALU.add).then_inc(x1b_ready, 1)

            batch = [0]
            group(0, 0, True, False)
            group(1, 1, False, False)
            with pool.Fori(1, NG // 2 - 1) as m:
                batch[0] = m
                group(2 * m, 0, False, False)
                group(2 * m + 1, 1, False, False)
            batch[0] = B - 1
            group(NG - 2, 0, False, False)
            group(NG - 1, 1, False, True)

        @block.tensor
        def _(pe):
            pe.wait_ge(w_in, 16 * 6)
            pe.wait_ge(consts, 8)
            for kt in range(KT):
                for i in range(KT):
                    mm = pe.matmul(M[kt][:, 0:B * SC], wk[:, i, kt * P:(kt + 1) * P], ctxT[:, i, :],
                                   start=(i == 0), stop=(i == KT - 1))
                mm.then_inc(kv_psum, 1)
            for b in range(B):
                for i in range(KT):
                    mm = pe.matmul(SP[b][0:SC, 0:DM], ctxT[:, i, b * SC:(b + 1) * SC], wvx[:, i, :],
                                   start=(i == 0), stop=(i == KT - 1))
                mm.then_inc(kv_psum, 1)
            pe.wait_ge(kv_all, 4 * KT + B)

            def take(bank_uses):
                bank, before = bank_uses
                if not (isinstance(before, int) and before == 0):
                    pe.wait_ge(m_free[bank], before)
                return M[bank], m_ready[bank]

            def project(g, par, a, bank_uses):
                if a == 0:
                    pe.wait_ge(in_ready, 32 * g + 32)
                m, ready = take(bank_uses)
                for i in range(PAIRS):
                    mm = pe.matmul(m[:, 0:DM], ot[:, i, a * P:(a + 1) * P], wo[:, i, :],
                                   start=(i == 0), stop=(i == PAIRS - 1))
                mm.then_inc(ready, 1)

            def x_scores(g, a):
                if a == 0:
                    pe.wait_ge(k_now, batch[0] + 1)
                    before_g = None if isinstance(g, int) and g == 0 else g - 1
                    for bank, before in (use(before_g, "q0"), use(before_g, "q1")):
                        pe.wait_ge(m_free[bank], before + 1)
                for c in range(4):
                    if not (isinstance(g, int) and g == 0 and a == 0):
                        pe.wait_ge(sc_free, 16 * g + 4 * a + c - 3)
                    pe.matmul(SP[c][:, 0:HC * SC], qT[:, c // 2, a * P:(a + 1) * P],
                              kbd[:, c // 2, (c % 2) * HC * SC:(c % 2 + 1) * HC * SC],
                              start=True, stop=True).then_inc(sc_ready, 1)

            def x_transposes(g, a):
                pe.wait_ge(p_ready, 4 * g + a + 1)
                for q in range(4):
                    bank, before = p_use(g, a, q)
                    if not (isinstance(before, int) and before == 0):
                        pe.wait_ge(t_free[bank], before)
                    for i in range(4):
                        h = 4 * q + i
                        mm = pe.transpose(T[bank][0:SC, i * P:(i + 1) * P], sc[:, a, h * SC:(h + 1) * SC], ident[:, :])
                    mm.then_inc(t_ready[bank], 1)

            def turn_x1(g, par, a, bank_uses):
                pe.wait_ge(x1_ready, 4 * g + a + 1)
                m, ready = take(bank_uses)
                for i in range(KT):
                    mm = pe.transpose(m[:, i * P:(i + 1) * P], x1[:, par, a, i * P:(i + 1) * P], ident[:, :])
                mm.then_inc(ready, 1)

            def turn_x2(g, a):
                pe.wait_ge(x2_ready, 4 * g + a - 3)
                bank, before = t_use(g, f"t{a}")
                pe.wait_ge(t_free[bank], before)
                for i in range(KT):
                    mm = pe.transpose(T[bank][:, i * P:(i + 1) * P], x2[:, a, i * P:(i + 1) * P], ident[:, :])
                mm.then_inc(t_ready[bank], 1)

            def gate(g):
                for name in ("t2", "t3"):
                    bank, before = t_use(g, name)
                    pe.wait_ge(t_free[bank], before + 1)
                for a in range(GT):
                    for i in range(KT):
                        mm = pe.matmul(T[0][:, a * E:(a + 1) * E], x2T[:, a, i, :], wg[:, i, :],
                                       start=(i == 0), stop=(i == KT - 1))
                mm.then_inc(t_ready[0], 1)

            def project_q(g, kt):
                m, ready = take(use(g, f"q{kt}"))
                if kt == 0:
                    bank, before = use(g, "x3")
                    pe.wait_ge(m_free[bank], before + 1)
                for i in range(KT):
                    mm = pe.matmul(m[:, :], wq[:, i, kt * P:(kt + 1) * P], x1T[:, i, :],
                                   start=(i == 0), stop=(i == KT - 1))
                mm.then_inc(ready, 1)

            def attend(g, hg):
                m, ready = take(use(g, f"o{hg}"))
                for i in range(4):
                    mm = pe.matmul(m[32 * i:32 * i + 32, :], vx[:, 4 * hg + i, :], pT[:, 4 * hg + i, :],
                                   start=True, stop=True)
                mm.then_inc(ready, 1)

            def project_out(g, a):
                own, before = use(g, f"y{a}")
                m, ready = take((own, before))
                if a == 0:
                    for bank, before in (use(g, "o2"), use(g, "o3")):
                        if bank != own:
                            pe.wait_ge(m_free[bank], before + 1)
                for i in range(4):
                    mm = pe.matmul(m[:, 0:DM], oT[:, i, a * P:(a + 1) * P], wox[:, i, :],
                                   start=(i == 0), stop=(i == 3))
                mm.then_inc(ready, 1)

            for a in range(GT):
                project(0, 0, a, use(None, f"p{a}"))
            for a in range(GT):
                turn_x1(0, 0, a, use(None, f"x{a}"))
            for kt in range(KT):
                project_q(None, kt)

            def group(g, par, first, last):
                def next_project(a):
                    if not last:
                        project(g + 1, 1 - par, a, use(g, f"p{a}"))

                x_scores(g, 0)
                next_project(0)
                x_scores(g, 1)
                for a in range(2):
                    if not first:
                        turn_x2(g, 2 * a)
                        turn_x2(g, 2 * a + 1)
                    next_project(1 + a)
                    x_scores(g, 2 + a)
                if not first:
                    gate(g)
                x_transposes(g, 0)
                next_project(3)
                x_transposes(g, 1)
                for a in range(2):
                    x_transposes(g, 2 + a)
                    if not last:
                        turn_x1(g + 1, 1 - par, 2 * a, use(g, f"x{2 * a}"))
                        turn_x1(g + 1, 1 - par, 2 * a + 1, use(g, f"x{2 * a + 1}"))
                for q in (2, 3):
                    bank, before = p_use(g, GT - 1, q)
                    pe.wait_ge(t_free[bank], before + 1)
                pe.wait_ge(v_now, batch[0] + 1)
                for hg in range(4):
                    attend(g, hg)
                for kt in range(2):
                    if not last:
                        project_q(g, kt)
                    if kt == 0:
                        project_out(g, 0)
                        project_out(g, 1)
                project_out(g, 2)
                project_out(g, 3)

            batch = [0]
            group(0, 0, True, False)
            group(1, 1, False, False)
            with pe.Fori(1, NG // 2 - 1) as m_:
                batch[0] = m_
                group(2 * m_, 0, False, False)
                group(2 * m_ + 1, 1, False, False)
            batch[0] = B - 1
            group(NG - 2, 0, False, False)
            group(NG - 1, 1, False, True)
            for a in range(GT):
                turn_x2(NG, a)
            gate(NG)

        @block.scalar
        def _(act):
            act.dma_start(bq[:, :], d["bq"]).then_inc(small_in, 16)
            act.dma_start(bk[:, :], d["bk"]).then_inc(small_in, 16)
            act.dma_start(bv[:, :], d["bv"].partition_broadcast(SC)).then_inc(small_in, 16)
            act.dma_start(bo[:, :], d["bo"].partition_broadcast(P)).then_inc(small_in, 16)
            act.dma_start(bg[:, :], d["bg"].partition_broadcast(P)).then_inc(small_in, 16)
            act.wait_ge(consts, 5)
            for i in range(4):
                act.dma_start(wox[32 * i:32 * i + XD], d["wox"][i]).then_inc(small_in, 16)
            act.wait_ge(small_in, 16 * 9)
            for kt in range(KT):
                act.wait_ge(kv_psum, kt + 1)
                act.activation(kT[:, kt, :], M[kt][:, 0:B * SC], ACT.Identity,
                               bias=bk[:, kt:kt + 1]).then_inc(kv_sb, 1)

            def read(g, name, out, rearranged=None, bias=None):
                bank, before = use(g, name)
                act.wait_ge(m_ready[bank], before + 1)
                m = M[bank][:, 0:512] if rearranged is None else rearranged(M[bank])
                if bias is None:
                    act.activation(out, m, ACT.Copy).then_inc(m_free[bank], 1)
                else:
                    act.activation(out, m, ACT.Identity, bias=bias).then_inc(m_free[bank], 1)

            def two(m):
                return m[:, 0:DM].rearrange("p (k i) -> p k i", k=KT)

            def turned_x1(g, a):
                read(g, f"x{a}", x1T[:, :, a * P:(a + 1) * P], two)

            def turned_x2(g, a):
                bank, before = t_use(g, f"t{a}")
                act.wait_ge(t_ready[bank], before + 1)
                act.activation(x2T[:, a], two(T[bank]), ACT.Copy).then_inc(t_free[bank], 1)

            def queries(g, kt):
                read(g, f"q{kt}", qT[:, kt, :], bias=bq[:, kt:kt + 1])

            def turned_p(g, a, q):
                bank, before = p_use(g, a, q)
                act.wait_ge(t_ready[bank], before + 1)
                act.activation(pT[:, 4 * q:4 * q + 4, a * P:(a + 1) * P],
                               T[bank][0:SC, :].rearrange("p (h i) -> p h i", i=P), ACT.Copy).then_inc(t_free[bank], 1)

            def expo(g, a):
                act.wait_ge(sc_free, 16 * g + 4 * a + 4)
                act.activation(sc[:, a], sc[:, a], ACT.Exp, scale=XD ** -0.5).then_inc(exp_ready, 1)

            for a in range(GT):
                turned_x1(None, a)
            for kt in range(KT):
                queries(None, kt)

            def group(g, par, first, last):
                for a in range(2):
                    expo(g, a)
                    if not first:
                        turned_x2(g, 2 * a)
                        turned_x2(g, 2 * a + 1)
                expo(g, 2)
                for q in range(4):
                    turned_p(g, 0, q)
                expo(g, 3)
                for q in range(4):
                    turned_p(g, 1, q)
                for a in range(2):
                    for q in (0, 2):
                        turned_p(g, 2 + a, q)
                    if not last:
                        turned_x1(g, 2 * a)
                        turned_x1(g, 2 * a + 1)
                for hg in (0, 2):
                    read(g, f"o{hg}", oT[:, hg, :])
                if not last:
                    for kt in range(KT):
                        queries(g, kt)

            groups(act, group)
            for a in range(GT):
                turned_x2(NG, a)

        @block.vector
        def _(dve):
            step = Steps()
            dve.wait_ge(small_in, 16 * 9)
            dve.wait_ge(consts, 8)
            for kt in range(KT):
                dve.wait_ge(kv_sb, kt + 1)
                for b in range(B):
                    dve.tensor_tensor(kbd_all[:, b, kt].rearrange("p (h j) -> p h j", j=SC),
                                      kT[:, kt, b * SC:(b + 1) * SC].unsqueeze(1).to_broadcast([P, 8, SC]),
                                      hmask[:, :].unsqueeze(2).to_broadcast([P, 8, SC]), ALU.mult).then_inc(kv_all, 1)
            for b in range(B):
                dve.wait_ge(kv_psum, KT + b + 1)
                dve.tensor_tensor(vx_all[:, b, :, 0:XD], SP[b][0:SC, 0:DM].rearrange("p (h e) -> p h e", e=XD),
                                  bv[:, :].rearrange("p (h e) -> p h e", e=XD), ALU.add).then_inc(kv_all, 1)

            def less_max(g, a):
                for c in range(4):
                    dve.wait_ge(sc_ready, 16 * g + 4 * a + c + 1)
                    dve.tensor_reduce(mx[:, a, HC * c:HC * c + HC],
                                      SP[c][:, 0:HC * SC].rearrange("p (h j) -> p h j", j=SC),
                                      AX.X, ALU.max).then_inc(dstep, step.one())
                dve.wait_ge(dstep, step.now())
                for c in range(4):
                    dve.tensor_tensor(sc[:, a, HC * SC * c:HC * SC * (c + 1)].rearrange("p (h j) -> p h j", j=SC),
                                      SP[c][:, 0:HC * SC].rearrange("p (h j) -> p h j", j=SC),
                                      mx[:, a, HC * c:HC * c + HC].unsqueeze(2).to_broadcast([P, HC, SC]),
                                      ALU.subtract).then_inc(sc_free, 1)

            def inverse(g, a):
                dve.wait_ge(exp_ready, 4 * g + a + 1)
                dve.tensor_reduce(sm[:, a], sc[:, a].rearrange("p (h j) -> p h j", j=SC), AX.X,
                                  ALU.add).then_inc(dstep, step.one())
                dve.wait_ge(dstep, step.now())
                dve.reciprocal(rc[:, a], sm[:, a]).then_inc(inv_ready, 1)

            def statistics(i, bank_uses, residual, a):
                bank, before = bank_uses
                dve.wait_ge(m_ready[bank], before + 1)
                dve.tensor_tensor(r[:, a % 2], M[bank][:, 0:DM], residual, ALU.add).then_inc(m_free[bank], 1)
                dve.wait_ge(m_free[bank], before + 1)
                if not (isinstance(i, int) and i == 0):
                    dve.wait_ge(var_ready, i)
                dve.bn_stats(st[:, :], r[:, a % 2]).then_inc(dstep, step.one())
                dve.wait_ge(dstep, step.now())
                dve.sem_inc(passed, 1)
                dve.bn_aggr(mv[:, a % 2], st[:, :]).then_inc(var_ready, 1)

            def norm(i, a, out, ready):
                dve.wait_ge(rstd_ready, i + 1)
                dve.tensor_scalar(out, r[:, a % 2], mv[:, a % 2, 0:1], rstd[:, a % 2:a % 2 + 1],
                                  ALU.subtract, ALU.mult).then_inc(ready, 1)

            def statistics1(i, g, a, bank_uses):
                if a == 0:
                    dve.wait_ge(in_ready, 32 * g + 32)
                if a >= 2:
                    dve.wait_ge(x1_ready, 4 * g + a - 1)
                elif not (isinstance(g, int) and g <= 1):
                    dve.wait_ge(x2_ready, 4 * g - 4)
                elif g == 1:
                    dve.wait_ge(x1_ready, 4)
                statistics(i, bank_uses, xin[:, a], a)

            for a in range(GT):
                statistics1(a, 0, a, use(None, f"p{a}"))
                norm(a, a, x1[:, 0, a], x1_ready)
            before_groups = step.now()
            a_group = 4 * 4 + 4 + 4 + 4

            def logit(g):
                bank, before = t_use(g, "logits")
                dve.wait_ge(t_ready[bank], before + 1)
                dve.tensor_tensor(logits[:, bass.ds(4 * g - 4, GT), :], T[bank][:, 0:GT * E].rearrange("p (a e) -> p a e", e=E),
                                  bg[:, :].unsqueeze(1).to_broadcast([P, GT, E]), ALU.add).then_inc(t_free[bank], 1)

            def turned_p(g, a, q):
                bank, before = p_use(g, a, q)
                dve.wait_ge(t_ready[bank], before + 1)
                dve.tensor_copy(pT[:, 4 * q:4 * q + 4, a * P:(a + 1) * P],
                                T[bank][0:SC, :].rearrange("p (h i) -> p h i", i=P)).then_inc(t_free[bank], 1)

            def group(g, par, first, last):
                step.start(before_groups + a_group * g)

                def next_statistics(a):
                    if not last:
                        statistics1(8 * g + 4 + a, g + 1, a, use(g, f"p{a}"))

                def next_norm(a):
                    if not last:
                        norm(8 * g + 4 + a, a, x1[:, 1 - par, a], x1_ready)

                less_max(g, 0)
                for a in range(3):
                    next_statistics(a)
                    less_max(g, 1 + a)
                    next_norm(a)
                    inverse(g, a)
                if not first:
                    logit(g)
                inverse(g, 3)
                next_statistics(3)
                turned_p(g, 2, 1)
                turned_p(g, 2, 3)
                next_norm(3)
                turned_p(g, 3, 1)
                turned_p(g, 3, 3)
                for hg in (1, 3):
                    bank, before = use(g, f"o{hg}")
                    dve.wait_ge(m_ready[bank], before + 1)
                    dve.tensor_copy(oT[:, hg, :], M[bank][:, :]).then_inc(m_free[bank], 1)
                for a in range(GT + 1):
                    if a < GT:
                        dve.wait_ge(x1b_ready, 4 * g + a + 1)
                        if a >= 2:
                            dve.wait_ge(x2_ready, 4 * g + a - 1)
                        elif last:
                            dve.wait_ge(x2_ready, 4 * g)
                        else:
                            dve.wait_ge(x1_ready, 4 * g + 8)
                        statistics(8 * g + (4 if last else 8) + a, use(g, f"y{a}"), x1b[:, par, a], a)
                    if a >= 1:
                        if not first:
                            dve.wait_ge(x2_kept, 4 * g + a - 4)
                        norm(8 * g + (4 if last else 8) + a - 1, a - 1, x2[:, a - 1], x2_ready)

            groups(dve, group)
            logit(NG)


def route(nc, sem, x2r, logits, pos, tile_e, XS):
    with ExitStack() as ctx:
        def sb(name, shape, dt=F32):
            return ctx.enter_context(nc.sbuf_tensor(name, shape, dt))

        tri = sb("tri", [P, P])
        ones = sb("ones", [P, P])
        eidx = sb("eidx", [P, E])
        t128 = sb("t128", [P, NT])
        tnum = sb("tnum", [1, XT])
        best = sb("best", [P, NT])
        p = sb("p", [P, NT, E])
        total = sb("total", [P, NT])
        inv = sb("inv3", [P, NT])
        first = sb("first", [P, NT])
        oh = sb("oh", [P, NT, E])
        cum = [sb("cum0", [P, NT, E]), sb("cum1", [P, NT, E])]
        count = sb("count", [P, E])
        more = sb("more", [P, E, NT])
        ntile = sb("ntile", [P, E])
        start = sb("start", [P, E])
        posf = sb("posf", [P, NT])
        tgt = sb("tgt", [1, XT, E])
        tef = sb("tef", [1, XT])
        U = ctx.enter_context(nc.psum_tensor("U", [P, 512], F32))
        V = ctx.enter_context(nc.psum_tensor("V", [P, 512], F32))
        consts = sem("r_consts")
        less_ready = sem("r_less")
        exp_ready = sem("r_exp")
        oh_ready = sem("r_oh")
        sums_ready = sem("r_sums")
        pos_ready = sem("r_pos")
        dstep = sem("r_dstep")
        sent = sem("r_sent")
        block = ctx.enter_context(nc.Block())

        @block.gpsimd
        def _(pool):
            pool.memset(tri[:, :], 1.0).then_inc(consts, 1)
            pool.memset(ones[:, :], 1.0).then_inc(consts, 1)
            pool.iota(eidx[:, :], [[1, E]], base=-E, channel_multiplier=0,
                      allow_small_or_imprecise_dtypes=True).then_inc(consts, 1)
            pool.iota(t128[:, :], [[P, NT]], base=0, channel_multiplier=0,
                      allow_small_or_imprecise_dtypes=True).then_inc(consts, 1)
            pool.iota(tnum[:, :], [[1, XT]], base=0, channel_multiplier=0,
                      allow_small_or_imprecise_dtypes=True).then_inc(consts, 1)
            pool.wait_ge(consts, 5)
            pool.affine_select(out=tri[:, :], in_=tri[:, :], compare_op=ALU.is_gt, fill=0.0,
                               base=0, pattern=[[1, P]], channel_multiplier=-1).then_inc(consts, 1)
            pool.wait_ge(pos_ready, 1)
            for t in range(NT):
                pool.indirect_dma_start(XS, bass.IndirectOffsetOnAxis(ap=pos[:, t:t + 1], axis=0),
                                        x2r[:, t, :], None).then_inc(sent, 16)
            pool.wait_ge(sent, 16 * NT)

        @block.scalar
        def _(act):
            act.wait_ge(less_ready, 1)
            act.activation(p[:, :, :], p[:, :, :], ACT.Exp).then_inc(exp_ready, 1)

        @block.tensor
        def _(pe):
            pe.wait_ge(consts, 6)
            pe.wait_ge(oh_ready, 1)
            flat = oh[:, :, :].rearrange("p t e -> p (t e)")
            pe.matmul(U[:, 0:NT * E], tri[:, :], flat, start=True, stop=True)
            pe.matmul(V[:, 0:NT * E], ones[:, :], flat, start=True, stop=True).then_inc(sums_ready, 1)

        @block.vector
        def _(dve):
            step = Steps()

            def done(ins):
                return ins.then_inc(dstep, step.one())

            def wide(a):
                return a.unsqueeze(2).to_broadcast([P, NT, E])

            def every(a, n=NT):
                return a.unsqueeze(1).to_broadcast([P, n, E])

            dve.wait_ge(consts, 6)
            done(dve.tensor_reduce(best[:, :], logits[:, :, :], AX.X, ALU.max))
            dve.wait_ge(dstep, step.now())
            dve.tensor_tensor(p[:, :, :], logits[:, :, :], wide(best[:, :]), ALU.subtract).then_inc(less_ready, 1)
            dve.wait_ge(exp_ready, 1)
            done(dve.tensor_reduce(total[:, :], p[:, :, :], AX.X, ALU.add))
            done(dve.tensor_reduce(best[:, :], p[:, :, :], AX.X, ALU.max))
            dve.wait_ge(dstep, step.now())
            done(dve.reciprocal(inv[:, :], total[:, :]))
            done(dve.tensor_tensor(oh[:, :, :], p[:, :, :], wide(best[:, :]), ALU.is_equal))
            dve.wait_ge(dstep, step.now())
            done(dve.tensor_tensor(x2r[:, :, DM], best[:, :], inv[:, :], ALU.mult))
            done(dve.tensor_tensor(p[:, :, :], oh[:, :, :], every(eidx[:, :]), ALU.mult))
            dve.wait_ge(dstep, step.now())
            done(dve.tensor_reduce(first[:, :], p[:, :, :], AX.X, ALU.min))
            dve.wait_ge(dstep, step.now())
            dve.tensor_tensor(oh[:, :, :], every(eidx[:, :]), wide(first[:, :]), ALU.is_equal).then_inc(oh_ready, 1)

            dve.wait_ge(sums_ready, 1)
            done(dve.memset(cum[0][:, 0, :], 0.0))
            done(dve.tensor_copy(cum[0][:, 1:NT, :], V[:, 0:(NT - 1) * E].rearrange("p (t e) -> p t e", e=E)))
            now, shift = 0, 1
            while shift < NT:
                a, b = cum[now], cum[1 - now]
                dve.wait_ge(dstep, step.now())
                done(dve.tensor_copy(b[:, 0:shift, :], a[:, 0:shift, :]))
                done(dve.tensor_tensor(b[:, shift:NT, :], a[:, shift:NT, :], a[:, 0:NT - shift, :], ALU.add))
                now, shift = 1 - now, 2 * shift
            c = cum[now]
            dve.wait_ge(dstep, step.now())
            done(dve.tensor_tensor(count[:, :], V[:, (NT - 1) * E:NT * E], c[:, NT - 1, :], ALU.add))
            done(dve.tensor_tensor(cum[1 - now][:, :, :], U[:, 0:NT * E].rearrange("p (t e) -> p t e", e=E),
                                   c[:, :, :], ALU.add))
            rank = cum[1 - now]
            dve.wait_ge(dstep, step.now())
            done(dve.tensor_tensor(more[:, :, :], count[:, :].unsqueeze(2).to_broadcast([P, E, NT]),
                                   t128[:, :].unsqueeze(1).to_broadcast([P, E, NT]), ALU.is_gt))
            dve.wait_ge(dstep, step.now())
            done(dve.tensor_reduce(ntile[:, :], more[:, :, :], AX.X, ALU.add))
            done(dve.memset(start[:, 0:1], 0.0))
            for e in range(1, E):
                dve.wait_ge(dstep, step.now())
                done(dve.tensor_tensor(start[:, e:e + 1], start[:, e - 1:e], ntile[:, e - 1:e], ALU.add))
            dve.wait_ge(dstep, step.now())
            done(dve.tensor_tensor(tgt[:, :, 0:E - 1], tnum[:, :].unsqueeze(2).to_broadcast([1, XT, E - 1]),
                                   start[0:1, 1:E].unsqueeze(1).to_broadcast([1, XT, E - 1]), ALU.is_ge))
            dve.wait_ge(dstep, step.now())
            done(dve.tensor_scalar(start[:, :], start[:, :], float(P), None, ALU.mult))
            dve.wait_ge(dstep, step.now())
            done(dve.tensor_reduce(tef[:, :], tgt[:, :, 0:E - 1], AX.X, ALU.add))
            done(dve.tensor_tensor(rank[:, :, :], rank[:, :, :], every(start[:, :]), ALU.add))
            dve.wait_ge(dstep, step.now())
            done(dve.tensor_copy(tile_e[:, :], tef[:, :]))
            done(dve.tensor_tensor(rank[:, :, :], rank[:, :, :], oh[:, :, :], ALU.mult))
            dve.wait_ge(dstep, step.now())
            done(dve.tensor_reduce(posf[:, :], rank[:, :, :], AX.X, ALU.add))
            dve.wait_ge(dstep, step.now())
            dve.tensor_copy(pos[:, :], posf[:, :]).then_inc(pos_ready, 1)


def experts(nc, sem, d, XS, FS, tile_e):
    with ExitStack() as ctx:
        def sb(name, shape, dt=F32):
            return ctx.enter_context(nc.sbuf_tensor(name, shape, dt))

        w1 = sb("w1", [P, E, KT, FF])
        w2 = sb("w2", [P, E, FF // P, DM])
        b1 = sb("b1", [P, E, FF])
        b2 = sb("b2", [P, E, DM])
        ident = sb("ident4", [P, P])
        xs = sb("xs", [P, 4, ROW])
        xsT = sb("xsT", [P, 2, KT, P])
        hid = sb("hid", [P, 2, FF])
        hT = sb("hT", [P, FF // P, P])
        y = sb("y", [P, DM])
        r = sb("r4", [P, DM])
        st = sb("st4", [P, 6])
        mv = sb("mv4", [P, 2])
        rstd = sb("rstd4", [P, 1])
        veps = sb("veps4", [P, 1])
        mhalf = sb("mhalf4", [P, 1])
        fo = sb("fo", [P, 2, DM])
        HP = [ctx.enter_context(nc.psum_tensor(f"HP{i}", [P, FF], F32)) for i in range(2)]
        HT = [ctx.enter_context(nc.psum_tensor(f"HT{i}", [P, 512], F32)) for i in range(2)]
        XP = ctx.enter_context(nc.psum_tensor("XP", [P, 512], F32))
        YP = ctx.enter_context(nc.psum_tensor("YP", [P, 512], F32))
        consts = sem("e_consts")
        b_in = sem("e_b_in")
        w_in = sem("e_w_in")
        x_in = [sem(f"e_x_in{i}") for i in range(4)]
        xp_ready, xt_ready = sem("e_xp"), sem("e_xt")
        hp_ready, pre_ready = sem("e_hp"), sem("e_pre")
        act_ready = sem("e_act")
        ht_ready = [sem("e_ht0"), sem("e_ht1")]
        hs_ready = [sem("e_hs0"), sem("e_hs1")]
        yp_ready, y_ready = sem("e_yp"), sem("e_y")
        veps_ready = sem("e_veps")
        var_ready, rstd_ready = sem("e_var"), sem("e_rstd")
        f_ready = sem("e_f")
        f_out = [sem("e_fo0"), sem("e_fo1")]
        dstep = sem("e_dstep")
        passed = sem("e_passed")
        block = ctx.enter_context(nc.Block())
        XSv = XS.rearrange("(t p) n -> t p n", p=P)
        FSv = FS.rearrange("(t p) n -> t p n", p=P)
        HEAD, TAIL = 3, 4

        def tiles(eng, body):
            for t in range(HEAD):
                body(0, t)
            with eng.Fori(0, (XT - HEAD - TAIL) // 4) as m:
                for i in range(4):
                    body(m, HEAD + i)
            for t in range(XT - TAIL, XT):
                body(0, t)

        def is_last(m, k):
            return isinstance(m, int) and k == XT - 1

        def loads_ahead(m, k):
            return not (isinstance(m, int) and k >= XT - 2)

        @block.sync
        def _(sp):
            for e in range(E):
                sp.dma_start(w1[:, e], d["W1"][e].rearrange("(kt p) n -> p kt n", p=P)).then_inc(w_in, 16)
                sp.dma_start(w2[:, e], d["W2"][e].rearrange("(kt p) n -> p kt n", p=P)).then_inc(w_in, 16)
                sp.wait_ge(w_in, 32 * e + 32)

        @block.gpsimd
        def _(pool):
            for t in range(3):
                pool.dma_start(xs[:, t], XSv[t]).then_inc(x_in[t], 16)
            pool.memset(mhalf[:, :], -0.5)
            pool.memset(ident[:, :], 0.0).then_inc(consts, 1)
            pool.wait_ge(consts, 1)
            pool.affine_select(out=ident[:, :], in_=ident[:, :], compare_op=ALU.not_equal, fill=1.0,
                               base=0, pattern=[[-1, P]], channel_multiplier=1).then_inc(consts, 1)

            def tile(m, k):
                t, q = 4 * m + k, k % 4
                if not (isinstance(m, int) and k >= XT - 3):
                    pool.dma_start(xs[:, (q + 3) % 4], XSv[t + 3]).then_inc(x_in[(q + 3) % 4], 16)
                pool.wait_ge(var_ready, t + 1)
                pool.sem_inc(passed, 1)
                pool.tensor_scalar(veps[:, :], mv[:, 1:2], EPS, None, ALU.add).then_inc(veps_ready, 1)
                pool.wait_ge(veps_ready, t + 1)
                pool.tensor_tensor(rstd[:, :], veps[:, :], mhalf[:, :], ALU.pow).then_inc(rstd_ready, 1)
                pool.wait_ge(f_ready, t + 1)
                pool.dma_start(FSv[t], fo[:, q % 2]).then_inc(f_out[q % 2], 16)

            tiles(pool, tile)
            pool.wait_ge(f_out[0], 16 * 20)
            pool.wait_ge(f_out[1], 16 * 19)

        @block.tensor
        def _(pe):
            pe.wait_ge(consts, 2)

            def turn_x(t, q, x_count, fresh=False):
                pe.wait_ge(x_in[q], 16 * x_count)
                if not fresh:
                    pe.wait_ge(xt_ready, t)
                for i in range(KT):
                    mm = pe.transpose(XP[:, i * P:(i + 1) * P], xs[:, q, i * P:(i + 1) * P], ident[:, :])
                mm.then_inc(xp_ready, 1)

            def up(t, q, e, fresh=False):
                pe.wait_ge(w_in, 32 * e + 32)
                pe.wait_ge(xt_ready, t + 1)
                if not fresh:
                    pe.wait_ge(pre_ready, t - 1)
                for c in range(2):
                    for i in range(KT):
                        mm = pe.matmul(HP[q % 2][:, c * 512:(c + 1) * 512], xsT[:, q % 2, i, :],
                                       w1[:, e, i, c * 512:(c + 1) * 512], start=(i == 0), stop=(i == KT - 1))
                mm.then_inc(hp_ready, 1)

            def expert(t):
                return pe.value_load(tile_e[0:1, bass.ds(t, 1)], min_val=0, max_val=E - 1)

            turn_x(0, 0, 1, fresh=True)
            turn_x(1, 1, 1)
            up(0, 0, expert(0), fresh=True)

            def tile(m, k):
                t, q, first = 4 * m + k, k % 4, isinstance(m, int) and k == 0
                if not is_last(m, k):
                    up(t + 1, (q + 1) % 4, expert(t + 1), fresh=first)
                e = expert(t)
                pe.wait_ge(act_ready, t + 1)
                for bank in range(2):
                    if not first:
                        pe.wait_ge(hs_ready[bank], t)
                    for i in range(4):
                        j = 4 * bank + i
                        mm = pe.transpose(HT[bank][:, i * P:(i + 1) * P], hid[:, q % 2, j * P:(j + 1) * P], ident[:, :])
                    mm.then_inc(ht_ready[bank], 1)
                if loads_ahead(m, k):
                    turn_x(t + 2, (q + 2) % 4, m + (k + 2) // 4 + 1)
                if not first:
                    pe.wait_ge(y_ready, t)
                for j in range(FF // P):
                    if j % 4 == 0:
                        pe.wait_ge(hs_ready[j // 4], t + 1)
                    mm = pe.matmul(YP[:, 0:DM], hT[:, j, :], w2[:, e, j, :], start=(j == 0), stop=(j == FF // P - 1))
                mm.then_inc(yp_ready, 1)

            tiles(pe, tile)

        @block.scalar
        def _(act):
            act.dma_start(b1[:, :, :], d["b1"].partition_broadcast(P)).then_inc(b_in, 16)
            act.dma_start(b2[:, :, :], d["b2"].partition_broadcast(P)).then_inc(b_in, 16)

            def tile(m, k):
                t, q = 4 * m + k, k % 4
                act.wait_ge(pre_ready, t + 1)
                act.activation(hid[:, q % 2], hid[:, q % 2], ACT.Silu).then_inc(act_ready, 1)
                act.wait_ge(ht_ready[0], t + 1)
                act.activation(hT[:, 0:4, :], HT[0][:, :].rearrange("p (j i) -> p j i", i=P),
                               ACT.Copy).then_inc(hs_ready[0], 1)

            tiles(act, tile)

        @block.vector
        def _(dve):
            step = Steps()
            dve.wait_ge(b_in, 32)

            def expert(t):
                return dve.value_load(tile_e[0:1, bass.ds(t, 1)], min_val=0, max_val=E - 1)

            def turned(t, q):
                dve.wait_ge(xp_ready, t + 1)
                dve.tensor_copy(xsT[:, q % 2], XP[:, 0:DM].rearrange("p (k i) -> p k i", i=P)).then_inc(xt_ready, 1)

            def biased(t, q):
                e = expert(t)
                dve.wait_ge(hp_ready, t + 1)
                dve.tensor_tensor(hid[:, q % 2], HP[q % 2][:, :], b1[:, e, :], ALU.add).then_inc(pre_ready, 1)

            turned(0, 0)
            turned(1, 1)
            biased(0, 0)

            def tile(m, k):
                t, q = 4 * m + k, k % 4
                step.start(2 * t)
                if not is_last(m, k):
                    biased(t + 1, (q + 1) % 4)
                dve.wait_ge(ht_ready[1], t + 1)
                dve.tensor_copy(hT[:, 4:8, :], HT[1][:, :].rearrange("p (j i) -> p j i", i=P)).then_inc(hs_ready[1], 1)
                if loads_ahead(m, k):
                    turned(t + 2, (q + 2) % 4)
                e = expert(t)
                dve.wait_ge(yp_ready, t + 1)
                dve.tensor_tensor(y[:, :], YP[:, 0:DM], b2[:, e, :], ALU.add).then_inc(y_ready, 1)
                dve.wait_ge(y_ready, t + 1)
                dve.scalar_tensor_tensor(out=r[:, :], in0=y[:, :], scalar=xs[:, q, DM:DM + 1], in1=xs[:, q, 0:DM],
                                         op0=ALU.mult, op1=ALU.add).then_inc(dstep, step.one())
                dve.wait_ge(dstep, step.now())
                dve.bn_stats(st[:, :], r[:, :]).then_inc(dstep, step.one())
                dve.wait_ge(dstep, step.now())
                dve.sem_inc(passed, 1)
                dve.bn_aggr(mv[:, :], st[:, :]).then_inc(var_ready, 1)
                dve.wait_ge(rstd_ready, t + 1)
                if not (isinstance(m, int) and k < 2):
                    dve.wait_ge(f_out[k % 2], 32 * m + 16 * (k // 2))
                dve.tensor_scalar(fo[:, q % 2], r[:, :], mv[:, 0:1], rstd[:, :], ALU.subtract,
                                  ALU.mult).then_inc(f_ready, 1)

            tiles(dve, tile)


def unsort(nc, sem, FS, pos, out):
    with ExitStack() as ctx:
        rows = ctx.enter_context(nc.sbuf_tensor("rows", [P, NT, DM], F32))
        got = [sem(f"u_got{i}") for i in range(NT // 4)]
        stored = sem("u_stored")
        block = ctx.enter_context(nc.Block())
        outv = out.rearrange("(t p) n -> p t n", p=P)

        @block.gpsimd
        def _(pool):
            for t in range(NT):
                pool.indirect_dma_start(rows[:, t, :], None, FS,
                                        bass.IndirectOffsetOnAxis(ap=pos[:, t:t + 1], axis=0)).then_inc(got[t // 4], 16)

        @block.sync
        def _(sp):
            for i in range(NT // 4):
                sp.wait_ge(got[i], 64)
                sp.dma_start(outv[:, 4 * i:4 * i + 4, :], rows[:, 4 * i:4 * i + 4, :]).then_inc(stored, 16)
            sp.wait_ge(stored, 16 * (NT // 4))


def decoder_layer(nc, a, out):
    OT = nc.dram_tensor("attention_t", (NI, P, L), F32).ap()
    XS = nc.dram_tensor("sorted_rows", (XT * P, ROW), F32).ap()
    FS = nc.dram_tensor("sorted_out", (XT * P, DM), F32).ap()

    def by_row_tile(w):
        return w.rearrange("(k p) n -> p k n", p=P)

    d = {
        "x": a["x"].rearrange("b (c a p) n -> p b c a n", c=2, p=P),
        "wo": by_row_tile(a["attn_W_out"]), "ctxT": by_row_tile(a["ctxT"]),
        "wq": by_row_tile(a["xattn_W_qT"]), "wk": by_row_tile(a["xattn_W_kT"]),
        "wv": by_row_tile(a["xattn_W_vT"]),
        "wox": a["xattn_W_outT"].rearrange("(g i e) n -> i e g n", i=4, e=XD),
        "bq": a["xattn_b_q"], "bk": a["xattn_b_k"], "bv": a["xattn_b_v"], "bo": a["xattn_b_out"],
        "wg": by_row_tile(a["ffn_Wg"]), "bg": a["ffn_bg"],
        "W1": a["ffn_W1"], "b1": a["ffn_b1"], "W2": a["ffn_W2"], "b2": a["ffn_b2"],
    }
    with ExitStack() as ctx:
        def sem(name):
            return ctx.enter_context(nc.semaphore(name))

        pos = ctx.enter_context(nc.sbuf_tensor("pos", [P, NT], I32))
        tile_e = ctx.enter_context(nc.sbuf_tensor("tile_e", [1, XT], I32))
        self_attention(nc, sem, by_row_tile(a["xT"]), a["attn_W_qkv"], OT, XS)
        with ExitStack() as rows:
            x2r = rows.enter_context(nc.sbuf_tensor("x2r", [P, NT, ROW], F32))
            logits = rows.enter_context(nc.sbuf_tensor("logits", [P, NT, E], F32))
            token_groups(nc, sem, d, OT, x2r, logits)
            route(nc, sem, x2r, logits, pos, tile_e, XS)
        experts(nc, sem, d, XS, FS, tile_e)
        unsort(nc, sem, FS, pos, out)


def kernel(**inputs):
    import numpy as np
    import concourse.bacc as bacc
    from concourse.bass_utils import run_bass_kernel_spmd

    i = {k: np.asarray(v) for k, v in inputs.items()}
    lay = {
        "x": i["x"], "xT": i["x"].reshape(TOK, DM).T,
        "ctxT": i["ctx_1024"].reshape(B * SC, DM).T,
        "attn_W_qkv": i["L0_attn_W_qkv"], "attn_W_out": i["L0_attn_W_out"],
        "xattn_W_qT": i["L0_xattn_W_q"].T, "xattn_W_kT": i["L0_xattn_W_k"].T,
        "xattn_W_vT": i["L0_xattn_W_v"].T, "xattn_W_outT": i["L0_xattn_W_out"].T,
        "xattn_b_q": i["L0_xattn_b_q"].reshape(KT, P).T, "xattn_b_k": i["L0_xattn_b_k"].reshape(KT, P).T,
        "xattn_b_v": i["L0_xattn_b_v"], "xattn_b_out": i["L0_xattn_b_out"],
        "ffn_Wg": i["L0_ffn_Wg"], "ffn_bg": i["L0_ffn_bg"], "ffn_W1": i["L0_ffn_W1"],
        "ffn_b1": i["L0_ffn_b1"], "ffn_W2": i["L0_ffn_W2"], "ffn_b2": i["L0_ffn_b2"],
    }
    nc = bacc.Bacc("TRN2", target_bir_lowering=False, num_devices=1)
    arrays, aps = {}, {}
    for name, v in lay.items():
        arrays[f"in_{name}"] = np.ascontiguousarray(v)
        aps[name] = nc.dram_tensor(f"in_{name}", v.shape, F32, kind="ExternalInput").ap()
    out = nc.dram_tensor("out", (TOK, DM), F32, kind="ExternalOutput").ap()
    decoder_layer(nc, aps, out)
    r = run_bass_kernel_spmd(nc, [arrays], core_ids=[0])
    return r.results[0]["out"].reshape(B, L, DM)
```

```python
import concourse.bass as bass
from concourse import mybir
from contextlib import ExitStack
import numpy as np

F32 = mybir.dt.float32
F32R = mybir.dt.float32r
BF16 = mybir.dt.bfloat16
I32 = mybir.dt.int32
ALU = mybir.AluOpType
ACT = mybir.ActivationFunctionType
AX = mybir.AxisListType

P = 128
B, L, DM = 4, 1024, 256
TOK = B * L
H, D = 16, 64
PAIRS = H // 2
NI = B * PAIRS
KT = DM // P
LT = L // P
SC = 77
XD = DM // H
E, FF = 8, 1024
NT = TOK // P
NG, GT = TOK // 512, 4
XT = NT + E - 1
ROW = 264
EARLY = 4
EPS = 1e-5
BIG = -1e30


PROJECT = {2: 0, 4: 1, 5: 2, 8: 3, 13: 4, 15: 5}
KEYS1 = {0: [0], 1: [1], 4: [2, 3], 5: [4, 5], 6: [6], 7: [7]}
KEYS0 = {8: [0], 9: [1], 12: [2], 13: [3]}
SPREAD1, SPREAD0 = 1, 11
RECIP1, RECIP0 = 0, 9
NORM1, NORM0 = 7, 13


def lookahead(s):
    return (s + 2) // 16, (s + 2) % 16


def self_attention(nc, sem, d, xT, w_qkv, OT, XS, g_in, in_ready, x2r):
    with ExitStack() as ctx:
        def sb(name, shape, dt=F32):
            return ctx.enter_context(nc.sbuf_tensor(name, shape, dt))

        xf = sb("xf", [P, KT, L])
        xh, xl = (g_in["ot"][:, 4 * i:4 * i + 4, :].rearrange("p a n -> p (a n)")
                  .rearrange("p (k n) -> p k n", k=KT).bitcast(F32R) for i in range(2))
        wraw = sb("wraw", [P, 2, KT, 3, P])
        wh = sb("wh", [P, 2, KT, 2, P], F32R)
        wl = sb("wl", [P, 2, KT, 2, P], F32R)
        qs = sb("qs", [P, 2, 2, L], F32R)
        k1 = sb("k1", [P, 2, 2, L], F32R)
        k2 = sb("k2", [P, 2, 2, L], F32R)
        v = sb("v", [P, 2, LT, P])
        prob = sb("prob", [P, 4, L])
        pt = [sb("pt0", [P, 2, 4, 512]), x2r[:, :, :].rearrange("p t n -> p (t n)")[:, 0:8192].rearrange("p (h j i) -> p h j i", h=2, j=8)]
        nmax = sb("nmax", [P, 2])
        sums = sb("sums", [P, 2, LT, 2])
        rec = sb("rec", [P, 2, LT, 2 * D])
        inv = sb("inv", [P, 8])
        rb = sb("rb", [P, 2, 512])
        ob = sb("ob", [P, 2, 512])
        ident = sb("ident", [P, P])
        identb = sb("identb", [P, P], BF16)
        maskb = sb("maskb", [P, P], BF16)
        S = [ctx.enter_context(nc.psum_tensor(f"S{i}", [P, L], F32)) for i in range(2)]
        TP = [ctx.enter_context(nc.psum_tensor(f"TP{i}", [P, 512], F32)) for i in range(2)]
        OP = ctx.enter_context(nc.psum_tensor("OP", [P, 512], F32))
        PR = ctx.enter_context(nc.psum_tensor("PR", [P, 512], F32))

        START = [PR, OP, TP[0], TP[1], PR, OP]

        zero = sb("zero", [P, ROW])
        g_loaded = sem("g_loaded")
        const_ready = sem("const_ready")
        zero_ready = sem("zero_ready")
        zero_out = sem("zero_out")
        passed = sem("a_passed")
        x_in = [sem("x_in0"), sem("x_in1")]
        w_in = [sem("w_in0"), sem("w_in1")]
        split = sem("split")
        high0, split0 = sem("high0"), sem("split0")
        high_split = sem("high_split")
        pr_ready = sem("pr_ready")
        hi_ready = sem("hi_ready")
        lo_ready = sem("lo_ready")
        v_ready = sem("v_ready")
        k2_ready = sem("k2_ready")
        s_ready = sem("s_ready")
        max_ready = sem("max_ready")
        p_ready = sem("p_ready")
        tp_ready = [sem("tp_ready0"), sem("tp_ready1")]
        pt_ready = [sem("pt_ready0"), sem("pt_ready1")]
        inv_ready = sem("inv_ready")
        rec_ready = sem("rec_ready")
        r_ready = sem("r_ready")
        rb_ready = sem("rb_ready")
        o_ready = sem("o_ready")
        ob_ready = sem("ob_ready")
        o_out = [sem("o_out0"), sem("o_out1")]
        block = ctx.enter_context(nc.Block())

        wv = w_qkv.rearrange("(kt p) (three c) -> p kt three c", p=P, three=3)

        def load_w(eng, par, pair):
            for kt in range(KT):
                eng.dma_start(wraw[:, par, kt], wv[:, kt, :, pair * P:(pair + 1) * P]).then_inc(w_in[par], 16)

        @block.sync
        def _(sp):
            def load_x(b, c):
                sp.dma_start(xf[:, :, c * 512:(c + 1) * 512],
                             xT[:, :, bass.ds(b * L + c * 512, 512)]).then_inc(x_in[c], 16)

            def swap(par, count):
                sp.wait_ge(lo_ready, count)
                for h in range(2):
                    for half in range(2):
                        a, z = half * 64, 64 - half * 64
                        sp.dma_start(k2[a:a + 64, par, h].bitcast(F32), k1[z:z + 64, par, h].bitcast(F32)).then_inc(k2_ready, 16)

            def store(n, c, count):
                sp.wait_ge(ob_ready, count)
                sp.dma_start(OT[n, :, c * 512:(c + 1) * 512], ob[:, c]).then_inc(o_out[c], 16)

            load_w(sp, 0, 0)
            load_x(0, 0)
            load_x(0, 1)
            load_w(sp, 1, 1)
            swap(0, 4)

            sp.wait_ge(zero_ready, 2)
            sp.dma_start(XS.rearrange("(t p) n -> p t n", p=P),
                         zero[:, :].unsqueeze(1).to_broadcast([P, XT, ROW])).then_inc(zero_out, 16)

            names = ("wk", "wvx:wv", "ctxT", "wo", "wq", "wox", "wg", "bq", "bk", "bv", "bo", "bg")
            for name in names:
                to, source = (name + ":" + name).split(":")[:2]
                whole = (slice(None),) * len(g_in[to].shape)
                source = d[source]
                if to in ("bv", "bo", "bg"):
                    source = source.partition_broadcast(g_in[to].shape[0])
                sp.dma_start(g_in[to][whole], source).then_inc(g_loaded, 16)
            def batch(b, first, last):
                for n8 in range(PAIRS):
                    n = b * PAIRS + n8
                    if not (first and n8 == 0):
                        store(n - 1, 1, 2 * n)
                    if not (last and n8 == PAIRS - 1):
                        swap((n8 + 1) % 2, 8 * n + 12)
                    if not (last and n8 >= PAIRS - 2):
                        load_w(sp, n8 % 2, (n8 + 2) % PAIRS)
                        if n8 == PAIRS - 2:
                            for c in range(2):
                                sp.wait_ge(v_ready, 2 * n + 3 + c)
                                load_x(b + 1, c)
                    store(n, 0, 2 * n + 1)

            batch(0, True, False)
            with sp.Fori(1, B - 1) as b:
                batch(b, False, False)
            batch(B - 1, False, True)
            sp.wait_ge(o_out[0], 16 * PAIRS)
            sp.wait_ge(pr_ready, 6 * NI)
            load_group(sp, d, OT, g_in["ot"], g_in["xin"], in_ready, 0, 0)
            store(NI - 1, 1, 2 * NI)
            sp.wait_ge(g_loaded, 16 * len(names))
            sp.wait_ge(in_ready, 32)
            for c in range(2):
                sp.wait_ge(o_out[c], 16 * NI)
            sp.wait_ge(zero_out, 16)

        @block.gpsimd
        def _(pool):
            pool.memset(ident[:, :], 0.0).then_inc(const_ready, 1)
            pool.memset(maskb[:, :], 0.0).then_inc(const_ready, 1)
            pool.memset(zero[:, :], 0.0).then_inc(zero_ready, 1)
            pool.wait_ge(zero_ready, 1)
            pool.iota(zero[:, DM + 1:DM + 2].bitcast(I32), [[0, 1]], base=TOK, channel_multiplier=1).then_inc(zero_ready, 1)
            pool.wait_ge(const_ready, 2)
            pool.affine_select(out=ident[:, :], in_=ident[:, :], compare_op=ALU.not_equal, fill=1.0,
                               base=0, pattern=[[-1, P]], channel_multiplier=1).then_inc(const_ready, 1)
            pool.affine_select(out=maskb[:, :], in_=maskb[:, :], compare_op=ALU.is_ge, fill=BIG,
                               base=0, pattern=[[-1, P]], channel_multiplier=1).then_inc(const_ready, 1)
            pool.wait_ge(const_ready, 4)
            pool.tensor_copy(identb[:, :], ident[:, :]).then_inc(const_ready, 1)

            step = Steps()

            def split_in_two(high, low, whole, last=None):
                pool.tensor_copy(high, whole).then_inc(high_split, step.one())
                pool.wait_ge(high_split, step.now())
                ins = pool.tensor_tensor(low, whole, high, ALU.subtract)
                if last is not None:
                    ins.then_inc(last, 1)

            def batch(b):
                first = isinstance(b, int)
                step.start(0 if first else (2 * PAIRS + 2) * b - 4)
                for k8 in range(1 if first else 0, PAIRS):
                    par = k8 % 2
                    for c, qk in ((0, 1), (1, 0)):
                        if c == 0:
                            pool.wait_ge(w_in[par], 128 * b + 32 * (k8 // 2 + 1))
                            pool.sem_inc(passed, 1)
                        split_in_two(wh[:, par, :, qk, :], wl[:, par, :, qk, :], wraw[:, par, :, qk, :],
                                     split if k8 > 0 else None)
                        if k8 == 0:
                            pool.wait_ge(x_in[c], 16 * b + 16)
                            pool.sem_inc(passed, 1)
                            cols = slice(c * 512, (c + 1) * 512)
                            split_in_two(xh[:, :, cols], xl[:, :, cols], xf[:, :, cols], split)

            batch(0)
            with pool.Fori(1, B) as b:
                batch(b)

        def pairs(eng, body):
            body(0, 0, True, False)
            body(1, 1, False, False)
            with eng.Fori(1, NI // 2 - 1) as m:
                body(2 * m, 0, False, False)
                body(2 * m + 1, 1, False, False)
            body(NI - 2, 0, False, False)
            body(NI - 1, 1, False, True)

        @block.tensor
        def _(pe):
            pe.wait_ge(const_ready, 5)

            def project(k, par, j, first=False):
                if j <= 1 and first:
                    pe.wait_ge(split0, 2 * j + 2)
                elif j <= 1:
                    pe.wait_ge(split, 2 * k + j - 1)
                if j == 0 and not first:
                    pe.wait_ge(v_ready, 2 * k)
                    if not (isinstance(k, int) and k == 1):
                        pe.wait_ge(rb_ready, 2 * k - 2)
                if 1 <= j <= 3 and not first:
                    pe.wait_ge(lo_ready, 8 * k + 2 * j)
                if j >= 4 and first:
                    pe.wait_ge(lo_ready, 2 * (j - 3))
                bank = START[j] if first else PR
                if j == 4 and not first:
                    pe.wait_ge(rb_ready, 2 * k - 1)
                if j == 5 and not first:
                    pe.wait_ge(v_ready, 2 * k + 1)
                if j < 4:
                    qk, c = 1 - j // 2, j % 2
                    terms = [(w, x, kt) for kt in range(KT) for w, x in ((wl, xh), (wh, xl), (wh, xh))]
                    for i, (w, x, kt) in enumerate(terms):
                        mm = pe.matmul(bank[:, :], w[:, par, kt, qk, :], x[:, kt, c * 512:(c + 1) * 512],
                                       start=(i == 0), stop=(i == len(terms) - 1))
                else:
                    for a in range(4):
                        t = (j - 4) * 4 + a
                        for kt in range(KT):
                            mm = pe.matmul(bank[:, a * P:(a + 1) * P], xf[:, kt, t * P:(t + 1) * P],
                                           wraw[:, par, kt, 2, :], start=(kt == 0), stop=(kt == KT - 1))
                mm.then_inc(pr_ready, 1)

            def scores(n, par, s, fresh=False):
                t, h = s // 2, s % 2
                if s == 0:
                    pe.wait_ge(lo_ready, 8 * n + 8)
                    pe.wait_ge(k2_ready, 64 * n + 64)
                if not (fresh and s < 2):
                    pe.wait_ge(p_ready, 16 * n + s - 1)
                width = (t + 1) * P
                for c in range((width + 511) // 512):
                    n_cols = max(min(width - 512 * c, 512), 256)
                    cols = slice(512 * c, 512 * c + n_cols)
                    q = qs[:, par, h, t * P:(t + 1) * P]
                    pe.matmul(S[s % 2][:, cols], q, k2[:, par, h, cols], start=True, stop=False)
                    mm = pe.matmul(S[s % 2][:, cols], q, k1[:, par, h, cols], start=False, stop=True)
                pe.matmul(S[s % 2][:, t * P:(t + 1) * P], identb[:, :], maskb[:, :], start=False, stop=True,
                          skip_group_check=True).then_inc(s_ready, 1)

            def transposes(n, s, fresh=False):
                t = s // 2
                pe.wait_ge(p_ready, 16 * n + s + 1)
                for bank in ([s % 2] if t < 4 else [0, 1]):
                    use = s // 2 if s < 8 else s - 4
                    if not (fresh and use == 0):
                        pe.wait_ge(pt_ready[bank], 12 * n + use)
                    j0 = 0 if t < 4 else 4 * bank
                    for j in range(j0, min(j0 + 4, t + 1)):
                        mm = pe.transpose(TP[bank][:, (j - j0) * P:(j - j0 + 1) * P],
                                          prob[:, s % 4, j * P:(j + 1) * P], ident[:, :])
                    mm.then_inc(tp_ready[bank], 1)

            def spread(n, par, c, last=False):
                pe.wait_ge(rec_ready, 2 * n + c + 1)
                if last:
                    pe.wait_ge(rb_ready, 2 * n + c)
                elif c == 0:
                    pe.wait_ge(lo_ready, 8 * n + 16)
                else:
                    pe.wait_ge(v_ready, 2 * n + 4)
                for a in range(4):
                    mm = pe.transpose(PR[:, a * P:(a + 1) * P],
                                      rec[:, par, 4 * c + a, :], ident[:, :])
                mm.then_inc(r_ready, 1)

            def weigh(n, par, c, keys, fresh=False):
                if keys[0] == 0:
                    for bank in range(2):
                        pe.wait_ge(pt_ready[bank], 12 * n + (4 if c == 0 else 12))
                    pe.wait_ge(v_ready, 2 * n + 2)
                    if not fresh:
                        pe.wait_ge(ob_ready, 2 * n + c)
                for j in keys:
                    i0 = max(0, j - 4 * c) * P
                    for h in range(2):
                        mm = pe.matmul(OP[h * D:(h + 1) * D, i0:512], v[:, par, j, h * D:(h + 1) * D],
                                       pt[c][:, h, j, i0:512], start=(j == 0), stop=(j == 4 * c + 3))
                if keys[-1] == 4 * c + 3:
                    mm.then_inc(o_ready, 1)

            for j in range(6):
                project(0, 0, j, first=True)
            scores(0, 0, 0, fresh=True)
            scores(0, 0, 1, fresh=True)

            def iteration(n, par, first, last):
                for s in range(16):
                    ahead, s2 = lookahead(s)
                    if not (last and ahead):
                        scores(n + ahead, (par + ahead) % 2, s2)
                    transposes(n, s, fresh=first)
                    if not first and s == SPREAD1:
                        spread(n - 1, 1 - par, 1)
                    if not first and s in KEYS1:
                        weigh(n - 1, 1 - par, 1, KEYS1[s])
                    if not last and s in PROJECT:
                        project(n + 1, 1 - par, PROJECT[s])
                    if s == SPREAD0:
                        spread(n, par, 0, last)
                    if s in KEYS0:
                        weigh(n, par, 0, KEYS0[s], fresh=first)

            pairs(pe, iteration)
            spread(NI - 1, 1, 1, True)
            weigh(NI - 1, 1, 1, range(8))

        @block.scalar
        def _(act):
            def high(k, par, j, first=False):
                c = j % 2
                bank = START[j] if first else PR
                act.wait_ge(pr_ready, 6 * k + j + 1)
                for h in range(2):
                    rows = slice(h * 64, h * 64 + 64)
                    out = (k1 if j < 2 else qs)[rows, par, h, c * 512:(c + 1) * 512]
                    act.activation(out, bank[rows, :], ACT.Copy,
                                   scale=1.0 if j < 2 else D ** -0.5).then_inc(hi_ready, 1)

            def expo(n, par, s):
                t, h = s // 2, s % 2
                act.wait_ge(max_ready, 16 * n + s + 1)
                act.activation(prob[:, s % 4, 0:(t + 1) * P], S[s % 2][:, 0:(t + 1) * P], ACT.Exp,
                               bias=nmax[:, s % 2:s % 2 + 1],
                               accum_out=sums[:, par, t, h:h + 1]).then_inc(p_ready, 1)

            def evacuate(n, s):
                t, h = s // 2, s % 2
                use = s // 2 if s < 8 else s - 4
                act.wait_ge(tp_ready[0], 12 * n + use + 1)
                nb = min(4, t + 1)
                act.activation(pt[t // 4][:, h, 0:nb, (t % 4) * P:(t % 4 + 1) * P],
                               TP[0][:, 0:nb * P].rearrange("p (j i) -> p j i", i=P),
                               ACT.Copy).then_inc(pt_ready[0], 1)

            def spread_copy(n, c):
                act.wait_ge(r_ready, 2 * n + c + 1)
                act.activation(rb[:, c], PR[:, :], ACT.Copy).then_inc(rb_ready, 1)

            act.wait_ge(w_in[0], 32)
            for c, qk in ((0, 1), (1, 0)):
                cols = slice(c * 512, (c + 1) * 512)
                act.activation(wh[:, 0, :, qk, :], wraw[:, 0, :, qk, :], ACT.Copy).then_inc(high0, 1)
                act.wait_ge(x_in[c], 16)
                act.activation(xh[:, :, cols], xf[:, :, cols], ACT.Copy).then_inc(high0, 1)
            for j in range(4):
                high(0, 0, j, first=True)
            expo(0, 0, 0)
            expo(0, 0, 1)

            def iteration(n, par, first, last):
                for s in range(16):
                    if s >= 8 or s % 2 == 0:
                        evacuate(n, s)
                    ahead, s2 = lookahead(s)
                    if not (last and ahead):
                        expo(n + ahead, (par + ahead) % 2, s2)
                    if s == SPREAD1 and not first:
                        spread_copy(n - 1, 1)
                    if not last and PROJECT.get(s, 4) < 4:
                        high(n + 1, 1 - par, PROJECT[s])
                    if s == SPREAD0:
                        spread_copy(n, 0)

            pairs(act, iteration)
            spread_copy(NI - 1, 1)

        @block.vector
        def _(dve):
            def low(k, par, j, first=False):
                c = j % 2
                bank = START[j] if first else PR
                for h in range(2):
                    rows, other = slice(h * 64, h * 64 + 64), slice(64 - h * 64, 128 - h * 64)
                    stack = (k1 if j < 2 else qs)
                    dve.wait_ge(hi_ready, 8 * k + 2 * j + 2)
                    dve.scalar_tensor_tensor(
                        out=stack[other, par, h, c * 512:(c + 1) * 512], in0=bank[rows, :],
                        scalar=1.0 if j < 2 else D ** -0.5,
                        in1=stack[rows, par, h, c * 512:(c + 1) * 512].bitcast(F32),
                        op0=ALU.mult, op1=ALU.subtract).then_inc(lo_ready, 1)

            def values(k, par, j, first=False):
                bank = START[j] if first else PR
                dve.wait_ge(pr_ready, 6 * k + j + 1)
                dve.tensor_copy(v[:, par, 4 * (j - 4):4 * (j - 4) + 4, :],
                                bank[:, :].rearrange("p (a c) -> p a c", c=P)).then_inc(v_ready, 1)

            def row_max(n, s):
                t = s // 2
                dve.wait_ge(s_ready, 16 * n + s + 1)
                dve.tensor_reduce(nmax[:, s % 2:s % 2 + 1], S[s % 2][:, 0:(t + 1) * P], AX.X, ALU.max,
                                  negate=True).then_inc(max_ready, 1)

            def evacuate(n, s):
                t, h = s // 2, s % 2
                use = s // 2 if s < 8 else s - 4
                dve.wait_ge(tp_ready[1], 12 * n + use + 1)
                j0 = 0 if t < 4 else 4
                nb = t + 1 - j0
                dve.tensor_copy(pt[t // 4][:, h, j0:j0 + nb, (t % 4) * P:(t % 4 + 1) * P],
                                TP[1][:, 0:nb * P].rearrange("p (j i) -> p j i", i=P)).then_inc(pt_ready[1], 1)

            def reciprocals(n, par, c):
                dve.wait_ge(p_ready, 16 * n + 8 * c + 8)
                dve.reciprocal(inv[:, :], sums[:, par, 4 * c:4 * c + 4, :].rearrange("p t h -> p (t h)"))\
                   .then_inc(inv_ready, 1)
                dve.wait_ge(inv_ready, 2 * n + c + 1)
                dve.tensor_copy(rec[:, par, 4 * c:4 * c + 4, :].rearrange("p t (h d) -> p (t h) d", h=2),
                                inv[:, :].unsqueeze(2).to_broadcast([P, 8, D])).then_inc(rec_ready, 1)

            def normalise(n, c, fresh):
                dve.wait_ge(o_ready, 2 * n + c + 1)
                dve.wait_ge(rb_ready, 2 * n + c + 1)
                if not fresh:
                    dve.wait_ge(o_out[c], 16 * n)
                dve.tensor_tensor(ob[:, c], OP[:, :], rb[:, c], ALU.mult).then_inc(ob_ready, 1)

            for c, qk in ((0, 1), (1, 0)):
                cols = slice(c * 512, (c + 1) * 512)
                dve.wait_ge(high0, 2 * c + 1)
                dve.tensor_tensor(wl[:, 0, :, qk, :], wraw[:, 0, :, qk, :], wh[:, 0, :, qk, :], ALU.subtract).then_inc(split0, 1)
                dve.wait_ge(high0, 2 * c + 2)
                dve.tensor_tensor(xl[:, :, cols], xf[:, :, cols], xh[:, :, cols], ALU.subtract).then_inc(split0, 1)
            for j in range(6):
                (low if j < 4 else values)(0, 0, j, first=True)
            row_max(0, 0)
            row_max(0, 1)

            def iteration(n, par, first, last):
                for s in range(16):
                    ahead, s2 = lookahead(s)
                    if not (last and ahead):
                        row_max(n + ahead, s2)
                    if s == RECIP1 and not first:
                        reciprocals(n - 1, 1 - par, 1)
                    if s >= 8 or s % 2 == 1:
                        evacuate(n, s)
                    if not last and s in PROJECT:
                        (low if PROJECT[s] < 4 else values)(n + 1, 1 - par, PROJECT[s])
                    if s == NORM1 and not first:
                        normalise(n - 1, 1, fresh=isinstance(n, int) and n == 1)
                    if s == RECIP0:
                        reciprocals(n, par, 0)
                    if s == NORM0:
                        normalise(n, 0, fresh=first)

            pairs(dve, iteration)
            reciprocals(NI - 1, 1, 1)
            normalise(NI - 1, 1, fresh=False)


class Steps:

    def __init__(self):
        self.base, self.n = 0, 0

    def start(self, base):
        self.base, self.n = base, 0

    def one(self):
        self.n += 1
        return 1

    def now(self):
        return self.base + self.n


def group_inputs(sb):
    return {
        "wo": sb("wo", [P, PAIRS, DM]), "wq": sb("wq", [P, KT, DM]), "wk": sb("wk", [P, KT, DM]),
        "wvx": sb("wvx", [P, KT, DM]),
        "wox": sb("wox", [P, KT, DM]),
        "wg": sb("wg", [P, KT, E]), "ctxT": sb("ctxT", [P, KT, B * SC]),
        "bq": sb("bq", [P, KT]), "bk": sb("bk", [P, KT]), "bv": sb("bv", [SC, DM]),
        "bo": sb("bo", [P, DM]), "bg": sb("bg", [P, E]),
        "ot": sb("ot", [P, PAIRS, 512]),
        "xin": sb("xin", [P, GT, DM]),
    }


def load_group(sp, d, OT, ot, xin, in_ready, b, c):
    sp.dma_start(ot[:, :, :], OT.rearrange("(b r) p (c i) -> p b r c i", b=B, c=2)[:, b, :, c, :]).then_inc(in_ready, 16)
    sp.dma_start(xin[:, :, :], d["x"][:, b, c]).then_inc(in_ready, 16)


def token_groups(nc, sem, d, OT, g_in, in_ready, x2r, logits):
    HC = 4
    with ExitStack() as ctx:
        def sb(name, shape, dt=F32):
            return ctx.enter_context(nc.sbuf_tensor(name, shape, dt))

        wo, wq, wk, wvx, wox, wg = (g_in[n] for n in ("wo", "wq", "wk", "wvx", "wox", "wg"))
        ctxT, bq, bk, bv, bo, bg = (g_in[n] for n in ("ctxT", "bq", "bk", "bv", "bo", "bg"))
        ot, xin = g_in["ot"], g_in["xin"]
        ident = sb("ident2", [P, P])
        hmask = sb("hmask", [P, 8])
        kbd_all = sb("kbd_all", [P, B, KT, 8 * SC])
        vx_all = sb("vx_all", [SC, B, H, 32])
        kbd = sb("kbd", [P, KT, 8 * SC])
        vx = sb("vx", [SC, H, 32])
        r = sb("r", [P, 2, DM])
        st = sb("st", [P, 6])
        mv = sb("mv", [P, 2, 2])
        rstd = sb("rstd", [P, 2])
        veps = sb("veps", [P, 1])
        mhalf = sb("mhalf", [P, 1])
        x1 = sb("x1", [P, 2, GT, DM])
        x1b = sb("x1b", [P, 2, GT, DM])
        x1T = sb("x1T", [P, KT, 512])
        kT = x1T[:, :, 0:B * SC]
        qT = sb("qT", [P, KT, 512])
        sc = sb("sc", [P, GT, H * SC])
        mx = sb("mx", [P, GT, H])
        sm = sb("sm", [P, GT, H])
        rc = sb("rc", [P, GT, H])
        pT = sb("pT", [SC, H, 512])
        oT = sb("oT", [P, KT, 512])
        x2 = sb("x2", [P, GT, DM])
        x2T = sb("x2T", [P, GT, KT, P])
        SP = [ctx.enter_context(nc.psum_tensor(f"SP{i}", [P, 512], F32)) for i in range(4)]
        M = [ctx.enter_context(nc.psum_tensor(f"M{i}", [P, 512], F32)) for i in range(2)]
        T = [ctx.enter_context(nc.psum_tensor(f"T{i}", [P, 512], F32)) for i in range(2)]

        consts = sem("g_consts")
        kv_psum = sem("g_kv_psum")
        kv_sb = sem("g_kv_sb")
        kv_all = sem("g_kv_all")
        k_now, v_now = sem("g_k_now"), sem("g_v_now")
        m_ready = [sem("g_m_ready0"), sem("g_m_ready1")]
        m_free = [sem("g_m_free0"), sem("g_m_free1")]
        t_ready = [sem("g_t_ready0"), sem("g_t_ready1")]
        t_free = [sem("g_t_free0"), sem("g_t_free1")]
        sc_ready = sem("g_sc_ready")
        sc_free = sem("g_sc_free")
        exp_ready = sem("g_exp_ready")
        inv_ready = sem("g_inv_ready")
        p_ready = sem("g_p_ready")
        x1_ready = sem("g_x1_ready")
        x1b_ready = sem("g_x1b_ready")
        x2_ready = sem("g_x2_ready")
        x2_kept = sem("g_x2_kept")
        veps_ready = sem("g_veps_ready")
        var_ready = sem("g_var_ready")
        rstd_ready = sem("g_rstd_ready")
        passed = sem("g_passed")
        dstep = sem("g_dstep")
        block = ctx.enter_context(nc.Block())

        BEFORE = "p0 p1 p2 p3 x0 x1 x2 x3 q0 q1".split()
        DURING = "p0 p1 p2 p3 x0 x1 x2 x3 o0 o1 q0 y0 y1 q1 y2 y3".split()
        LAST = "o0 o1 y0 y1 y2 y3".split()

        def use(g, name):
            names = BEFORE if g is None else LAST if isinstance(g, int) and g == NG - 1 else DURING
            u = names.index(name)
            return u % 2, (0 if g is None else 5 + 8 * g) + u // 2

        def t_use(g, name):
            bank, nth = {"t0": (0, 0), "t1": (1, 0), "t2": (0, 1), "t3": (1, 1), "logits": (0, 2)}[name]
            return bank, (11 * g - 3, 10 * g - 2)[bank] + nth

        def p_use(g, a, q):
            bank, nth = q % 2, 2 * a + q // 2
            return bank, nth if isinstance(g, int) and g == 0 else (11 * g, 10 * g)[bank] + nth

        def groups(eng, body):
            body(0, 0, True, False)
            body(1, 1, False, False)
            with eng.Fori(1, NG // 2 - 1) as m:
                body(2 * m, 0, False, False)
                body(2 * m + 1, 1, False, False)
            body(NG - 2, 0, False, False)
            body(NG - 1, 1, False, True)

        @block.sync
        def _(sp):
            def load(b, c):
                load_group(sp, d, OT, ot, xin, in_ready, b, c)

            sp.wait_ge(x1_ready, 4)
            load(0, 1)
            with sp.Fori(1, B) as b:
                sp.wait_ge(x1_ready, 8 * b)
                load(b, 0)
                sp.wait_ge(x1_ready, 8 * b + 4)
                load(b, 1)

        @block.gpsimd
        def _(pool):
            pool.memset(ident[:, :], 0.0).then_inc(consts, 1)
            pool.memset(hmask[:, :], 1.0).then_inc(consts, 1)
            pool.memset(mhalf[:, :], -0.5)
            pool.memset(vx_all[:, :, :, :], 0.0).then_inc(consts, 1)
            pool.memset(x2r[:, :, DM:ROW], 0.0).then_inc(consts, 1)
            pool.wait_ge(consts, 4)
            pool.affine_select(out=ident[:, :], in_=ident[:, :], compare_op=ALU.not_equal, fill=1.0,
                               base=0, pattern=[[-1, P]], channel_multiplier=1).then_inc(consts, 1)
            pool.affine_select(out=hmask[:, :], in_=hmask[:, :], compare_op=ALU.is_ge, fill=0.0,
                               base=0, pattern=[[-XD, 8]], channel_multiplier=1).then_inc(consts, 1)
            pool.wait_ge(consts, 6)
            pool.iota(x2r[:, :, DM + 1:DM + 2].bitcast(I32), [[P, NT], [0, 1]], base=0, channel_multiplier=1).then_inc(consts, 1)
            pool.affine_select(out=hmask[:, :], in_=hmask[:, :], compare_op=ALU.is_ge, fill=0.0,
                               base=XD - 1, pattern=[[XD, 8]], channel_multiplier=-1).then_inc(consts, 1)
            pool.wait_ge(kv_all, B * KT + 2 * B)

            def group(g, par, first, last):
                b = batch[0]
                if par == 0:
                    if not first:
                        bank, before = use(g - 1, "o1")
                        pool.wait_ge(m_ready[bank], before + 1)
                        pool.sem_inc(passed, 1)
                    pool.tensor_copy(vx[:, :, :], vx_all[:, b]).then_inc(v_now, 1)
                if first:
                    pool.tensor_copy(kbd[:, :, :], kbd_all[:, 0]).then_inc(k_now, 1)
                    for a in range(GT):
                        root(a, a)
                    bias_x1(0, 0)
                for a in range(3):
                    if not last:
                        root(8 * g + 4 + a, a)
                    share_out(g, a)
                share_out(g, 3)
                if not last:
                    root(8 * g + 7, 3)
                if par == 1 and not last:
                    pool.wait_ge(sc_ready, 16 * g + 16)
                    pool.sem_inc(passed, 1)
                    pool.tensor_copy(kbd[:, :, :], kbd_all[:, b + 1]).then_inc(k_now, 1)
                if not last:
                    bias_x1(g + 1, 1 - par)
                for a in range(GT + 1):
                    if a < GT:
                        root(8 * g + (4 if last else 8) + a, a)
                    if a >= 1:
                        pool.wait_ge(x2_ready, 4 * g + a)
                        pool.sem_inc(passed, 1)
                        pool.tensor_copy(x2r[:, 4 * g + a - 1, 0:DM], x2[:, a - 1]).then_inc(x2_kept, 1)

            def share_out(g, a):
                pool.wait_ge(inv_ready, 4 * g + a + 1)
                pv = sc[:, a].rearrange("p (h j) -> p h j", j=SC)
                pool.tensor_tensor(pv, pv, rc[:, a].unsqueeze(2).to_broadcast([P, H, SC]),
                                   ALU.mult).then_inc(p_ready, 1)

            def root(i, a):
                pool.wait_ge(var_ready, i + 1)
                if not (isinstance(i, int) and i == 0):
                    pool.wait_ge(rstd_ready, i)
                pool.sem_inc(passed, 1)
                pool.tensor_scalar(veps[:, :], mv[:, a % 2, 1:2], EPS, None, ALU.add).then_inc(veps_ready, 1)
                pool.wait_ge(veps_ready, i + 1)
                pool.tensor_tensor(rstd[:, a % 2:a % 2 + 1], veps[:, :], mhalf[:, :], ALU.pow).then_inc(rstd_ready, 1)

            def bias_x1(g, par):
                for a in range(GT):
                    pool.wait_ge(x1_ready, 4 * g + a + 1)
                    pool.tensor_tensor(x1b[:, par, a], x1[:, par, a], bo[:, :], ALU.add).then_inc(x1b_ready, 1)

            batch = [0]
            group(0, 0, True, False)
            group(1, 1, False, False)
            with pool.Fori(1, NG // 2 - 1) as m:
                batch[0] = m
                group(2 * m, 0, False, False)
                group(2 * m + 1, 1, False, False)
            batch[0] = B - 1
            group(NG - 2, 0, False, False)
            group(NG - 1, 1, False, True)

        @block.tensor
        def _(pe):
            for kt in range(KT):
                for i in range(KT):
                    mm = pe.matmul(M[kt][:, 0:B * SC], wk[:, i, kt * P:(kt + 1) * P], ctxT[:, i, :],
                                   start=(i == 0), stop=(i == KT - 1))
                mm.then_inc(kv_psum, 1)
            for b in range(B):
                for i in range(KT):
                    mm = pe.matmul(SP[b][0:SC, 0:DM], ctxT[:, i, b * SC:(b + 1) * SC], wvx[:, i, :],
                                   start=(i == 0), stop=(i == KT - 1))
                mm.then_inc(kv_psum, 1)
            pe.wait_ge(kv_sb, KT)

            def take(bank_uses):
                bank, before = bank_uses
                if not (isinstance(before, int) and before == 0):
                    pe.wait_ge(m_free[bank], before)
                return M[bank], m_ready[bank]

            def project(g, par, a, bank_uses):
                if a == 0:
                    pe.wait_ge(in_ready, 32 * g + 32)
                m, ready = take(bank_uses)
                for i in range(PAIRS):
                    mm = pe.matmul(m[:, 0:DM], ot[:, i, a * P:(a + 1) * P], wo[:, i, :],
                                   start=(i == 0), stop=(i == PAIRS - 1))
                mm.then_inc(ready, 1)

            def x_scores(g, a):
                if a == 0:
                    pe.wait_ge(k_now, batch[0] + 1)
                    before_g = None if isinstance(g, int) and g == 0 else g - 1
                    for bank, before in (use(before_g, "q0"), use(before_g, "q1")):
                        pe.wait_ge(m_free[bank], before + 1)
                for c in range(4):
                    if not (isinstance(g, int) and g == 0 and a == 0):
                        pe.wait_ge(sc_free, 16 * g + 4 * a + c - 3)
                    pe.matmul(SP[c][:, 0:HC * SC], qT[:, c // 2, a * P:(a + 1) * P],
                              kbd[:, c // 2, (c % 2) * HC * SC:(c % 2 + 1) * HC * SC],
                              start=True, stop=True).then_inc(sc_ready, 1)

            def x_transposes(g, a):
                pe.wait_ge(p_ready, 4 * g + a + 1)
                for q in range(4):
                    bank, before = p_use(g, a, q)
                    if not (isinstance(before, int) and before == 0):
                        pe.wait_ge(t_free[bank], before)
                    for i in range(4):
                        h = 4 * q + i
                        mm = pe.transpose(T[bank][0:SC, i * P:(i + 1) * P], sc[:, a, h * SC:(h + 1) * SC], ident[:, :])
                    mm.then_inc(t_ready[bank], 1)

            def turn_x1(g, par, a, bank_uses):
                pe.wait_ge(x1_ready, 4 * g + a + 1)
                m, ready = take(bank_uses)
                for i in range(KT):
                    mm = pe.transpose(m[:, i * P:(i + 1) * P], x1[:, par, a, i * P:(i + 1) * P], ident[:, :])
                mm.then_inc(ready, 1)

            def turn_x2(g, a):
                pe.wait_ge(x2_ready, 4 * g + a - 3)
                bank, before = t_use(g, f"t{a}")
                pe.wait_ge(t_free[bank], before)
                for i in range(KT):
                    mm = pe.transpose(T[bank][:, i * P:(i + 1) * P], x2[:, a, i * P:(i + 1) * P], ident[:, :])
                mm.then_inc(t_ready[bank], 1)

            def gate(g):
                for name in ("t2", "t3"):
                    bank, before = t_use(g, name)
                    pe.wait_ge(t_free[bank], before + 1)
                for a in range(GT):
                    for i in range(KT):
                        mm = pe.matmul(T[0][:, a * E:(a + 1) * E], x2T[:, a, i, :], wg[:, i, :],
                                       start=(i == 0), stop=(i == KT - 1))
                mm.then_inc(t_ready[0], 1)

            def project_q(g, kt):
                m, ready = take(use(g, f"q{kt}"))
                if kt == 0:
                    bank, before = use(g, "x3")
                    pe.wait_ge(m_free[bank], before + 1)
                for i in range(KT):
                    mm = pe.matmul(m[:, :], wq[:, i, kt * P:(kt + 1) * P], x1T[:, i, :],
                                   start=(i == 0), stop=(i == KT - 1))
                mm.then_inc(ready, 1)

            def attend(g, hg):
                m, ready = take(use(g, f"o{hg}"))
                for j in range(2):
                    for i in range(4):
                        h = 8 * hg + 2 * i + j
                        mm = pe.matmul(m[32 * i:32 * i + 32, :], vx[:, h, :], pT[:, h, :],
                                       start=(j == 0), stop=(j == 1))
                mm.then_inc(ready, 1)

            def project_out(g, a):
                own, before = use(g, f"y{a}")
                m, ready = take((own, before))
                if a == 0:
                    for bank, before in (use(g, "o0"), use(g, "o1")):
                        if bank != own:
                            pe.wait_ge(m_free[bank], before + 1)
                for i in range(KT):
                    mm = pe.matmul(m[:, 0:DM], oT[:, i, a * P:(a + 1) * P], wox[:, i, :],
                                   start=(i == 0), stop=(i == KT - 1))
                mm.then_inc(ready, 1)

            for a in range(GT):
                project(0, 0, a, use(None, f"p{a}"))
            pe.wait_ge(consts, 8)
            pe.wait_ge(kv_all, B * KT + 2 * B)
            for a in range(GT):
                turn_x1(0, 0, a, use(None, f"x{a}"))
            for kt in range(KT):
                project_q(None, kt)

            def group(g, par, first, last):
                def next_project(a):
                    if not last:
                        project(g + 1, 1 - par, a, use(g, f"p{a}"))

                x_scores(g, 0)
                next_project(0)
                x_scores(g, 1)
                for a in range(2):
                    if not first:
                        turn_x2(g, 2 * a)
                        turn_x2(g, 2 * a + 1)
                    next_project(1 + a)
                    if a == 1 and not first:
                        gate(g)
                    x_scores(g, 2 + a)
                x_transposes(g, 0)
                next_project(3)
                x_transposes(g, 1)
                for a in range(2):
                    x_transposes(g, 2 + a)
                    if not last:
                        turn_x1(g + 1, 1 - par, 2 * a, use(g, f"x{2 * a}"))
                        turn_x1(g + 1, 1 - par, 2 * a + 1, use(g, f"x{2 * a + 1}"))
                for q in (2, 3):
                    bank, before = p_use(g, GT - 1, q)
                    pe.wait_ge(t_free[bank], before + 1)
                pe.wait_ge(v_now, batch[0] + 1)
                for hg in range(2):
                    attend(g, hg)
                for kt in range(2):
                    if not last:
                        project_q(g, kt)
                    if kt == 0:
                        project_out(g, 0)
                        project_out(g, 1)
                project_out(g, 2)
                project_out(g, 3)

            batch = [0]
            group(0, 0, True, False)
            group(1, 1, False, False)
            with pe.Fori(1, NG // 2 - 1) as m_:
                batch[0] = m_
                group(2 * m_, 0, False, False)
                group(2 * m_ + 1, 1, False, False)
            batch[0] = B - 1
            group(NG - 2, 0, False, False)
            group(NG - 1, 1, False, True)
            for a in range(GT):
                turn_x2(NG, a)
            gate(NG)

        @block.scalar
        def _(act):
            for kt in range(KT):
                act.wait_ge(kv_psum, kt + 1)
                act.activation(kT[:, kt, :], M[kt][:, 0:B * SC], ACT.Identity,
                               bias=bk[:, kt:kt + 1]).then_inc(kv_sb, 1)

            def read(g, name, out, rearranged=None, bias=None):
                bank, before = use(g, name)
                act.wait_ge(m_ready[bank], before + 1)
                m = M[bank][:, 0:512] if rearranged is None else rearranged(M[bank])
                if bias is None:
                    act.activation(out, m, ACT.Copy).then_inc(m_free[bank], 1)
                else:
                    act.activation(out, m, ACT.Identity, bias=bias).then_inc(m_free[bank], 1)

            def two(m):
                return m[:, 0:DM].rearrange("p (k i) -> p k i", k=KT)

            def turned_x1(g, a):
                read(g, f"x{a}", x1T[:, :, a * P:(a + 1) * P], two)

            def turned_x2(g, a):
                bank, before = t_use(g, f"t{a}")
                act.wait_ge(t_ready[bank], before + 1)
                act.activation(x2T[:, a], two(T[bank]), ACT.Copy).then_inc(t_free[bank], 1)

            def queries(g, kt):
                read(g, f"q{kt}", qT[:, kt, :], bias=bq[:, kt:kt + 1])

            def turned_p(g, a, q):
                bank, before = p_use(g, a, q)
                act.wait_ge(t_ready[bank], before + 1)
                act.activation(pT[:, 4 * q:4 * q + 4, a * P:(a + 1) * P],
                               T[bank][0:SC, :].rearrange("p (h i) -> p h i", i=P), ACT.Copy).then_inc(t_free[bank], 1)

            def expo(g, a):
                act.wait_ge(sc_free, 16 * g + 4 * a + 4)
                act.activation(sc[:, a], sc[:, a], ACT.Exp, scale=XD ** -0.5).then_inc(exp_ready, 1)

            for a in range(GT):
                turned_x1(None, a)
            for kt in range(KT):
                queries(None, kt)

            def group(g, par, first, last):
                for a in range(2):
                    expo(g, a)
                    if not first:
                        turned_x2(g, 2 * a)
                        turned_x2(g, 2 * a + 1)
                expo(g, 2)
                for q in range(4):
                    turned_p(g, 0, q)
                expo(g, 3)
                for q in range(4):
                    turned_p(g, 1, q)
                for a in range(2):
                    for q in range(4):
                        turned_p(g, 2 + a, q)
                    if not last:
                        turned_x1(g, 2 * a)
                        turned_x1(g, 2 * a + 1)
                read(g, "o0", oT[:, 0, :])
                if not last:
                    for kt in range(KT):
                        queries(g, kt)

            groups(act, group)
            for a in range(GT):
                turned_x2(NG, a)

        @block.vector
        def _(dve):
            step = Steps()
            dve.wait_ge(consts, 8)
            for kt in range(KT):
                dve.wait_ge(kv_sb, kt + 1)
                for b in range(B):
                    dve.tensor_tensor(kbd_all[:, b, kt].rearrange("p (h j) -> p h j", j=SC),
                                      kT[:, kt, b * SC:(b + 1) * SC].unsqueeze(1).to_broadcast([P, 8, SC]),
                                      hmask[:, :].unsqueeze(2).to_broadcast([P, 8, SC]), ALU.mult).then_inc(kv_all, 1)
            for b in range(B):
                dve.wait_ge(kv_psum, KT + b + 1)
                for j in range(2):
                    dve.tensor_tensor(
                        vx_all[:, b].rearrange("p (i j) e -> p i j e", j=2)[:, :, j, XD * j:XD * j + XD],
                        SP[b][0:SC, 0:DM].rearrange("p (i j e) -> p i j e", j=2, e=XD)[:, :, j, :],
                        bv[:, :].rearrange("p (i j e) -> p i j e", j=2, e=XD)[:, :, j, :],
                        ALU.add).then_inc(kv_all, 1)

            def less_max(g, a):
                for c in range(4):
                    dve.wait_ge(sc_ready, 16 * g + 4 * a + c + 1)
                    dve.tensor_reduce(mx[:, a, HC * c:HC * c + HC],
                                      SP[c][:, 0:HC * SC].rearrange("p (h j) -> p h j", j=SC),
                                      AX.X, ALU.max).then_inc(dstep, step.one())
                dve.wait_ge(dstep, step.now())
                for c in range(4):
                    dve.tensor_tensor(sc[:, a, HC * SC * c:HC * SC * (c + 1)].rearrange("p (h j) -> p h j", j=SC),
                                      SP[c][:, 0:HC * SC].rearrange("p (h j) -> p h j", j=SC),
                                      mx[:, a, HC * c:HC * c + HC].unsqueeze(2).to_broadcast([P, HC, SC]),
                                      ALU.subtract).then_inc(sc_free, 1)

            def inverse(g, a):
                dve.wait_ge(exp_ready, 4 * g + a + 1)
                dve.tensor_reduce(sm[:, a], sc[:, a].rearrange("p (h j) -> p h j", j=SC), AX.X,
                                  ALU.add).then_inc(dstep, step.one())
                dve.wait_ge(dstep, step.now())
                dve.reciprocal(rc[:, a], sm[:, a]).then_inc(inv_ready, 1)

            def statistics(i, bank_uses, residual, a):
                bank, before = bank_uses
                dve.wait_ge(m_ready[bank], before + 1)
                dve.tensor_tensor(r[:, a % 2], M[bank][:, 0:DM], residual, ALU.add).then_inc(m_free[bank], 1)
                dve.wait_ge(m_free[bank], before + 1)
                if not (isinstance(i, int) and i == 0):
                    dve.wait_ge(var_ready, i)
                dve.bn_stats(st[:, :], r[:, a % 2]).then_inc(dstep, step.one())
                dve.wait_ge(dstep, step.now())
                dve.sem_inc(passed, 1)
                dve.bn_aggr(mv[:, a % 2], st[:, :]).then_inc(var_ready, 1)

            def norm(i, a, out, ready):
                dve.wait_ge(rstd_ready, i + 1)
                dve.tensor_scalar(out, r[:, a % 2], mv[:, a % 2, 0:1], rstd[:, a % 2:a % 2 + 1],
                                  ALU.subtract, ALU.mult).then_inc(ready, 1)

            def statistics1(i, g, a, bank_uses):
                if a == 0:
                    dve.wait_ge(in_ready, 32 * g + 32)
                if a >= 2:
                    dve.wait_ge(x1_ready, 4 * g + a - 1)
                elif not (isinstance(g, int) and g <= 1):
                    dve.wait_ge(x2_ready, 4 * g - 4)
                elif g == 1:
                    dve.wait_ge(x1_ready, 4)
                statistics(i, bank_uses, xin[:, a], a)

            for a in range(GT):
                statistics1(a, 0, a, use(None, f"p{a}"))
                norm(a, a, x1[:, 0, a], x1_ready)
            before_groups = step.now()
            a_group = 4 * 4 + 4 + 4 + 4

            def logit(g):
                bank, before = t_use(g, "logits")
                dve.wait_ge(t_ready[bank], before + 1)
                dve.tensor_tensor(logits[:, bass.ds(4 * g - 4, GT), :], T[bank][:, 0:GT * E].rearrange("p (a e) -> p a e", e=E),
                                  bg[:, :].unsqueeze(1).to_broadcast([P, GT, E]), ALU.add).then_inc(t_free[bank], 1)

            def group(g, par, first, last):
                step.start(before_groups + a_group * g)

                def next_statistics(a):
                    if not last:
                        statistics1(8 * g + 4 + a, g + 1, a, use(g, f"p{a}"))

                def next_norm(a):
                    if not last:
                        norm(8 * g + 4 + a, a, x1[:, 1 - par, a], x1_ready)

                less_max(g, 0)
                for a in range(3):
                    next_statistics(a)
                    if a == 2 and not first:
                        logit(g)
                    less_max(g, 1 + a)
                    next_norm(a)
                    inverse(g, a)
                inverse(g, 3)
                next_statistics(3)
                next_norm(3)
                bank, before = use(g, "o1")
                dve.wait_ge(m_ready[bank], before + 1)
                dve.tensor_copy(oT[:, 1, :], M[bank][:, :]).then_inc(m_free[bank], 1)
                for a in range(GT + 1):
                    if a < GT:
                        dve.wait_ge(x1b_ready, 4 * g + a + 1)
                        if a >= 2:
                            dve.wait_ge(x2_ready, 4 * g + a - 1)
                        elif last:
                            dve.wait_ge(x2_ready, 4 * g)
                        else:
                            dve.wait_ge(x1_ready, 4 * g + 8)
                        statistics(8 * g + (4 if last else 8) + a, use(g, f"y{a}"), x1b[:, par, a], a)
                    if a >= 1:
                        if not first:
                            dve.wait_ge(x2_kept, 4 * g + a - 4)
                        norm(8 * g + (4 if last else 8) + a - 1, a - 1, x2[:, a - 1], x2_ready)

            groups(dve, group)
            logit(NG)


def route(nc, sem, d, x2r, logits, tile_e, XS, w1, w2, b1, w_in):
    with ExitStack() as ctx:
        def sb(name, shape, dt=F32):
            return ctx.enter_context(nc.sbuf_tensor(name, shape, dt))

        tri = sb("tri", [P, P])
        ones = sb("ones", [P, P])
        eidx = sb("eidx", [P, E])
        t128 = sb("t128", [P, NT])
        tnum = sb("tnum", [1, XT])
        best = sb("best", [P, NT])
        p = sb("p", [P, NT, E])
        total = sb("total", [P, NT])
        inv = sb("inv3", [P, NT])
        first = sb("first", [P, NT])
        oh = sb("oh", [P, NT, E])
        cum = [sb("cum0", [P, NT, E]), sb("cum1", [P, NT, E])]
        count = sb("count", [P, E])
        more = sb("more", [P, E, NT])
        ntile = sb("ntile", [P, E])
        start = sb("start", [P, E])
        posf = sb("posf", [P, NT])
        pos = sb("pos", [P, NT], I32)
        tgt = sb("tgt", [1, XT, E])
        tef = sb("tef", [1, XT])
        U = ctx.enter_context(nc.psum_tensor("U", [P, 512], F32))
        V = ctx.enter_context(nc.psum_tensor("V", [P, 512], F32))
        consts = sem("r_consts")
        less_ready = sem("r_less")
        exp_ready = sem("r_exp")
        oh_ready = sem("r_oh")
        sums_ready = sem("r_sums")
        pos_ready = sem("r_pos")
        dstep = sem("r_dstep")
        sent = sem("r_sent")
        b_in = sem("r_b_in")
        block = ctx.enter_context(nc.Block())

        @block.sync
        def _(sp):
            for e in range(EARLY):
                load_expert(sp, d, w1, w2, w_in, e)
            sp.wait_ge(w_in, 32 * EARLY)

        @block.gpsimd
        def _(pool):
            pool.memset(tri[:, :], 1.0).then_inc(consts, 1)
            pool.memset(ones[:, :], 1.0).then_inc(consts, 1)
            pool.iota(eidx[:, :], [[1, E]], base=-E, channel_multiplier=0,
                      allow_small_or_imprecise_dtypes=True).then_inc(consts, 1)
            pool.iota(t128[:, :], [[P, NT]], base=0, channel_multiplier=0,
                      allow_small_or_imprecise_dtypes=True).then_inc(consts, 1)
            pool.iota(tnum[:, :], [[1, XT]], base=0, channel_multiplier=0,
                      allow_small_or_imprecise_dtypes=True).then_inc(consts, 1)
            pool.wait_ge(consts, 5)
            pool.affine_select(out=tri[:, :], in_=tri[:, :], compare_op=ALU.is_gt, fill=0.0,
                               base=0, pattern=[[1, P]], channel_multiplier=-1).then_inc(consts, 1)
            pool.wait_ge(pos_ready, 1)
            for t in range(NT):
                pool.indirect_dma_start(XS, bass.IndirectOffsetOnAxis(ap=pos[:, t:t + 1], axis=0),
                                        x2r[:, t, :], None).then_inc(sent, 16)
            pool.wait_ge(sent, 16 * NT)

        @block.scalar
        def _(act):
            act.dma_start(b1[:, :, :], d["b1"].partition_broadcast(P)).then_inc(b_in, 16)
            act.wait_ge(less_ready, 1)
            act.activation(p[:, :, :], p[:, :, :], ACT.Exp).then_inc(exp_ready, 1)
            act.wait_ge(b_in, 16)

        @block.tensor
        def _(pe):
            pe.wait_ge(consts, 6)
            pe.wait_ge(oh_ready, 1)
            flat = oh[:, :, :].rearrange("p t e -> p (t e)")
            pe.matmul(U[:, 0:NT * E], tri[:, :], flat, start=True, stop=True)
            pe.matmul(V[:, 0:NT * E], ones[:, :], flat, start=True, stop=True).then_inc(sums_ready, 1)

        @block.vector
        def _(dve):
            step = Steps()

            def done(ins):
                return ins.then_inc(dstep, step.one())

            def wide(a):
                return a.unsqueeze(2).to_broadcast([P, NT, E])

            def every(a, n=NT):
                return a.unsqueeze(1).to_broadcast([P, n, E])

            done(dve.tensor_reduce(best[:, :], logits[:, :, :], AX.X, ALU.max))
            dve.wait_ge(dstep, step.now())
            dve.tensor_tensor(p[:, :, :], logits[:, :, :], wide(best[:, :]), ALU.subtract).then_inc(less_ready, 1)
            dve.wait_ge(exp_ready, 1)
            done(dve.tensor_reduce(total[:, :], p[:, :, :], AX.X, ALU.add))
            done(dve.tensor_reduce(best[:, :], p[:, :, :], AX.X, ALU.max))
            dve.wait_ge(dstep, step.now())
            done(dve.reciprocal(inv[:, :], total[:, :]))
            done(dve.tensor_tensor(oh[:, :, :], p[:, :, :], wide(best[:, :]), ALU.is_equal))
            dve.wait_ge(dstep, step.now())
            done(dve.tensor_tensor(x2r[:, :, DM], best[:, :], inv[:, :], ALU.mult))
            dve.wait_ge(consts, 6)
            done(dve.tensor_tensor(p[:, :, :], oh[:, :, :], every(eidx[:, :]), ALU.mult))
            dve.wait_ge(dstep, step.now())
            done(dve.tensor_reduce(first[:, :], p[:, :, :], AX.X, ALU.min))
            dve.wait_ge(dstep, step.now())
            dve.tensor_tensor(oh[:, :, :], every(eidx[:, :]), wide(first[:, :]), ALU.is_equal).then_inc(oh_ready, 1)

            dve.wait_ge(sums_ready, 1)
            done(dve.memset(cum[0][:, 0, :], 0.0))
            done(dve.tensor_copy(cum[0][:, 1:NT, :], V[:, 0:(NT - 1) * E].rearrange("p (t e) -> p t e", e=E)))
            now, shift = 0, 1
            while shift < NT:
                a, b = cum[now], cum[1 - now]
                dve.wait_ge(dstep, step.now())
                done(dve.tensor_copy(b[:, 0:shift, :], a[:, 0:shift, :]))
                done(dve.tensor_tensor(b[:, shift:NT, :], a[:, shift:NT, :], a[:, 0:NT - shift, :], ALU.add))
                now, shift = 1 - now, 2 * shift
            c = cum[now]
            dve.wait_ge(dstep, step.now())
            done(dve.tensor_tensor(count[:, :], V[:, (NT - 1) * E:NT * E], c[:, NT - 1, :], ALU.add))
            done(dve.tensor_tensor(cum[1 - now][:, :, :], U[:, 0:NT * E].rearrange("p (t e) -> p t e", e=E),
                                   c[:, :, :], ALU.add))
            rank = cum[1 - now]
            dve.wait_ge(dstep, step.now())
            done(dve.tensor_tensor(more[:, :, :], count[:, :].unsqueeze(2).to_broadcast([P, E, NT]),
                                   t128[:, :].unsqueeze(1).to_broadcast([P, E, NT]), ALU.is_gt))
            dve.wait_ge(dstep, step.now())
            done(dve.tensor_reduce(ntile[:, :], more[:, :, :], AX.X, ALU.add))
            done(dve.memset(start[:, 0:1], 0.0))
            for e in range(1, E):
                dve.wait_ge(dstep, step.now())
                done(dve.tensor_tensor(start[:, e:e + 1], start[:, e - 1:e], ntile[:, e - 1:e], ALU.add))
            dve.wait_ge(dstep, step.now())
            done(dve.tensor_tensor(tgt[:, :, 0:E - 1], tnum[:, :].unsqueeze(2).to_broadcast([1, XT, E - 1]),
                                   start[0:1, 1:E].unsqueeze(1).to_broadcast([1, XT, E - 1]), ALU.is_ge))
            dve.wait_ge(dstep, step.now())
            done(dve.tensor_scalar(start[:, :], start[:, :], float(P), None, ALU.mult))
            dve.wait_ge(dstep, step.now())
            done(dve.tensor_reduce(tef[:, :], tgt[:, :, 0:E - 1], AX.X, ALU.add))
            done(dve.tensor_tensor(rank[:, :, :], rank[:, :, :], every(start[:, :]), ALU.add))
            dve.wait_ge(dstep, step.now())
            done(dve.tensor_copy(tile_e[:, :], tef[:, :]))
            done(dve.tensor_tensor(rank[:, :, :], rank[:, :, :], oh[:, :, :], ALU.mult))
            dve.wait_ge(dstep, step.now())
            done(dve.tensor_reduce(posf[:, :], rank[:, :, :], AX.X, ALU.add))
            dve.wait_ge(dstep, step.now())
            dve.tensor_copy(pos[:, :], posf[:, :]).then_inc(pos_ready, 1)


def experts(nc, sem, d, x2r, XS, tile_e, w1, w2, b1, w_in, out):
    with ExitStack() as ctx:
        def sb(name, shape, dt=F32):
            return ctx.enter_context(nc.sbuf_tensor(name, shape, dt))

        room, used = x2r[:, :, :].rearrange("p t n -> p (t n)"), [0]

        def place(*shape):
            n, used[0] = used[0], used[0] + int(np.prod(shape))
            a = room[:, n:used[0]]
            if len(shape) == 2:
                return a.rearrange("p (a b) -> p a b", a=shape[0])
            if len(shape) == 3:
                return a.rearrange("p (a b c) -> p a b c", a=shape[0], b=shape[1])
            return a

        xs = place(4, ROW)
        xsT = place(2, KT, P)
        hid = place(2, FF)
        hT = place(FF // P, P)
        y = place(DM)
        r = place(DM)
        fo = place(2, DM)
        ident = place(P)
        b2 = place(E, DM)
        st = sb("st4", [P, 6])
        mv = sb("mv4", [P, 2])
        rstd = sb("rstd4", [P, 1])
        veps = sb("veps4", [P, 1])
        mhalf = sb("mhalf4", [P, 1])
        HP = [ctx.enter_context(nc.psum_tensor(f"HP{i}", [P, FF], F32)) for i in range(2)]
        HT = [ctx.enter_context(nc.psum_tensor(f"HT{i}", [P, 512], F32)) for i in range(2)]
        XP = ctx.enter_context(nc.psum_tensor("XP", [P, 512], F32))
        YP = ctx.enter_context(nc.psum_tensor("YP", [P, 512], F32))
        consts = sem("e_consts")
        x_in = [sem(f"e_x_in{i}") for i in range(4)]
        b2_in = sem("e_b2_in")
        xp_ready, xt_ready = sem("e_xp"), sem("e_xt")
        hp_ready, pre_ready = sem("e_hp"), sem("e_pre")
        act_ready = sem("e_act")
        ht_ready = [sem("e_ht0"), sem("e_ht1")]
        hs_ready = [sem("e_hs0"), sem("e_hs1")]
        yp_ready, y_ready = sem("e_yp"), sem("e_y")
        veps_ready = sem("e_veps")
        var_ready, rstd_ready = sem("e_var"), sem("e_rstd")
        f_ready = sem("e_f")
        f_out = [sem("e_fo0"), sem("e_fo1")]
        dstep = sem("e_dstep")
        passed = sem("e_passed")
        block = ctx.enter_context(nc.Block())
        XSv = XS.rearrange("(t p) n -> t p n", p=P)
        HEAD, TAIL = 3, 4

        def tiles(eng, body):
            for t in range(HEAD):
                body(0, t)
            with eng.Fori(0, (XT - HEAD - TAIL) // 4) as m:
                for i in range(4):
                    body(m, HEAD + i)
            for t in range(XT - TAIL, XT):
                body(0, t)

        def is_last(m, k):
            return isinstance(m, int) and k == XT - 1

        def loads_ahead(m, k):
            return not (isinstance(m, int) and k >= XT - 2)

        @block.sync
        def _(sp):
            for q in range(4):
                sp.wait_ge(x_in[q], 16)
            for e in range(EARLY, E):
                load_expert(sp, d, w1, w2, w_in, e, one_by_one=True)
                sp.wait_ge(w_in, 32 * e + 32)

        @block.gpsimd
        def _(pool):
            for t in range(3):
                pool.dma_start(xs[:, t], XSv[t]).then_inc(x_in[t], 16)
            pool.memset(mhalf[:, :], -0.5)
            pool.memset(ident[:, :], 0.0).then_inc(consts, 1)
            pool.wait_ge(consts, 1)
            pool.affine_select(out=ident[:, :], in_=ident[:, :], compare_op=ALU.not_equal, fill=1.0,
                               base=0, pattern=[[-1, P]], channel_multiplier=1).then_inc(consts, 1)

            def tile(m, k):
                t, q = 4 * m + k, k % 4
                if not (isinstance(m, int) and k >= XT - 3):
                    if not (isinstance(m, int) and k == 0):
                        pool.wait_ge(f_out[(k - 1) % 2], 32 * m + 16 * ((k + 1) // 2))
                    pool.dma_start(xs[:, (q + 3) % 4], XSv[t + 3]).then_inc(x_in[(q + 3) % 4], 16)
                pool.wait_ge(var_ready, t + 1)
                pool.sem_inc(passed, 1)
                pool.tensor_scalar(veps[:, :], mv[:, 1:2], EPS, None, ALU.add).then_inc(veps_ready, 1)
                pool.wait_ge(veps_ready, t + 1)
                pool.tensor_tensor(rstd[:, :], veps[:, :], mhalf[:, :], ALU.pow).then_inc(rstd_ready, 1)
                pool.wait_ge(f_ready, t + 1)
                pool.sem_inc(passed, 1)
                pool.indirect_dma_start(out, bass.IndirectOffsetOnAxis(ap=xs[:, q, DM + 1:DM + 2].bitcast(I32), axis=0),
                                        fo[:, q % 2], None, bounds_check=TOK - 1, oob_is_err=False).then_inc(f_out[q % 2], 16)

            tiles(pool, tile)
            pool.wait_ge(f_out[0], 16 * 20)
            pool.wait_ge(f_out[1], 16 * 19)

        @block.tensor
        def _(pe):
            pe.wait_ge(consts, 2)

            def turn_x(t, q, x_count, fresh=False):
                pe.wait_ge(x_in[q], 16 * x_count)
                if not fresh:
                    pe.wait_ge(xt_ready, t)
                for i in range(KT):
                    mm = pe.transpose(XP[:, i * P:(i + 1) * P], xs[:, q, i * P:(i + 1) * P], ident[:, :])
                mm.then_inc(xp_ready, 1)

            def up(t, q, e, c, fresh=False):
                if c == 0:
                    pe.wait_ge(w_in, 32 * e + 32)
                    pe.wait_ge(xt_ready, t + 1)
                    if not fresh:
                        pe.wait_ge(pre_ready, t - 1)
                for i in range(KT):
                    mm = pe.matmul(HP[q % 2][:, c * 512:(c + 1) * 512], xsT[:, q % 2, i, :],
                                   w1[:, e, i, c * 512:(c + 1) * 512], start=(i == 0), stop=(i == KT - 1))
                if c == 1:
                    mm.then_inc(hp_ready, 1)

            def expert(t):
                return pe.value_load(tile_e[0:1, bass.ds(t, 1)], min_val=0, max_val=E - 1)

            turn_x(0, 0, 1, fresh=True)
            turn_x(1, 1, 1)
            for c in range(2):
                up(0, 0, expert(0), c, fresh=True)

            def tile(m, k):
                t, q, first = 4 * m + k, k % 4, isinstance(m, int) and k == 0
                if not is_last(m, k):
                    e_next = expert(t + 1)
                    up(t + 1, (q + 1) % 4, e_next, 0, fresh=first)
                e = expert(t)
                pe.wait_ge(act_ready, t + 1)
                for bank in range(2):
                    if not first:
                        pe.wait_ge(hs_ready[bank], t)
                    for i in range(4):
                        j = 4 * bank + i
                        mm = pe.transpose(HT[bank][:, i * P:(i + 1) * P], hid[:, q % 2, j * P:(j + 1) * P], ident[:, :])
                    mm.then_inc(ht_ready[bank], 1)
                if loads_ahead(m, k):
                    turn_x(t + 2, (q + 2) % 4, m + (k + 2) // 4 + 1)
                if not is_last(m, k):
                    up(t + 1, (q + 1) % 4, e_next, 1)
                if not first:
                    pe.wait_ge(y_ready, t)
                for j in range(FF // P):
                    if j % 4 == 0:
                        pe.wait_ge(hs_ready[j // 4], t + 1)
                    mm = pe.matmul(YP[:, 0:DM], hT[:, j, :], w2[:, e, j, :], start=(j == 0), stop=(j == FF // P - 1))
                mm.then_inc(yp_ready, 1)

            tiles(pe, tile)

        @block.scalar
        def _(act):
            act.wait_ge(x_in[1], 16)
            act.dma_start(b2[:, :, :], d["b2"].partition_broadcast(P)).then_inc(b2_in, 16)

            def tile(m, k):
                t, q = 4 * m + k, k % 4
                act.wait_ge(pre_ready, t + 1)
                act.activation(hid[:, q % 2], hid[:, q % 2], ACT.Silu).then_inc(act_ready, 1)
                act.wait_ge(ht_ready[0], t + 1)
                act.activation(hT[:, 0:4, :], HT[0][:, :].rearrange("p (j i) -> p j i", i=P),
                               ACT.Copy).then_inc(hs_ready[0], 1)

            tiles(act, tile)

        @block.vector
        def _(dve):
            step = Steps()

            def expert(t):
                return dve.value_load(tile_e[0:1, bass.ds(t, 1)], min_val=0, max_val=E - 1)

            def turned(t, q):
                dve.wait_ge(xp_ready, t + 1)
                dve.tensor_copy(xsT[:, q % 2], XP[:, 0:DM].rearrange("p (k i) -> p k i", i=P)).then_inc(xt_ready, 1)

            def biased(t, q):
                e = expert(t)
                dve.wait_ge(hp_ready, t + 1)
                dve.tensor_tensor(hid[:, q % 2], HP[q % 2][:, :], b1[:, e, :], ALU.add).then_inc(pre_ready, 1)

            turned(0, 0)
            turned(1, 1)
            biased(0, 0)

            def tile(m, k):
                t, q = 4 * m + k, k % 4
                step.start(2 * t)
                dve.wait_ge(ht_ready[1], t + 1)
                dve.tensor_copy(hT[:, 4:8, :], HT[1][:, :].rearrange("p (j i) -> p j i", i=P)).then_inc(hs_ready[1], 1)
                if loads_ahead(m, k):
                    turned(t + 2, (q + 2) % 4)
                if not is_last(m, k):
                    biased(t + 1, (q + 1) % 4)
                e = expert(t)
                if isinstance(m, int) and k == 0:
                    dve.wait_ge(b2_in, 16)
                dve.wait_ge(yp_ready, t + 1)
                dve.tensor_tensor(y[:, :], YP[:, 0:DM], b2[:, e, :], ALU.add).then_inc(y_ready, 1)
                dve.wait_ge(y_ready, t + 1)
                dve.scalar_tensor_tensor(out=r[:, :], in0=y[:, :], scalar=xs[:, q, DM:DM + 1], in1=xs[:, q, 0:DM],
                                         op0=ALU.mult, op1=ALU.add).then_inc(dstep, step.one())
                dve.wait_ge(dstep, step.now())
                dve.bn_stats(st[:, :], r[:, :]).then_inc(dstep, step.one())
                dve.wait_ge(dstep, step.now())
                dve.sem_inc(passed, 1)
                dve.bn_aggr(mv[:, :], st[:, :]).then_inc(var_ready, 1)
                dve.wait_ge(rstd_ready, t + 1)
                if not (isinstance(m, int) and k < 2):
                    dve.wait_ge(f_out[k % 2], 32 * m + 16 * (k // 2))
                dve.tensor_scalar(fo[:, q % 2], r[:, :], mv[:, 0:1], rstd[:, :], ALU.subtract,
                                  ALU.mult).then_inc(f_ready, 1)

            tiles(dve, tile)


def load_expert(sp, d, w1, w2, w_in, e, one_by_one=False):
    sp.dma_start(w1[:, e], d["W1"][e].rearrange("(kt p) n -> p kt n", p=P)).then_inc(w_in, 16)
    if one_by_one:
        sp.wait_ge(w_in, 32 * e + 16)
    sp.dma_start(w2[:, e], d["W2"][e].rearrange("(kt p) n -> p kt n", p=P)).then_inc(w_in, 16)


def decoder_layer(nc, a, out):
    OT = nc.dram_tensor("attention_t", (NI, P, L), F32).ap()
    XS = nc.dram_tensor("sorted_rows", (XT * P, ROW), F32).ap()

    def by_row_tile(w):
        return w.rearrange("(k p) n -> p k n", p=P)

    d = {
        "x": a["x"].rearrange("b (c a p) n -> p b c a n", c=2, p=P),
        "wo": by_row_tile(a["attn_W_out"]), "ctxT": by_row_tile(a["ctxT"]),
        "wq": by_row_tile(a["xattn_W_qT"]), "wk": by_row_tile(a["xattn_W_kT"]),
        "wv": by_row_tile(a["xattn_W_vT"]),
        "wox": by_row_tile(a["xattn_W_outT"]),
        "bq": a["xattn_b_q"], "bk": a["xattn_b_k"], "bv": a["xattn_b_v"], "bo": a["xattn_b_out"],
        "wg": by_row_tile(a["ffn_Wg"]), "bg": a["ffn_bg"],
        "W1": a["ffn_W1"], "b1": a["ffn_b1"], "W2": a["ffn_W2"], "b2": a["ffn_b2"],
    }
    with ExitStack() as ctx:
        def sem(name):
            return ctx.enter_context(nc.semaphore(name))

        tile_e = ctx.enter_context(nc.sbuf_tensor("tile_e", [1, XT], I32))
        x2r = ctx.enter_context(nc.sbuf_tensor("x2r", [P, NT, ROW], F32))
        logits = ctx.enter_context(nc.sbuf_tensor("logits", [P, NT, E], F32))
        with ExitStack() as before_routing:
            g_in = group_inputs(lambda name, shape: before_routing.enter_context(nc.sbuf_tensor(name, shape, F32)))
            in_ready = sem("g_in")
            self_attention(nc, sem, d, by_row_tile(a["xT"]), a["attn_W_qkv"], OT, XS, g_in, in_ready, x2r)
            token_groups(nc, sem, d, OT, g_in, in_ready, x2r, logits)
        w1 = ctx.enter_context(nc.sbuf_tensor("w1", [P, E, KT, FF], F32))
        w2 = ctx.enter_context(nc.sbuf_tensor("w2", [P, E, FF // P, DM], F32))
        b1 = ctx.enter_context(nc.sbuf_tensor("b1", [P, E, FF], F32))
        w_in = sem("e_w_in")
        route(nc, sem, d, x2r, logits, tile_e, XS, w1, w2, b1, w_in)
        experts(nc, sem, d, x2r, XS, tile_e, w1, w2, b1, w_in, out)


def kernel(**inputs):
    import concourse.bacc as bacc
    from concourse.bass_utils import run_bass_kernel_spmd

    i = {k: np.asarray(v) for k, v in inputs.items()}
    lay = {
        "x": i["x"], "xT": i["x"].reshape(TOK, DM).T,
        "ctxT": i["ctx_1024"].reshape(B * SC, DM).T,
        "attn_W_qkv": i["L0_attn_W_qkv"], "attn_W_out": i["L0_attn_W_out"],
        "xattn_W_qT": i["L0_xattn_W_q"].T, "xattn_W_kT": i["L0_xattn_W_k"].T,
        "xattn_W_vT": i["L0_xattn_W_v"].T, "xattn_W_outT": i["L0_xattn_W_out"].T,
        "xattn_b_q": i["L0_xattn_b_q"].reshape(KT, P).T, "xattn_b_k": i["L0_xattn_b_k"].reshape(KT, P).T,
        "xattn_b_v": i["L0_xattn_b_v"], "xattn_b_out": i["L0_xattn_b_out"],
        "ffn_Wg": i["L0_ffn_Wg"], "ffn_bg": i["L0_ffn_bg"], "ffn_W1": i["L0_ffn_W1"],
        "ffn_b1": i["L0_ffn_b1"], "ffn_W2": i["L0_ffn_W2"], "ffn_b2": i["L0_ffn_b2"],
    }
    nc = bacc.Bacc("TRN2", target_bir_lowering=False, num_devices=1)
    arrays, aps = {}, {}
    for name, v in lay.items():
        arrays[f"in_{name}"] = np.ascontiguousarray(v)
        aps[name] = nc.dram_tensor(f"in_{name}", v.shape, F32, kind="ExternalInput").ap()
    out = nc.dram_tensor("out", (TOK, DM), F32, kind="ExternalOutput").ap()
    decoder_layer(nc, aps, out)
    r = run_bass_kernel_spmd(nc, [arrays], core_ids=[0])
    return r.results[0]["out"].reshape(B, L, DM)
```
